# Optimizing a Trainium2 kernel written in Bass

```python
import numpy as np
import jax
import jax.numpy as jnp

def _softmax(x, axis=-1):
    return jax.nn.softmax(x, axis=axis)

def _gelu(x):
    return jax.nn.gelu(x, approximate=True)

def _silu(x):
    return jax.nn.silu(x)

def _sigmoid(x):
    return jax.nn.sigmoid(x)

def _layernorm(x, axis=-1, eps=1e-05):
    m = jnp.mean(x, axis=axis, keepdims=True)
    v = jnp.var(x, axis=axis, keepdims=True)
    return (x - m) / jnp.sqrt(v + eps)

def _scatter_add(tgt, idx, src, axis=0):
    return tgt.at[idx].add(src)

def _segment_sum(src, seg, n):
    return jax.ops.segment_sum(src, seg, n)
kernel_name = 'mk_seq_postln_d2_jaxref_r8_3ea232'

def setup_inputs(seed: int=0):
    np.random.seed(seed)
    _w = jnp.asarray

    def _L0_attn_setup():
        import jax, jax.numpy as jnp
        import numpy as np
        N_HEADS = 16
        N_KV_HEADS = 4
        WINDOW = 128
        THETA = 10000.0

        def _rope_cos_sin(T, half):
            inv = 1.0 / THETA ** (jnp.arange(half, dtype=jnp.float32) / half)
            f = jnp.arange(T, dtype=jnp.float32)[:, None] * inv[None, :]
            return (jnp.cos(f), jnp.sin(f))

        def _apply_rope(x, cos, sin):
            xr, xi = (x[..., 0::2], x[..., 1::2])
            out_r = xr * cos - xi * sin
            out_i = xr * sin + xi * cos
            return jnp.stack([out_r, out_i], axis=-1).reshape(x.shape)
        key = jax.random.key(seed)
        ks = jax.random.split(key, 6)
        B, T, C = (1, 512, 256)
        kvC = C // N_HEADS * N_KV_HEADS
        return {'x': jax.random.normal(ks[0], (B, T, C), dtype=jnp.float32), 'wq': jax.random.normal(ks[1], (C, C), dtype=jnp.float32) * 0.02, 'wk': jax.random.normal(ks[2], (C, kvC), dtype=jnp.float32) * 0.02, 'wv': jax.random.normal(ks[3], (C, kvC), dtype=jnp.float32) * 0.02, 'wo': jax.random.normal(ks[4], (C, C), dtype=jnp.float32) * 0.02, 'sink': jnp.zeros((1, N_HEADS, 1, 1), dtype=jnp.float32)}
    _L0_attn_in = _L0_attn_setup()

    def _L0_ffn_setup():
        import jax, jax.numpy as jnp
        import numpy as np
        HIDDEN = 256
        INTER = 1024
        B, S = (4, 128)

        def _qmatmul(x, w_int8, scale):
            y = jnp.einsum('bsh,ho->bso', x, w_int8.astype(x.dtype))
            return y * scale
        key = jax.random.key(seed)
        ks = jax.random.split(key, 7)
        x = jax.random.normal(ks[0], (B, S, HIDDEN), dtype=jnp.float32)
        w_gate = jax.random.randint(ks[1], (HIDDEN, INTER), -128, 128, dtype=jnp.int32).astype(jnp.int8)
        w_up = jax.random.randint(ks[2], (HIDDEN, INTER), -128, 128, dtype=jnp.int32).astype(jnp.int8)
        w_down = jax.random.randint(ks[3], (INTER, HIDDEN), -128, 128, dtype=jnp.int32).astype(jnp.int8)
        s_gate = jax.random.uniform(ks[4], (INTER,), dtype=jnp.float32) * 0.02 + 0.001
        s_up = jax.random.uniform(ks[5], (INTER,), dtype=jnp.float32) * 0.02 + 0.001
        s_down = jax.random.uniform(ks[6], (HIDDEN,), dtype=jnp.float32) * 0.02 + 0.001
        return {'x': x, 'w_gate': w_gate, 'w_up': w_up, 'w_down': w_down, 's_gate': s_gate, 's_up': s_up, 's_down': s_down}
    _L0_ffn_in = _L0_ffn_setup()

    def _L1_attn_setup():
        import jax, jax.numpy as jnp
        import numpy as np
        import math
        NUM_HEADS = 16
        BASE = 10000.0

        def _rope_tables(T, head_size, dtype):
            half = head_size // 2
            thetas = BASE ** (-jnp.arange(half, dtype=jnp.float32) / half)
            ang = jnp.arange(T, dtype=jnp.float32)[:, None] * thetas[None, :]
            return (jnp.sin(ang).astype(dtype), jnp.cos(ang).astype(dtype))

        def _apply_rope(x, sin, cos):
            x1 = x[..., 0::2]
            x2 = x[..., 1::2]
            r1 = x1 * cos - x2 * sin
            r2 = x1 * sin + x2 * cos
            return jnp.stack([r1, r2], axis=-1).reshape(x.shape)
        key = jax.random.key(seed)
        ks = jax.random.split(key, 5)
        B, T, C = (4, 256, 256)
        return {'x': jax.random.normal(ks[0], (B, T, C), dtype=jnp.float32), 'w_qkv': jax.random.normal(ks[1], (3 * C, C), dtype=jnp.float32) * (1.0 / math.sqrt(C)), 'b_qkv': jax.random.normal(ks[2], (3 * C,), dtype=jnp.float32) * 0.02, 'w_out': jax.random.normal(ks[3], (C, C), dtype=jnp.float32) * (1.0 / math.sqrt(C)), 'b_out': jax.random.normal(ks[4], (C,), dtype=jnp.float32) * 0.02}
    _L1_attn_in = _L1_attn_setup()

    def _L1_ffn_setup():
        import jax, jax.numpy as jnp
        import numpy as np
        TOPK = 2

        def _mlp(x, w1, w2, w3):
            a = jnp.dot(x, w1.T).astype(jnp.float32)
            b = jnp.dot(x, w3.T).astype(jnp.float32)
            h = (jax.nn.silu(a) * b).astype(x.dtype)
            return jnp.dot(h, w2.T)
        key = jax.random.key(seed)
        ks = jax.random.split(key, 8)
        B, S, D, I, E = (4, 256, 256, 176, 16)
        SI = I * 2
        sc = 0.02
        return {'x': jax.random.normal(ks[0], (B, S, D), jnp.bfloat16), 'gate_w': jax.random.normal(ks[1], (E, D), jnp.float32) * sc, 'w1': jax.random.normal(ks[2], (E, I, D), jnp.bfloat16) * sc, 'w2': jax.random.normal(ks[3], (E, D, I), jnp.bfloat16) * sc, 'w3': jax.random.normal(ks[4], (E, I, D), jnp.bfloat16) * sc, 'sw1': jax.random.normal(ks[5], (SI, D), jnp.bfloat16) * sc, 'sw2': jax.random.normal(ks[6], (D, SI), jnp.bfloat16) * sc, 'sw3': jax.random.normal(ks[7], (SI, D), jnp.bfloat16) * sc}
    _L1_ffn_in = _L1_ffn_setup()
    _d = {'L0_attn_x': _L0_attn_in['x'], 'L0_attn_wq': _L0_attn_in['wq'], 'L0_attn_wk': _L0_attn_in['wk'], 'L0_attn_wv': _L0_attn_in['wv'], 'L0_attn_wo': _L0_attn_in['wo'], 'L0_attn_sink': _L0_attn_in['sink'], 'L0_ffn_w_gate': _L0_ffn_in['w_gate'], 'L0_ffn_w_up': _L0_ffn_in['w_up'], 'L0_ffn_w_down': _L0_ffn_in['w_down'], 'L0_ffn_s_gate': _L0_ffn_in['s_gate'], 'L0_ffn_s_up': _L0_ffn_in['s_up'], 'L0_ffn_s_down': _L0_ffn_in['s_down'], 'L1_attn_w_qkv': _L1_attn_in['w_qkv'], 'L1_attn_b_qkv': _L1_attn_in['b_qkv'], 'L1_attn_w_out': _L1_attn_in['w_out'], 'L1_attn_b_out': _L1_attn_in['b_out'], 'L1_ffn_gate_w': _L1_ffn_in['gate_w'], 'L1_ffn_w1': _L1_ffn_in['w1'], 'L1_ffn_w2': _L1_ffn_in['w2'], 'L1_ffn_w3': _L1_ffn_in['w3'], 'L1_ffn_sw1': _L1_ffn_in['sw1'], 'L1_ffn_sw2': _L1_ffn_in['sw2'], 'L1_ffn_sw3': _L1_ffn_in['sw3']}
    _x0 = _d['L0_attn_x']
    _d['L0_attn_x'] = jax.random.normal(jax.random.fold_in(jax.random.key(seed), 1), (4, 512, 256), dtype=_x0.dtype)
    del _x0
    return _d

def reference(L0_attn_x, L0_attn_wq, L0_attn_wk, L0_attn_wv, L0_attn_wo, L0_attn_sink, L0_ffn_w_gate, L0_ffn_w_up, L0_ffn_w_down, L0_ffn_s_gate, L0_ffn_s_up, L0_ffn_s_down, L1_attn_w_qkv, L1_attn_b_qkv, L1_attn_w_out, L1_attn_b_out, L1_ffn_gate_w, L1_ffn_w1, L1_ffn_w2, L1_ffn_w3, L1_ffn_sw1, L1_ffn_sw2, L1_ffn_sw3):

    def _L0_attn_ref(x, wq, wk, wv, wo, sink):
        import jax, jax.numpy as jnp
        import numpy as np
        N_HEADS = 16
        N_KV_HEADS = 4
        WINDOW = 128
        THETA = 10000.0

        def _rope_cos_sin(T, half):
            inv = 1.0 / THETA ** (jnp.arange(half, dtype=jnp.float32) / half)
            f = jnp.arange(T, dtype=jnp.float32)[:, None] * inv[None, :]
            return (jnp.cos(f), jnp.sin(f))

        def _apply_rope(x, cos, sin):
            xr, xi = (x[..., 0::2], x[..., 1::2])
            out_r = xr * cos - xi * sin
            out_i = xr * sin + xi * cos
            return jnp.stack([out_r, out_i], axis=-1).reshape(x.shape)
        B, T, C = x.shape
        hd = C // N_HEADS
        n_rep = N_HEADS // N_KV_HEADS
        q = (x @ wq).reshape(B, T, N_HEADS, hd).transpose(0, 2, 1, 3)
        k = (x @ wk).reshape(B, T, N_KV_HEADS, hd).transpose(0, 2, 1, 3)
        v = (x @ wv).reshape(B, T, N_KV_HEADS, hd).transpose(0, 2, 1, 3)
        cos, sin = _rope_cos_sin(T, hd // 2)
        q = _apply_rope(q, cos, sin)
        k = _apply_rope(k, cos, sin)
        k = jnp.repeat(k, n_rep, axis=1)
        v = jnp.repeat(v, n_rep, axis=1)
        att = jnp.einsum('bhqd,bhkd->bhqk', q, k) * hd ** (-0.5) + sink
        idx = jnp.arange(T)
        band = jnp.abs(idx[:, None] - idx[None, :]) <= WINDOW // 2
        att = jnp.where(band[None, None, :, :], att, -jnp.inf)
        att = jax.nn.softmax(att, axis=-1)
        att = jnp.where(jnp.isnan(att), 1.0 / T, att)
        out = jnp.einsum('bhqk,bhkd->bqhd', att, v).reshape(B, T, C)
        return out @ wo

    def _L0_ffn_ref(x, w_gate, w_up, w_down, s_gate, s_up, s_down):
        import jax, jax.numpy as jnp
        import numpy as np
        HIDDEN = 256
        INTER = 1024
        B, S = (4, 128)

        def _qmatmul(x, w_int8, scale):
            y = jnp.einsum('bsh,ho->bso', x, w_int8.astype(x.dtype))
            return y * scale
        gate = jax.nn.silu(_qmatmul(x, w_gate, s_gate))
        up = _qmatmul(x, w_up, s_up)
        fuse = gate * up
        return _qmatmul(fuse, w_down, s_down)

    def _L1_attn_ref(x, w_qkv, b_qkv, w_out, b_out):
        import jax, jax.numpy as jnp
        import numpy as np
        import math
        NUM_HEADS = 16
        BASE = 10000.0

        def _rope_tables(T, head_size, dtype):
            half = head_size // 2
            thetas = BASE ** (-jnp.arange(half, dtype=jnp.float32) / half)
            ang = jnp.arange(T, dtype=jnp.float32)[:, None] * thetas[None, :]
            return (jnp.sin(ang).astype(dtype), jnp.cos(ang).astype(dtype))

        def _apply_rope(x, sin, cos):
            x1 = x[..., 0::2]
            x2 = x[..., 1::2]
            r1 = x1 * cos - x2 * sin
            r2 = x1 * sin + x2 * cos
            return jnp.stack([r1, r2], axis=-1).reshape(x.shape)
        B, T, C = x.shape
        H = NUM_HEADS
        D = C // H
        scale = 1.0 / math.sqrt(D)
        qkv = x @ w_qkv.T + b_qkv
        qkv = qkv.reshape(B, T, 3, H, D)
        qkv = jnp.transpose(qkv, (2, 0, 3, 1, 4))
        q, k, v = (qkv[0], qkv[1], qkv[2])
        sin, cos = _rope_tables(T, D, x.dtype)
        q = _apply_rope(q, sin, cos)
        k = _apply_rope(k, sin, cos)
        att = jnp.einsum('bhtd,bhsd->bhts', q, k) * scale
        causal = jnp.triu(jnp.ones((T, T), dtype=bool), k=1)
        att = jnp.where(causal, -jnp.inf, att)
        att_prob = jax.nn.softmax(att, axis=-1)
        att_v = jnp.einsum('bhts,bhsd->bhtd', att_prob, v)
        att_v = jnp.transpose(att_v, (0, 2, 1, 3)).reshape(B, T, C)
        return att_v @ w_out.T + b_out

    def _L1_ffn_ref(x, gate_w, w1, w2, w3, sw1, sw2, sw3):
        import jax, jax.numpy as jnp
        import numpy as np
        TOPK = 2

        def _mlp(x, w1, w2, w3):
            a = jnp.dot(x, w1.T).astype(jnp.float32)
            b = jnp.dot(x, w3.T).astype(jnp.float32)
            h = (jax.nn.silu(a) * b).astype(x.dtype)
            return jnp.dot(h, w2.T)
        B, S, D = x.shape
        E = gate_w.shape[0]
        xf = x.reshape(-1, D)
        T = xf.shape[0]
        scores = jax.nn.sigmoid(jnp.dot(xf.astype(jnp.float32), gate_w.T))
        topv, topi = jax.lax.top_k(scores, TOPK)
        topv = topv / topv.sum(axis=-1, keepdims=True)
        dw = jnp.zeros((T, E), jnp.float32).at[jnp.arange(T)[:, None], topi].add(topv)
        y0 = _mlp(xf, sw1, sw2, sw3).astype(jnp.float32)

        def step(y, ws):
            e1, e2, e3, we = ws
            out = _mlp(xf, e1, e2, e3).astype(jnp.float32)
            return (y + out * we[:, None], None)
        y, _ = jax.lax.scan(step, y0, (w1, w2, w3, dw.T))
        return y.astype(x.dtype).reshape(B, S, D)
    x = L0_attn_x
    x = _layernorm(x + _L0_attn_ref(x, L0_attn_wq, L0_attn_wk, L0_attn_wv, L0_attn_wo, L0_attn_sink), axis=-1)
    x = _layernorm(x + _L0_ffn_ref(x, L0_ffn_w_gate, L0_ffn_w_up, L0_ffn_w_down, L0_ffn_s_gate, L0_ffn_s_up, L0_ffn_s_down), axis=-1)
    x = _layernorm(x + _L1_attn_ref(x, L1_attn_w_qkv, L1_attn_b_qkv, L1_attn_w_out, L1_attn_b_out), axis=-1)
    x = _layernorm(x + _L1_ffn_ref(x, L1_ffn_gate_w, L1_ffn_w1, L1_ffn_w2, L1_ffn_w3, L1_ffn_sw1, L1_ffn_sw2, L1_ffn_sw3), axis=-1)
    return x

_drawn_inputs = setup_inputs


def setup_inputs(seed=0):
    import zlib

    import numpy as np

    out = dict(_drawn_inputs(seed))
    spreads = {'L0_attn_sink': (0.0, 0.8)}
    factors = {'L0_attn_wq': 8.0,
     'L0_attn_wk': 8.0,
     'L0_attn_wv': 3.918,
     'L0_attn_wo': 3.905,
     'L1_attn_b_out': 2.948,
     'L1_ffn_gate_w': 6.203,
     'L1_ffn_w1': 5.829,
     'L1_ffn_w2': 5.768,
     'L1_ffn_w3': 5.769,
     'L1_ffn_sw1': 2.906,
     'L1_ffn_sw2': 2.885,
     'L1_ffn_sw3': 2.871}
    for name, (base, spread) in spreads.items():
        noise = np.random.default_rng([zlib.crc32(name.encode()), seed]).standard_normal(out[name].shape)
        drawn = base * np.exp(spread * noise) if base else spread * noise
        out[name] = jnp.asarray(drawn.astype(out[name].dtype))
    for name, factor in factors.items():
        out[name] = (out[name] * factor).astype(out[name].dtype)
    return out
```

```python
import numpy as np
import concourse.bass as bass
from concourse import mybir
from contextlib import ExitStack

F32, F32R, BF16 = mybir.dt.float32, mybir.dt.float32r, mybir.dt.bfloat16
I8, U32 = mybir.dt.int8, mybir.dt.uint32
ALU = mybir.AluOpType
ACT = mybir.ActivationFunctionType
AX = mybir.AxisListType

P = 128
B, T, C = 4, 512, 256
NT, KC = T // P, C // P
H, HD = 16, 16
KVH0 = 4
HALF_WINDOW = 64
NG, GH = 4, 4
NQKV = (C + 2 * KVH0 * HD, 3 * C)
QKH = (H + KVH0, 2 * H)
INTER = 1024
NI = INTER // P
E, I = 16, 176
SHARED = 2
NE = E + SHARED
IH = I // 2
TOK = B * T
EPS = 1e-5
SCALE = HD ** -0.5
MASKED = -1e30

STACK = 64
SHIFT = 3 * HD
PAIRS = H // 2


def key_tile_queries(layer, kt):
    if layer == 1:
        return kt * P, T - kt * P
    lo, hi = max(0, kt * P - HALF_WINDOW), min(T, (kt + 1) * P + HALF_WINDOW)
    return lo, hi - lo


def query_tile_keys(layer, t):
    if layer == 1:
        return 0, (t + 1) * P
    return key_tile_queries(0, t)


PARTS = ([[(0, 0), (1, 192)], [(2, 0), (3, 256)]],
         [[(0, 0)], [(1, 0), (3, 384)], [(2, 0)]])
PART_COLS = tuple([sum(key_tile_queries(l, kt)[1] for kt, _ in part) for part in PARTS[l]] for l in (0, 1))
PROB_COLS = max(sum(c) for c in PART_COLS)
MAX_HEADS = tuple([min(2, 512 // query_tile_keys(l, t)[1]) for t in range(NT)] for l in (0, 1))
MAX_ITEMS = tuple([(t, j) for t in range(NT) for j in range(GH // MAX_HEADS[l][t])] for l in (0, 1))


class Signal:

    def __init__(self, sem, per, primed=0):
        self.sem, self.per, self.primed = sem, per, primed

    def at(self, turn, n):
        return self.sem, turn * self.per + n + self.primed


def rotary_tables():
    half = HD // 2
    inv = (np.float32(1.0) / np.float32(10000.0) ** (np.arange(half, dtype=np.float32) / np.float32(half))).astype(np.float32)
    f = np.arange(T, dtype=np.float32)[:, None] * inv[None, :]
    c, s = np.cos(f).astype(np.float32), np.sin(f).astype(np.float32)
    cos = np.stack([c, c], -1).reshape(T, HD)
    sin = np.stack([-s, s], -1).reshape(T, HD)
    return np.ascontiguousarray(np.concatenate([cos, sin], 1))


def build(nc, x, wqkv0, wo0, sink, w_gate, w_up, w_down, s_gate, s_up, s_down,
          wqkv1, b_qkv, wo1, b_out, gate_w, w13, w2, rotary, out):
    ctx = ExitStack()
    scope = [ctx]

    def sb(name, shape, dt=F32):
        return scope[-1].enter_context(nc.sbuf_tensor(name, shape, dt))

    def signal(name, per, primed=0):
        return Signal(ctx.enter_context(nc.semaphore(name)), per, primed)

    x3_dram = nc.dram_tensor("x3_scratch", (TOK, C), F32, kind="Internal").ap()

    with ctx:
        ps = ctx.enter_context(nc.psum_tensor("ps", [P, 8, 512], F32))

        ident = sb("ident", [P, P])
        ident_b = sb("ident_b", [P, P], BF16)
        band = sb("band", [P, 256], BF16)
        causal_q = sb("causal_q", [P, P], BF16)
        causal_k = sb("causal_k", [P, P], BF16)
        rot = sb("rot", [P, NT, 2, HD])
        carry = sb("carry", [P, 8])
        neg_half = sb("neg_half", [P, 1])
        sink4 = sb("sink4", [P, H])
        iota_e = sb("iota_e", [P, E])
        zero_r = sb("zero_r", [P, 512])
        phase1 = ExitStack()
        scope.append(phase1)
        wqkv_s = [sb(f"wqkv{l}_s", [P, 2, KC, NQKV[l]], F32R) for l in (0, 1)]
        wo_s = [sb(f"wo{l}_s", [P, 2, KC, C], F32R) for l in (0, 1)]
        wg_sb = sb("wg_sb", [P, KC, INTER], F32R)
        wu_sb = sb("wu_sb", [P, KC, INTER], F32R)
        wd_sb = sb("wd_sb", [P, NI, C], F32R)
        sg_sb = sb("sg_sb", [P, NI])
        su_sb = sb("su_sb", [P, NI])
        sd_sb = sb("sd_sb", [P, C])
        bqkv_sb = sb("bqkv_sb", [P, 3 * C])
        bout_sb = sb("bout_sb", [P, C])
        x0 = sb("x0", [P, 2, NT, C])
        x1 = sb("x1", [P, NT, C])
        x2 = sb("x2", [P, NT, C])
        x3 = sb("x3", [P, NT, C])
        xT = sb("xT", [P, 2, KC, T], F32R)
        mv = sb("mv", [P, NT, 2])
        stats = sb("stats", [P, NT, 6])
        rstd = sb("rstd", [P, NT])
        q_st = sb("q_st", [P, H, STACK])
        k_st = sb("k_st", [P, H, STACK])
        v_aug = [sb(f"v_aug{l}", [P, NT, (KVH0, H)[l], 32]) for l in (0, 1)]
        attn_scope = ExitStack()
        scope.append(attn_scope)
        qkv_sb = sb("qkv_sb", [P, 2, 3 * C])
        rot_c = sb("rot_c", [P, 2 * C])
        rot_s = sb("rot_s", [P, 2, 2 * C])
        qT = sb("qT", [P, PAIRS, T], F32R)
        kT = sb("kT", [P, PAIRS, T], F32R)
        negmax = sb("negmax", [P, NT, H])
        shift_row = sb("shift_row", [GH, 2, T], F32R)
        prob = sb("prob", [P, 2, GH, PROB_COLS])
        oT = sb("oT", [P, T])
        rden = sb("rden", [P, NT, GH])
        o_sb = sb("o_sb", [P, NT, C])
        scope.pop()
        attn_scope.close()
        ffn_scope = ExitStack()
        scope.append(ffn_scope)
        gate_sb = sb("gate_sb", [P, 2, T])
        fuse_sb = sb("fuse_sb", [P, 2, T])
        fT = sb("fT", [P, 2, NI, T], F32R)
        scope.pop()
        ffn_scope.close()
        stage_scope = ExitStack()
        scope.append(stage_scope)
        w_raw = [sb(f"w_raw{i}", [P, KC, n]) for i, n in enumerate((NQKV[0], C, NQKV[1], C))]
        scope.pop()
        stage_scope.close()
        scope.pop()
        phase1.close()
        phase2 = ExitStack()
        scope.append(phase2)
        w13_sb = sb("w13_sb", [P, NE, KC, 2 * I], F32R)
        w2_sb = sb("w2_sb", [IH, NE, 2, C], F32R)
        gw_raw = sb("gw_raw", [P, KC, E])
        gw_s = sb("gw_s", [P, 2, KC, E], F32R)
        xg = sb("xg", [P, NT, C])
        xgT = sb("xgT", [P, 2, KC, T], F32R)
        score = sb("score", [P, NT, E])
        top8 = sb("top8", [P, NT, 8])
        idx8 = sb("idx8", [P, NT, 8], U32)
        idxf = sb("idxf", [P, NT, 2])
        topw = sb("topw", [P, NT, 2])
        tsum = sb("tsum", [P, NT])
        hot = sb("hot", [P, NT, 2, E])
        dw = sb("dw", [P, NE, NT])
        act_a = sb("act_a", [P, NT, I])
        h_sb = sb("h_sb", [P, NT, I])
        hT = sb("hT", [IH, 2, 2, 2, P], F32R)
        yy = sb("yy", [P, NT, C])
        yo = sb("yo", [P, NT, C])
        mv2 = sb("mv2", [P, NT, 2])
        stats2 = sb("stats2", [P, NT, 6])
        rstd2 = sb("rstd2", [P, NT])
        scope.pop()
        phase2.close()

        w_in = [signal(f"w_in{i}", 0) for i in range(4)]
        consts_in = signal("consts_in", 0)
        w_int8 = signal("w_int8", 0)
        made = signal("made", 0)
        w_hi = signal("w_hi", 0)
        w_lo = signal("w_lo", 0)
        start_dve = signal("start_dve", 0)
        x0_in = signal("x0_in", 16)
        tr, hi, lo = {}, {}, {}
        for n in ("x0", "o0", "x1", "x2", "o1"):
            tr[n], hi[n], lo[n] = (signal(f"{n}_{s}", NT) for s in ("tr", "hi", "lo"))
        qkv, qkv_out, cosd, roped, st_hi, st_lo, v_put = ([signal(f"{s}{l}", n) for l in (0, 1)] for s, n in (
            ("qkv", NT), ("qkv_out", NT), ("cosd", NT), ("roped", NT), ("st_hi", 2 * NT), ("st_lo", 2 * NT), ("v_put", NT)))
        q_tr, k_tr, q_out, k_out = ([signal(f"{s}{l}", NT) for l in (0, 1)] for s in ("q_tr", "k_tr", "q_out", "k_out"))
        raw_score = [signal(f"raw_score{l}", NG * len(MAX_ITEMS[l])) for l in (0, 1)]
        maxed = [signal(f"maxed{l}", NG * len(MAX_ITEMS[l])) for l in (0, 1)]
        sunk = signal("sunk", NG)
        sh_tr, sh_out = ([signal(f"{s}{l}", NG) for l in (0, 1)] for s in ("sh_tr", "sh_out"))
        sh_row = [[signal(f"sh_row{l}_{g}", GH * 16) for g in range(NG)] for l in (0, 1)]
        scored, exped = ([signal(f"{s}{l}", NG * GH * len(PARTS[l])) for l in (0, 1)] for s in ("scored", "exped"))
        pv = [signal(f"pv{l}", NG * len(PARTS[l])) for l in (0, 1)]
        oT_out, o_tr, o_put = ([signal(f"{s}{l}", NG) for l in (0, 1)] for s in ("oT_out", "o_tr", "o_put"))
        rden_done = [signal(f"rden{l}", NG) for l in (0, 1)]
        proj = [signal(f"proj{l}", NT) for l in (0, 1)]
        var_done, rstd_done = ([signal(f"{s}{i}", NT) for i in range(3)] for s in ("var", "rstd"))
        normed = [signal(f"normed{i}", NT, primed=int(i == 0)) for i in range(3)]
        gated, upped, silued, fused, f_hi, f_lo = (signal(s, NI) for s in ("gated", "upped", "silued", "fused", "f_hi", "f_lo"))
        down = signal("down", NT)
        biased = signal("biased", NT)
        x3_out = signal("x3_out", 16)
        DVE_STEPS = 2 * NT + NG + 10 * NT
        dve_step = signal("dve_step", DVE_STEPS)
        UNITS = NE * NT
        w13_in, w2_in, gw_in = signal("w13_in", 0), signal("w2_in", 0), signal("gw_in", 0)
        gw_split = signal("gw_split", 0)
        xg_in = signal("xg_in", 16)
        xg_tr, xg_hi, xg_lo = (signal(s, NT) for s in ("xg_tr", "xg_hi", "xg_lo"))
        logits, exp_l = signal("logits", 1), signal("exp_l", 1)
        routed = signal("routed", 1)
        a_up, a_silu, h_tr, h_hi, h_lo, h_down = (signal(s, UNITS) for s in ("a_up", "a_silu", "h_tr", "h_hi", "h_lo", "h_down"))
        a_h = signal("a_h", UNITS, 1)
        y_done, y_var, y_rstd, y_norm = signal("y_done", 1, 1), signal("y_var", NT), signal("y_rstd", NT), signal("y_norm", NT, 1)
        MOE_STEPS = 10 + 4 * NT
        moe_step = signal("moe_step", MOE_STEPS)
        y_out = signal("y_out", 16, 16)

        block = ctx.enter_context(nc.Block())

        @block.sync
        def _(sp):
            raw = (wqkv0, wo0, wqkv1, wo1)
            for i in range(4):
                sp.dma_start(w_raw[i][:], raw[i].rearrange("(k p) n -> p k n", p=P)).then_inc(w_in[i].sem, 16)
            with sp.Fori(0, B) as b:
                sp.wait_ge(*normed[0].at(b, 0))
                sp.dma_start(x0[:, 0, :, :], x.rearrange("b (t p) c -> b p t c", p=P)[b]).then_inc(x0_in.sem, 16)
                for l in (0, 1):
                    for g in range(NG):
                        sp.wait_ge(*sh_out[l].at(b, g + 1))
                        for j in range(GH):
                            r = STACK * (j % 2) + SHIFT
                            sp.dma_start(qT[r:r + 1, 2 * g + j // 2, :].bitcast(F32),
                                         shift_row[j:j + 1, g % 2, :].bitcast(F32)).then_inc(sh_row[l][g].sem, 16)
                sp.wait_ge(*normed[2].at(b, NT))
                sp.dma_start(x3_dram.rearrange("(b t p) c -> b p t c", b=B, p=P)[b], x3[:]).then_inc(x3_out.sem, 16)
            sp.wait_ge(*x3_out.at(B, 0))
            sp.dma_start(gw_raw[:], gate_w.rearrange("(k p) e -> p k e", p=P)).then_inc(gw_in.sem, 16)
            with sp.Fori(0, B) as b:
                sp.wait_ge(*y_norm.at(b, 0))
                sp.dma_start(xg[:], x3_dram.rearrange("(b t p) c -> b p t c", b=B, p=P)[b]).then_inc(xg_in.sem, 16)
                sp.wait_ge(*y_norm.at(b, NT))
                sp.dma_start(out.rearrange("b (t p) c -> b p t c", p=P)[b], yo[:]).then_inc(y_out.sem, 16)
            sp.wait_ge(*y_out.at(B, 0))

        @block.gpsimd
        def _(pool):
            n_made = [0]

            def then(ins):
                n_made[0] += 1
                ins.then_inc(made.sem, 1)
                pool.wait_ge(made.sem, n_made[0])

            then(pool.memset(ident[:], 0.0))
            then(pool.affine_select(out=ident[:], in_=ident[:], compare_op=ALU.not_equal, fill=1.0, base=0,
                                    pattern=[[-1, P]], channel_multiplier=1))
            pool.dma_start(wg_sb[:], w_gate.bitcast(I8).rearrange("(k p) n -> p k n", p=P)).then_inc(w_int8.sem, 16)
            pool.dma_start(wu_sb[:], w_up.bitcast(I8).rearrange("(k p) n -> p k n", p=P)).then_inc(w_int8.sem, 16)
            pool.dma_start(wd_sb[:], w_down.bitcast(I8).rearrange("(k p) n -> p k n", p=P)).then_inc(w_int8.sem, 16)
            then(pool.memset(ident_b[:], 0.0))
            then(pool.affine_select(out=ident_b[:], in_=ident_b[:], compare_op=ALU.not_equal, fill=1.0, base=0,
                                    pattern=[[-1, P]], channel_multiplier=1))
            then(pool.memset(band[:], 0.0))
            then(pool.affine_select(out=band[:], in_=band[:], compare_op=ALU.is_ge, fill=MASKED, base=0,
                                    pattern=[[1, 256]], channel_multiplier=-1))
            then(pool.affine_select(out=band[:], in_=band[:], compare_op=ALU.is_ge, fill=MASKED, base=2 * HALF_WINDOW,
                                    pattern=[[-1, 256]], channel_multiplier=1))
            then(pool.memset(causal_q[:], 0.0))
            then(pool.affine_select(out=causal_q[:], in_=causal_q[:], compare_op=ALU.is_ge, fill=MASKED, base=0,
                                    pattern=[[-1, P]], channel_multiplier=1))
            then(pool.memset(causal_k[:], 0.0))
            then(pool.affine_select(out=causal_k[:], in_=causal_k[:], compare_op=ALU.is_ge, fill=MASKED, base=0,
                                    pattern=[[1, P]], channel_multiplier=-1))
            then(pool.memset(neg_half[:], -0.5))
            then(pool.iota(iota_e[:], pattern=[[1, E]], base=0, channel_multiplier=0,
                           allow_small_or_imprecise_dtypes=True))
            pool.wait_ge(consts_in.sem, 7 * 16)
            then(pool.tensor_scalar(out=sink4[:], in0=sink4[:], scalar1=1.0 / SCALE, scalar2=None, op0=ALU.mult))
            pool.wait_ge(w_lo.sem, 4)
            then(pool.memset(q_st[:], 0.0))
            then(pool.memset(k_st[:], 0.0))
            then(pool.memset(k_st[:, :, SHIFT:SHIFT + 1], 1.0))
            for l in (0, 1):
                then(pool.memset(v_aug[l][:], 0.0))
                then(pool.memset(v_aug[l][:, :, :, HD:HD + 1], 1.0))
            assert n_made[0] == MADE

            with pool.Fori(0, B) as b:

                def rstd_of(i):
                    for t in range(NT):
                        pool.wait_ge(*var_done[i].at(b, t + 1))
                        pool.tensor_tensor(out=rstd[:, t:t + 1], in0=mv[:, t, 1:2], in1=neg_half[:],
                                           op=ALU.pow).then_inc(rstd_done[i].sem, 1)

                for l in (0, 1):
                    nh = QKH[l]
                    kvh = (KVH0, H)[l]
                    for t in range(NT):
                        pool.wait_ge(*qkv_out[l].at(b, t + 1))
                        if t >= 1:
                            pool.wait_ge(*roped[l].at(b, t))
                        cos = rot[:, t, 0, :].unsqueeze(1).to_broadcast([P, nh, HD])
                        pool.tensor_tensor(out=rot_c[:, 0:nh * HD].rearrange("p (h d) -> p h d", d=HD),
                                           in0=qkv_sb[:, t % 2, 0:nh * HD].rearrange("p (h d) -> p h d", d=HD),
                                           in1=cos, op=ALU.mult).then_inc(cosd[l].sem, 1)
                        pool.tensor_copy(v_aug[l][:, t, :, 0:HD],
                                         qkv_sb[:, t % 2, nh * HD:(nh + kvh) * HD].rearrange("p (h d) -> p h d", d=HD)
                                         ).then_inc(v_put[l].sem, 1)
                    if l == 1:
                        for t in range(NT):
                            pool.wait_ge(*lo["x2"].at(b, t + 1))
                            pool.tensor_tensor(out=x2[:, t, :], in0=x2[:, t, :], in1=bout_sb[:],
                                               op=ALU.add).then_inc(biased.sem, 1)
                    rstd_of((0, 2)[l])
                    if l == 0:
                        for m in range(NI):
                            pool.wait_ge(*f_hi.at(b, m + 1))
                            pool.tensor_tensor(out=fT[:, 1, m, :], in0=fuse_sb[:, m % 2, :],
                                               in1=fT[:, 0, m, :].bitcast(F32), op=ALU.subtract).then_inc(f_lo.sem, 1)
                        rstd_of(1)

            pool.wait_ge(*x3_out.at(B, 0))
            for e in range(0, NE, 3):
                pool.dma_start(w13_sb[:, e:e + 3, :, :], w13[:, e:e + 3, :, :]).then_inc(w13_in.sem, 16)
                pool.dma_start(w2_sb[:, e:e + 3, :, :], w2[:, e:e + 3, :, :]).then_inc(w2_in.sem, 16)
            with pool.Fori(0, B) as b:
                for t in range(NT):
                    pool.wait_ge(*y_var.at(b, t + 1))
                    pool.tensor_tensor(out=rstd2[:, t:t + 1], in0=mv2[:, t, 1:2], in1=neg_half[:],
                                       op=ALU.pow).then_inc(y_rstd.sem, 1)

        @block.scalar
        def _(act):
            act.dma_start(rot[:], rotary.rearrange("(t p) (a d) -> p t a d", p=P, a=2)).then_inc(consts_in.sem, 16)
            act.dma_start(sink4[:], sink.partition_broadcast(P)).then_inc(consts_in.sem, 16)
            act.dma_start(sg_sb[:], s_gate).then_inc(consts_in.sem, 16)
            act.dma_start(su_sb[:], s_up).then_inc(consts_in.sem, 16)
            act.dma_start(sd_sb[:], s_down.partition_broadcast(P)).then_inc(consts_in.sem, 16)
            act.dma_start(bqkv_sb[:], b_qkv.partition_broadcast(P)).then_inc(consts_in.sem, 16)
            act.dma_start(bout_sb[:], b_out.partition_broadcast(P)).then_inc(consts_in.sem, 16)
            dst = (wqkv_s[0], wo_s[0], wqkv_s[1], wo_s[1])
            for i in range(4):
                act.wait_ge(w_in[i].sem, 16)
                act.activation(dst[i][:, 0, :, :], w_raw[i][:], ACT.Copy).then_inc(w_hi.sem, 1)

            with act.Fori(0, B) as b:

                def split_hi(n, t):
                    act.wait_ge(*tr[n].at(b, t + 1))
                    act.activation(xT[:, 0, :, t * P:(t + 1) * P],
                                   ps[:, 6 + t % 2, 0:C].rearrange("p (k q) -> p k q", k=KC),
                                   ACT.Copy).then_inc(hi[n].sem, 1)

                def attention(l):
                    n_parts = len(PARTS[l])
                    for t in range(NT):
                        split_hi(("x0", "x2")[l], t)
                    def q_copy(t):
                        act.wait_ge(*q_tr[l].at(b, t + 1))
                        act.activation(qT[:, :, t * P:(t + 1) * P], ps[:, 2:4, :].rearrange("p a (n q) -> p (a n) q", q=P),
                                       ACT.Copy).then_inc(q_out[l].sem, 1)

                    def qkv_copy(t):
                        act.wait_ge(*qkv[0].at(b, t + 1))
                        if t >= 2:
                            act.wait_ge(*roped[0].at(b, t - 1))
                            act.wait_ge(*v_put[0].at(b, t - 1))
                        act.activation(qkv_sb[:, t % 2, 0:NQKV[0]], ps[:, t % 2, 0:NQKV[0]],
                                       ACT.Copy).then_inc(qkv_out[0].sem, 1)

                    if l == 0:
                        qkv_copy(0)
                        qkv_copy(1)
                    for t in range(NT):
                        act.wait_ge(*roped[l].at(b, t + 1))
                        if t >= 1:
                            act.wait_ge(*q_tr[l].at(b, t))
                        q = rot_s[:, t % 2, 0:C].rearrange("p (h d) -> p h d", d=HD)
                        act.activation(q_st[:, :, 0:2 * HD].rearrange("p h (r d) -> p h r d", r=2).bitcast(F32R),
                                       q.unsqueeze(2).to_broadcast([P, H, 2, HD]), ACT.Copy).then_inc(st_hi[l].sem, 1)
                        if t >= 1:
                            act.wait_ge(*k_tr[l].at(b, t))
                        nk = QKH[l] - H
                        k = rot_s[:, t % 2, C:C + nk * HD].rearrange("p (h d) -> p h d", d=HD)
                        if l == 1:
                            kd = k_st[:, :, 0:4 * HD].rearrange("p h (r d) -> p h r d", r=2)[:, :, :, 0:HD]
                            act.activation(kd.bitcast(F32R), k.unsqueeze(2).to_broadcast([P, H, 2, HD]),
                                           ACT.Copy).then_inc(st_hi[l].sem, 1)
                        else:
                            kk = k_st[:, 0:2 * KVH0, :].rearrange("p (h r) s -> p h r s", r=2)
                            kb = k.unsqueeze(2).to_broadcast([P, KVH0, 2, HD])
                            act.activation(kk[:, :, :, 0:HD].bitcast(F32R), kb, ACT.Copy)
                            act.activation(kk[:, :, :, 2 * HD:3 * HD].bitcast(F32R), kb,
                                           ACT.Copy).then_inc(st_hi[l].sem, 1)
                        if l == 0 and t + 2 < NT:
                            qkv_copy(t + 2)
                        if t >= 1:
                            q_copy(t - 1)
                    q_copy(NT - 1)

                    def shift_out(g):
                        act.wait_ge(*sh_tr[l].at(b, g + 1))
                        if g >= 2:
                            act.wait_ge(*sh_row[l][g - 2].at(b, GH * 16))
                        act.activation(shift_row[:, g % 2, :], ps[0:GH, 7, :], ACT.Copy).then_inc(sh_out[l].sem, 1)

                    def oT_copy(g):
                        act.wait_ge(*pv[l].at(b, (g + 1) * n_parts))
                        if g >= 1:
                            act.wait_ge(*o_tr[l].at(b, g))
                        act.activation(oT[:], ps[:, 6, :], ACT.Copy).then_inc(oT_out[l].sem, 1)

                    for s in range(NG + 2):
                        if 1 <= s <= NG:
                            shift_out(s - 1)
                        g = s - 2
                        if g < 0:
                            continue
                        if g >= 2:
                            act.wait_ge(*pv[l].at(b, (g - 1) * n_parts))
                        col = 0
                        for p in range(n_parts):
                            n = PART_COLS[l][p]
                            for j in range(GH):
                                i = (g * n_parts + p) * GH + j
                                act.wait_ge(*scored[l].at(b, i + 1))
                                act.activation(prob[:, g % 2, j, col:col + n], ps[:, 3 + i % 3, 0:n], ACT.Exp,
                                               scale=SCALE).then_inc(exped[l].sem, 1)
                            col += n
                            if p == 0 and g >= 1:
                                oT_copy(g - 1)
                    oT_copy(NG - 1)
                    for t in range(NT):
                        split_hi(("o0", "o1")[l], t)

                attention(0)
                for t in range(NT):
                    split_hi("x1", t)
                for m in range(NI):
                    act.wait_ge(*gated.at(b, m + 1))
                    if m >= 2:
                        act.wait_ge(*fused.at(b, m - 1))
                    act.activation(gate_sb[:, m % 2, :], ps[:, m % 2, :], ACT.Silu,
                                   scale=sg_sb[:, m:m + 1]).then_inc(silued.sem, 1)
                    if m >= 1:
                        act.wait_ge(*fused.at(b, m))
                        act.activation(fT[:, 0, m - 1, :], fuse_sb[:, (m - 1) % 2, :], ACT.Copy).then_inc(f_hi.sem, 1)
                act.wait_ge(*fused.at(b, NI))
                act.activation(fT[:, 0, NI - 1, :], fuse_sb[:, (NI - 1) % 2, :], ACT.Copy).then_inc(f_hi.sem, 1)
                attention(1)

            act.wait_ge(gw_in.sem, 16)
            act.activation(gw_s[:, 0, :, :], gw_raw[:], ACT.Copy).then_inc(gw_split.sem, 1)
            with act.Fori(0, B) as b:
                for t in range(NT):
                    act.wait_ge(*xg_tr.at(b, t + 1))
                    act.activation(xgT[:, 0, :, t * P:(t + 1) * P],
                                   ps[:, 3 + t % 2, 0:C].rearrange("p (k q) -> p k q", k=KC),
                                   ACT.Copy).then_inc(xg_hi.sem, 1)
                act.wait_ge(*logits.at(b, 1))
                act.activation(score[:], ps[:, 7, 0:NT * E].rearrange("p (t e) -> p t e", e=E), ACT.Exp,
                               scale=-1.0).then_inc(exp_l.sem, 1)
                with act.Fori(0, NE) as e:
                    def hi_of(t):
                        act.wait_ge(h_tr.sem, b * UNITS + e * NT + t + 1)
                        act.activation(hT[:, t % 2, 0, :, :], ps[0:IH, 3 + t % 2, 0:2 * P].rearrange("p (k q) -> p k q", k=2),
                                       ACT.Copy).then_inc(h_hi.sem, 1)
                    for t in range(NT):
                        act.wait_ge(a_up.sem, b * UNITS + e * NT + t + 1)
                        act.activation(act_a[:, t, :], ps[:, (0, 1, 2, 7)[t], 0:I], ACT.Silu).then_inc(a_silu.sem, 1)
                        if t >= 1:
                            hi_of(t - 1)
                    hi_of(NT - 1)

        @block.vector
        def _(dve):
            dst = (wqkv_s[0], wo_s[0], wqkv_s[1], wo_s[1])
            dve.memset(zero_r[:], 0.0).then_inc(start_dve.sem, 1)
            for i, sig in enumerate((normed[0], y_done, y_norm, a_h, y_out)):
                dve.memset(carry[:, i + 1:i + 2], 0.0).then_inc(sig.sem, sig.primed)
            for i in range(4):
                dve.wait_ge(w_hi.sem, i + 1)
                dve.tensor_tensor(out=dst[i][:, 1, :, :], in0=w_raw[i][:], in1=dst[i][:, 0, :, :].bitcast(F32),
                                  op=ALU.subtract).then_inc(w_lo.sem, 1)
            dve.wait_ge(consts_in.sem, 7 * 16)
            dve.wait_ge(made.sem, MADE)

            with dve.Fori(0, B) as b:
                steps = [0]

                def then(ins, carrier=False):
                    steps[0] += 1
                    ins.then_inc(dve_step.sem, 1)
                    dve.wait_ge(*dve_step.at(b, steps[0]))
                    if carrier:
                        dve.memset(carry[:, 0:1], 0.0)

                def split_lo(n, t):
                    dve.wait_ge(*hi[n].at(b, t + 1))
                    dve.tensor_tensor(out=xT[:, 1, :, t * P:(t + 1) * P],
                                      in0=ps[:, 6 + t % 2, 0:C].rearrange("p (k q) -> p k q", k=KC),
                                      in1=xT[:, 0, :, t * P:(t + 1) * P].bitcast(F32),
                                      op=ALU.subtract).then_inc(lo[n].sem, 1)

                def norm(i, ready, bank0, scale, residual, result):
                    for t in range(NT):
                        dve.wait_ge(*ready.at(b, t + 1))
                        y = ps[:, bank0 + t % 2, 0:C]
                        if scale is not None:
                            then(dve.tensor_tensor(out=result[:, t, :], in0=y, in1=scale, op=ALU.mult))
                            y = result[:, t, :]
                        if i == 2:
                            dve.wait_ge(*biased.at(b, t + 1))
                        then(dve.tensor_tensor(out=result[:, t, :], in0=y, in1=residual[:, t, :], op=ALU.add))
                        then(dve.bn_stats(out=stats[:, t, :], in_=result[:, t, :]), carrier=True)
                        then(dve.bn_aggr(out=mv[:, t, :], in_=stats[:, t, :]))
                        dve.tensor_scalar(out=mv[:, t, 1:2], in0=mv[:, t, 1:2], scalar1=EPS, scalar2=None,
                                          op0=ALU.add).then_inc(var_done[i].sem, 1)
                        if t >= 1:
                            scale_tile(i, t - 1, result)
                    scale_tile(i, NT - 1, result)

                def scale_tile(i, t, result):
                    dve.wait_ge(*rstd_done[i].at(b, t + 1))
                    dve.tensor_scalar(out=result[:, t, :], in0=result[:, t, :], scalar1=mv[:, t, 0:1],
                                      scalar2=rstd[:, t:t + 1], op0=ALU.subtract, op1=ALU.mult).then_inc(normed[i].sem, 1)

                def attention(l):
                    n_parts, n_items = len(PARTS[l]), len(MAX_ITEMS[l])
                    nh = QKH[l]
                    nk = nh - H
                    for t in range(NT):
                        split_lo(("x0", "x2")[l], t)

                    def bias_out(t):
                        dve.wait_ge(*qkv[1].at(b, t + 1))
                        if t >= 2:
                            dve.wait_ge(*v_put[1].at(b, t - 1))
                            dve.wait_ge(*roped[1].at(b, t - 1))
                        bank = (0, 4)[t % 2]
                        dve.tensor_tensor(out=qkv_sb[:, t % 2, :], in0=ps[:, bank:bank + 2, :].rearrange("p a n -> p (a n)")[:, 0:3 * C],
                                          in1=bqkv_sb[:], op=ALU.add).then_inc(qkv_out[1].sem, 1)

                    if l == 1:
                        bias_out(0)
                    for t in range(NT):
                        if l == 1 and t + 1 < NT:
                            bias_out(t + 1)
                        dve.wait_ge(*qkv_out[l].at(b, t + 1))
                        src = qkv_sb[:, t % 2, 0:nh * HD].rearrange("p (h i a) -> p h i a", i=HD // 2, a=2)
                        dst_ = rot_s[:, t % 2, 0:nh * HD].rearrange("p (h i a) -> p h i a", i=HD // 2, a=2)
                        sin = rot[:, t, 1, :].rearrange("p (i a) -> p i a", a=2)
                        if t >= 2:
                            dve.wait_ge(*st_hi[l].at(b, 2 * (t - 1)))
                            dve.wait_ge(*st_lo[l].at(b, 2 * (t - 1)))
                        for a in (0, 1):
                            ins = dve.tensor_tensor(out=dst_[:, :, :, a], in0=src[:, :, :, 1 - a],
                                                    in1=sin[:, :, a].unsqueeze(1).to_broadcast([P, nh, HD // 2]), op=ALU.mult)
                            if a:
                                then(ins)
                        dve.wait_ge(*cosd[l].at(b, t + 1))
                        dve.tensor_tensor(out=rot_s[:, t % 2, 0:nh * HD], in0=rot_s[:, t % 2, 0:nh * HD],
                                          in1=rot_c[:, 0:nh * HD], op=ALU.add).then_inc(roped[l].sem, 1)
                        dve.wait_ge(*st_hi[l].at(b, 2 * t + 1))
                        q = rot_s[:, t % 2, 0:C].rearrange("p (h d) -> p h d", d=HD)
                        dve.tensor_tensor(out=q_st[:, :, 2 * HD:3 * HD], in0=q, in1=q_st[:, :, 0:HD],
                                          op=ALU.subtract).then_inc(st_lo[l].sem, 1)
                        dve.wait_ge(*st_hi[l].at(b, 2 * t + 2))
                        k = rot_s[:, t % 2, C:C + nk * HD].rearrange("p (h d) -> p h d", d=HD)
                        if l == 1:
                            dve.tensor_tensor(out=k_st[:, :, HD:2 * HD], in0=k, in1=k_st[:, :, 0:HD],
                                              op=ALU.subtract).then_inc(st_lo[l].sem, 1)
                        else:
                            kk = k_st[:, 0:2 * KVH0, :].rearrange("p (h r) s -> p h r s", r=2)
                            dve.tensor_tensor(out=kk[:, :, :, HD:2 * HD], in0=k.unsqueeze(2).to_broadcast([P, KVH0, 2, HD]),
                                              in1=kk[:, :, :, 0:HD], op=ALU.subtract).then_inc(st_lo[l].sem, 1)
                        if t >= 1:
                            k_copy(l, t - 1)
                    k_copy(l, NT - 1)

                    def normalise(g):
                        dve.wait_ge(*o_tr[l].at(b, g + 1))
                        o4 = ps[:, 7, :].rearrange("p (t h d) -> p t h d", t=NT, d=32)
                        dve.reciprocal(rden[:], o4[:, :, :, HD]).then_inc(rden_done[l].sem, 1)
                        dve.wait_ge(*rden_done[l].at(b, g + 1))
                        dve.tensor_tensor(
                            out=o_sb[:, :, g * GH * HD:(g + 1) * GH * HD].rearrange("p t (h d) -> p t h d", d=HD),
                            in0=o4[:, :, :, 0:HD], in1=rden[:].unsqueeze(3).to_broadcast([P, NT, GH, HD]),
                            op=ALU.mult).then_inc(o_put[l].sem, 1)

                    for s in range(NG + 2):
                        if s < NG:
                            for i, (t, j) in enumerate(MAX_ITEMS[l]):
                                n = query_tile_keys(l, t)[1]
                                mh = MAX_HEADS[l][t]
                                k = s * n_items + i
                                dve.wait_ge(*raw_score[l].at(b, k + 1))
                                dve.tensor_reduce(out=negmax[:, t, s * GH + j:(s + 1) * GH:GH // mh],
                                                  in_=ps[:, k % 3, 0:mh * n].rearrange("p (h n) -> p h n", n=n),
                                                  axis=AX.X, op=ALU.max, negate=True).then_inc(maxed[l].sem, 1)
                            if l == 0:
                                dve.wait_ge(*maxed[0].at(b, (s + 1) * n_items))
                                nm = negmax[:, :, s * GH:(s + 1) * GH]
                                sk = sink4[:, s * GH:(s + 1) * GH].unsqueeze(1).to_broadcast([P, NT, GH])
                                then(dve.tensor_tensor(out=nm, in0=nm, in1=sk, op=ALU.subtract))
                                dve.tensor_tensor(out=nm, in0=nm, in1=sk, op=ALU.add).then_inc(sunk.sem, 1)
                        if s >= 3:
                            normalise(s - 3)
                    normalise(NG - 1)
                    for t in range(NT):
                        split_lo(("o0", "o1")[l], t)

                def k_copy(l, t):
                    n_blk = (KVH0, PAIRS)[l]
                    dve.wait_ge(*k_tr[l].at(b, t + 1))
                    dve.tensor_copy(kT[:, 0:n_blk, t * P:(t + 1) * P],
                                    ps[:, 6:8, :].rearrange("p a (n q) -> p (a n) q", q=P)[:, 0:n_blk, :]).then_inc(k_out[l].sem, 1)

                attention(0)
                norm(0, proj[0], 0, None, x0[:, 0, :, :], x1)
                for t in range(NT):
                    split_lo("x1", t)
                for m in range(NI):
                    dve.wait_ge(*silued.at(b, m + 1))
                    dve.wait_ge(*upped.at(b, m + 1))
                    if m >= 2:
                        dve.wait_ge(*f_lo.at(b, m - 1))
                    dve.scalar_tensor_tensor(out=fuse_sb[:, m % 2, :], in0=ps[:, 2 + m % 2, :], scalar=su_sb[:, m:m + 1],
                                             in1=gate_sb[:, m % 2, :], op0=ALU.mult, op1=ALU.mult).then_inc(fused.sem, 1)
                norm(1, down, 4, sd_sb[:], x1, x2)
                attention(1)
                norm(2, proj[1], 0, None, x2, x3)
                assert steps[0] == DVE_STEPS, steps[0]

            dve.wait_ge(gw_split.sem, 1)
            dve.tensor_tensor(out=gw_s[:, 1, :, :], in0=gw_raw[:], in1=gw_s[:, 0, :, :].bitcast(F32),
                              op=ALU.subtract).then_inc(gw_split.sem, 1)
            dve.memset(dw[:], 1.0).then_inc(start_dve.sem, 1)
            dve.wait_ge(start_dve.sem, 2)
            with dve.Fori(0, B) as b:
                steps = [0]

                def then(ins, carrier=False):
                    steps[0] += 1
                    ins.then_inc(moe_step.sem, 1)
                    dve.wait_ge(*moe_step.at(b, steps[0]))
                    if carrier:
                        dve.memset(carry[:, 0:1], 0.0)

                for t in range(NT):
                    dve.wait_ge(*xg_hi.at(b, t + 1))
                    dve.tensor_tensor(out=xgT[:, 1, :, t * P:(t + 1) * P],
                                      in0=ps[:, 3 + t % 2, 0:C].rearrange("p (k q) -> p k q", k=KC),
                                      in1=xgT[:, 0, :, t * P:(t + 1) * P].bitcast(F32),
                                      op=ALU.subtract).then_inc(xg_lo.sem, 1)
                dve.wait_ge(*exp_l.at(b, 1))
                then(dve.tensor_scalar(out=score[:], in0=score[:], scalar1=1.0, scalar2=None, op0=ALU.add))
                then(dve.reciprocal(score[:], score[:]), carrier=True)
                for t in range(NT):
                    then(dve.max(out=top8[:, t, :], in_=score[:, t, :]), carrier=True)
                    then(dve.max_index(out=idx8[:, t, :], in_max=top8[:, t, :], in_values=score[:, t, :]), carrier=t < NT - 1)
                then(dve.tensor_copy(idxf[:], idx8[:, :, 0:2]))
                then(dve.tensor_tensor(out=tsum[:], in0=top8[:, :, 0], in1=top8[:, :, 1], op=ALU.add))
                then(dve.reciprocal(tsum[:], tsum[:]))
                then(dve.tensor_tensor(out=topw[:], in0=top8[:, :, 0:2], in1=tsum[:].unsqueeze(2).to_broadcast([P, NT, 2]),
                                       op=ALU.mult))
                for s in (0, 1):
                    then(dve.tensor_tensor(out=hot[:, :, s, :], in0=iota_e[:].unsqueeze(1).to_broadcast([P, NT, E]),
                                           in1=idxf[:, :, s:s + 1].to_broadcast([P, NT, E]), op=ALU.is_equal))
                    then(dve.tensor_tensor(out=hot[:, :, s, :], in0=hot[:, :, s, :],
                                           in1=topw[:, :, s:s + 1].to_broadcast([P, NT, E]), op=ALU.mult))
                dve.tensor_tensor(out=dw[:, 0:E, :].rearrange("p e t -> p t e"), in0=hot[:, :, 0, :], in1=hot[:, :, 1, :],
                                  op=ALU.add).then_inc(routed.sem, 1)
                dve.wait_ge(*routed.at(b, 1))
                dve.memset(carry[:, 0:1], 0.0)
                with dve.Fori(0, NE) as e:
                    def lo_of(t):
                        dve.wait_ge(h_hi.sem, b * UNITS + e * NT + t + 1)
                        dve.tensor_tensor(out=hT[:, t % 2, 1, :, :], in0=ps[0:IH, 3 + t % 2, 0:2 * P].rearrange("p (k q) -> p k q", k=2),
                                          in1=hT[:, t % 2, 0, :, :].bitcast(F32), op=ALU.subtract).then_inc(h_lo.sem, 1)
                    for t in range(NT):
                        dve.wait_ge(a_silu.sem, b * UNITS + e * NT + t + 1)
                        dve.scalar_tensor_tensor(out=h_sb[:, t, :], in0=act_a[:, t, :], scalar=dw[:, bass.ds(e, 1), t],
                                                 in1=ps[:, (0, 1, 2, 7)[t], I:2 * I], op0=ALU.mult,
                                                 op1=ALU.mult).then_inc(a_h.sem, 1)
                        if t >= 1:
                            lo_of(t - 1)
                    lo_of(NT - 1)
                dve.wait_ge(*h_down.at(b, UNITS))
                dve.tensor_tensor(out=yy[:], in0=ps[:, 5:7, :].rearrange("p a (t c) -> p (a t) c", c=C), in1=xg[:],
                                  op=ALU.add).then_inc(y_done.sem, 1)
                dve.wait_ge(*y_done.at(b, 1))
                for t in range(NT):
                    then(dve.bn_stats(out=stats2[:, t, :], in_=yy[:, t, :]), carrier=True)
                    then(dve.bn_aggr(out=mv2[:, t, :], in_=stats2[:, t, :]))
                    dve.tensor_scalar(out=mv2[:, t, 1:2], in0=mv2[:, t, 1:2], scalar1=EPS, scalar2=None,
                                      op0=ALU.add).then_inc(y_var.sem, 1)
                dve.wait_ge(*y_out.at(b, 0))
                for t in range(NT):
                    dve.wait_ge(*y_rstd.at(b, t + 1))
                    dve.tensor_scalar(out=yo[:, t, :], in0=yy[:, t, :], scalar1=mv2[:, t, 0:1], scalar2=rstd2[:, t:t + 1],
                                      op0=ALU.subtract, op1=ALU.mult).then_inc(y_norm.sem, 1)
                assert steps[0] == MOE_STEPS, steps[0]

        @block.tensor
        def _(pe):
            pe.wait_ge(made.sem, MADE)
            pe.wait_ge(start_dve.sem, 1)
            pe.wait_ge(w_lo.sem, 4)
            EXACT = ((0, 0), (0, 1), (1, 0))
            with pe.Fori(0, B) as b:

                def split_tr(n, src, ready, t):
                    pe.wait_ge(*ready)
                    if t >= 2:
                        pe.wait_ge(*lo[n].at(b, t - 1))
                    for k in range(KC):
                        ins = pe.transpose(ps[:, 6 + t % 2, k * P:(k + 1) * P], src[:, t, k * P:(k + 1) * P], ident[:])
                    ins.then_inc(tr[n].sem, 1)

                def product(dst, t, w, c0, n):
                    for i, (a, w_part) in enumerate(EXACT):
                        for k in range(KC):
                            ins = pe.matmul(dst, xT[:, a, k, t * P:(t + 1) * P], w[:, w_part, k, c0:c0 + n],
                                            start=(i + k == 0), stop=(i == 2 and k == KC - 1))
                    return ins

                def attention(l, src):
                    name = ("x0", "x2")[l]
                    n_parts, n_items = len(PARTS[l]), len(MAX_ITEMS[l])
                    for t in range(NT):
                        split_tr(name, src, x0_in.at(b, 16) if l == 0 else normed[1].at(b, t + 1), t)
                    for t in range(NT):
                        pe.wait_ge(*lo[name].at(b, t + 1))
                        if t >= 2:
                            pe.wait_ge(*qkv_out[l].at(b, t - 1))
                        if l == 0:
                            product(ps[:, t % 2, 0:NQKV[0]], t, wqkv_s[0], 0, NQKV[0]).then_inc(qkv[0].sem, 1)
                        else:
                            bank = (0, 4)[t % 2]
                            product(ps[:, bank, :], t, wqkv_s[1], 0, 512)
                            product(ps[:, bank + 1, 0:256], t, wqkv_s[1], 512, 256).then_inc(qkv[1].sem, 1)
                    n_blk = (KVH0, PAIRS)[l]
                    for t in range(NT):
                        pe.wait_ge(*st_lo[l].at(b, 2 * t + 1))
                        if t >= 1:
                            pe.wait_ge(*q_out[l].at(b, t))
                        for n in range(PAIRS):
                            ins = pe.transpose(ps[:, 2 + n // 4, (n % 4) * P:(n % 4 + 1) * P],
                                               q_st[:, 2 * n:2 * n + 2, :].rearrange("p h s -> p (h s)"), ident[:])
                        ins.then_inc(q_tr[l].sem, 1)
                        pe.wait_ge(*st_lo[l].at(b, 2 * t + 2))
                        if t >= 1:
                            pe.wait_ge(*k_out[l].at(b, t))
                        for n in range(n_blk):
                            ins = pe.transpose(ps[:, 6 + n // 4, (n % 4) * P:(n % 4 + 1) * P],
                                               k_st[:, 2 * n:2 * n + 2, :].rearrange("p h s -> p (h s)"), ident[:])
                        ins.then_inc(k_tr[l].sem, 1)

                    def raw_item(g, i):
                        t, j = MAX_ITEMS[l][i]
                        k0, n = query_tile_keys(l, t)
                        item = g * n_items + i
                        if item >= 3:
                            pe.wait_ge(*maxed[l].at(b, item - 2))
                        bank = item % 3
                        for jj in range(MAX_HEADS[l][t]):
                            h = g * GH + j + jj * (GH // MAX_HEADS[l][t])
                            p0 = STACK * (h % 2)
                            dst = ps[:, bank, jj * n:(jj + 1) * n]
                            if l == 0:
                                m0 = k0 - (t * P - HALF_WINDOW)
                                pe.matmul(dst, ident_b[:], band[:, m0:m0 + n], start=True, stop=False, skip_group_check=True)
                            else:
                                pe.matmul(ps[:, bank, (jj + 1) * n - P:(jj + 1) * n], ident_b[:], causal_q[:],
                                          start=True, stop=False, skip_group_check=True)
                            ins = pe.matmul(dst, qT[p0:p0 + SHIFT, h // 2, t * P:(t + 1) * P],
                                            kT[p0:p0 + SHIFT, h // 4 if l == 0 else h // 2, k0:k0 + n],
                                            start=False, stop=True, skip_group_check=True)
                        ins.then_inc(raw_score[l].sem, 1)

                    def score_item(g, i):
                        p, j = i // GH, i % GH
                        h = g * GH + j
                        item = g * n_parts * GH + i
                        if item >= 3:
                            pe.wait_ge(*exped[l].at(b, item - 2))
                        p0 = STACK * (h % 2)
                        for kt, col in PARTS[l][p]:
                            q0, n = key_tile_queries(l, kt)
                            dst = ps[:, 3 + item % 3, col:col + n]
                            if l == 0:
                                m0 = q0 - (kt * P - HALF_WINDOW)
                                pe.matmul(dst, ident_b[:], band[:, m0:m0 + n], start=True, stop=False, skip_group_check=True)
                            else:
                                pe.matmul(ps[:, 3 + item % 3, col:col + P], ident_b[:], causal_k[:],
                                          start=True, stop=False, skip_group_check=True)
                            ins = pe.matmul(dst, kT[p0:p0 + SHIFT + 1, h // 4 if l == 0 else h // 2, kt * P:(kt + 1) * P],
                                            qT[p0:p0 + SHIFT + 1, h // 2, q0:q0 + n], start=False, stop=True,
                                            skip_group_check=True)
                        ins.then_inc(scored[l].sem, 1)

                    def pv_part(g, p):
                        pe.wait_ge(*exped[l].at(b, (g * n_parts + p + 1) * GH))
                        if p == 0 and g >= 1:
                            pe.wait_ge(*oT_out[l].at(b, g))
                        off = sum(PART_COLS[l][:p])
                        for i, (kt, _) in enumerate(PARTS[l][p]):
                            q0, n = key_tile_queries(l, kt)
                            for j in range(GH):
                                h = g * GH + j
                                ins = pe.matmul(ps[32 * j:32 * j + 32, 6, q0:q0 + n],
                                                v_aug[l][:, kt, h // 4 if l == 0 else h, :],
                                                prob[:, g % 2, j, off:off + n], start=(p == 0 and i == 0),
                                                stop=(p == n_parts - 1 and i == len(PARTS[l][p]) - 1), skip_group_check=True)
                            off += n
                        ins.then_inc(pv[l].sem, 1)

                    def o_transposes(g):
                        pe.wait_ge(*oT_out[l].at(b, g + 1))
                        if g >= 1:
                            pe.wait_ge(*o_put[l].at(b, g))
                        for t in range(NT):
                            ins = pe.transpose(ps[:, 7, t * P:(t + 1) * P], oT[:, t * P:(t + 1) * P], ident[:])
                        ins.then_inc(o_tr[l].sem, 1)

                    pe.wait_ge(*q_out[l].at(b, NT))
                    pe.wait_ge(*k_out[l].at(b, NT))
                    pe.wait_ge(*v_put[l].at(b, NT))
                    for s in range(NG + 2):
                        g = s - 2
                        if 1 <= s <= NG:
                            if l == 0:
                                pe.wait_ge(*sunk.at(b, s))
                            else:
                                pe.wait_ge(*maxed[1].at(b, s * n_items))
                            if s >= 2:
                                pe.wait_ge(*sh_out[l].at(b, s - 1))
                            if s >= 4:
                                pe.wait_ge(*o_put[l].at(b, s - 3))
                            for t in range(NT):
                                ins = pe.transpose(ps[0:GH, 7, t * P:(t + 1) * P], negmax[:, t, (s - 1) * GH:s * GH], ident[:])
                            ins.then_inc(sh_tr[l].sem, 1)
                        if g >= 0:
                            pe.wait_ge(*sh_row[l][g].at(b, GH * 16))
                        for i in range(max(n_items, n_parts * GH)):
                            if g >= 0 and i < n_parts * GH:
                                score_item(g, i)
                            if s < NG and i < n_items:
                                raw_item(s, i)
                            if g >= 1 and i == 1:
                                pv_part(g - 1, n_parts - 1)
                            if g >= 1 and i == GH + 2:
                                if s <= NG:
                                    pe.wait_ge(*sh_out[l].at(b, s))
                                o_transposes(g - 1)
                            if g >= 0 and i % GH == 2 and 1 <= i // GH < n_parts:
                                pv_part(g, i // GH - 1)
                    pv_part(NG - 1, n_parts - 1)
                    o_transposes(NG - 1)
                    name = ("o0", "o1")[l]
                    for t in range(NT):
                        split_tr(name, o_sb, o_put[l].at(b, NG), t)
                    for t in range(NT):
                        pe.wait_ge(*lo[name].at(b, t + 1))
                        if t >= 2:
                            pe.wait_ge(*normed[2 * l].at(b, t - 1))
                        product(ps[:, t % 2, 0:C], t, wo_s[l], 0, C).then_inc(proj[l].sem, 1)

                attention(0, x0[:, 0, :, :])
                for t in range(NT):
                    split_tr("x1", x1, normed[0].at(b, t + 1), t)
                pe.wait_ge(w_int8.sem, 48)
                pe.wait_ge(*lo["x1"].at(b, NT))
                for m in range(NI):
                    for w, bank0, sig, free in ((wg_sb, 0, gated, silued), (wu_sb, 2, upped, fused)):
                        if m >= 2:
                            pe.wait_ge(*free.at(b, m - 1))
                        for part in (0, 1):
                            for k in range(KC):
                                ins = pe.matmul(ps[:, bank0 + m % 2, :], w[:, k, m * P:(m + 1) * P], xT[:, part, k, :],
                                                start=(part + k == 0), stop=(part == 1 and k == KC - 1))
                        ins.then_inc(sig.sem, 1)
                for t in range(NT):
                    if t >= 2:
                        pe.wait_ge(*normed[1].at(b, t - 1))
                    for m in range(NI):
                        if t == 0:
                            pe.wait_ge(*f_lo.at(b, m + 1))
                        for part in (0, 1):
                            ins = pe.matmul(ps[:, 4 + t % 2, 0:C], fT[:, part, m, t * P:(t + 1) * P], wd_sb[:, m, :],
                                            start=(m + part == 0), stop=(m == NI - 1 and part == 1))
                    ins.then_inc(down.sem, 1)
                attention(1, x2)

            pe.wait_ge(*normed[2].at(B, 0))
            pe.wait_ge(gw_split.sem, 2)
            with pe.Fori(0, B) as b:
                pe.wait_ge(*xg_in.at(b, 16))
                for t in range(NT):
                    if t >= 2:
                        pe.wait_ge(*xg_lo.at(b, t - 1))
                    for k in range(KC):
                        ins = pe.transpose(ps[:, 3 + t % 2, k * P:(k + 1) * P], xg[:, t, k * P:(k + 1) * P], ident[:])
                    ins.then_inc(xg_tr.sem, 1)
                pe.wait_ge(*xg_lo.at(b, NT))
                for t in range(NT):
                    for i, (a, w_part) in enumerate(EXACT):
                        for k in range(KC):
                            ins = pe.matmul(ps[:, 7, t * E:(t + 1) * E], xgT[:, a, k, t * P:(t + 1) * P], gw_s[:, w_part, k, :],
                                            start=(i + k == 0), stop=(i == 2 and k == KC - 1))
                ins.then_inc(logits.sem, 1)
                pe.wait_ge(*y_done.at(b, 0))
                pe.wait_ge(*routed.at(b, 1))
                pe.wait_ge(w13_in.sem, 16 * NE // 3)
                pe.wait_ge(w2_in.sem, 16 * NE // 3)
                for bank in (5, 6):
                    pe.matmul(ps[:, bank, :], zero_r[:, 0:P], zero_r[:], start=True, stop=False, skip_group_check=True)
                with pe.Fori(0, NE) as e:
                    def up(t):
                        pe.wait_ge(a_h.sem, 1 + b * UNITS + e * NT)
                        for part in (0, 1):
                            for k in range(KC):
                                ins = pe.matmul(ps[:, (0, 1, 2, 7)[t], 0:2 * I], xgT[:, part, k, t * P:(t + 1) * P],
                                                w13_sb[:, bass.ds(e, 1), k, :], start=(part + k == 0), stop=(part == 1 and k == KC - 1))
                        ins.then_inc(a_up.sem, 1)

                    def transposes(t):
                        pe.wait_ge(a_h.sem, 1 + b * UNITS + e * NT + t + 1)
                        if t >= 2:
                            pe.wait_ge(h_lo.sem, b * UNITS + e * NT + t - 1)
                        for k in (0, 1):
                            ins = pe.transpose(ps[0:IH, 3 + t % 2, k * P:(k + 1) * P], h_sb[:, t, k * IH:(k + 1) * IH], ident[:])
                        ins.then_inc(h_tr.sem, 1)

                    def down_(t):
                        pe.wait_ge(h_lo.sem, b * UNITS + e * NT + t + 1)
                        for part in (0, 1):
                            for k in (0, 1):
                                ins = pe.matmul(ps[:, 5 + t // 2, (t % 2) * C:(t % 2 + 1) * C], hT[:, t % 2, part, k, :],
                                                w2_sb[:, bass.ds(e, 1), k, :], start=False, stop=False, skip_group_check=True)
                        ins.then_inc(h_down.sem, 1)

                    for t in range(NT + 2):
                        if t < NT:
                            up(t)
                        if 1 <= t <= NT:
                            transposes(t - 1)
                        if t >= 2:
                            down_(t - 2)


MADE = 21
_INPUTS = ("x", "wqkv0", "wo0", "sink", "w_gate", "w_up", "w_down", "s_gate", "s_up", "s_down",
           "wqkv1", "b_qkv", "wo1", "b_out", "gate_w", "w13", "w2", "rotary")


def lay_out(inputs):
    g = {n: np.asarray(v) for n, v in inputs.items()}
    a = {
        "x": g["L0_attn_x"],
        "wqkv0": np.concatenate([g["L0_attn_wq"], g["L0_attn_wk"], g["L0_attn_wv"]], 1),
        "wo0": g["L0_attn_wo"], "sink": g["L0_attn_sink"].reshape(H),
        "w_gate": np.ascontiguousarray(g["L0_ffn_w_gate"]).view(np.int32), "w_up": np.ascontiguousarray(g["L0_ffn_w_up"]).view(np.int32), "w_down": np.ascontiguousarray(g["L0_ffn_w_down"]).view(np.int32),
        "s_gate": g["L0_ffn_s_gate"].reshape(NI, P).T, "s_up": g["L0_ffn_s_up"].reshape(NI, P).T, "s_down": g["L0_ffn_s_down"],
        "wqkv1": g["L1_attn_w_qkv"].T, "b_qkv": g["L1_attn_b_qkv"],
        "wo1": g["L1_attn_w_out"].T, "b_out": g["L1_attn_b_out"], "gate_w": g["L1_ffn_gate_w"].T,
        "rotary": rotary_tables(),
    }
    w1 = np.concatenate([g["L1_ffn_w1"], g["L1_ffn_sw1"].reshape(SHARED, I, C)])
    w3 = np.concatenate([g["L1_ffn_w3"], g["L1_ffn_sw3"].reshape(SHARED, I, C)])
    w2 = np.concatenate([g["L1_ffn_w2"], g["L1_ffn_sw2"].reshape(C, SHARED, I).transpose(1, 0, 2)])
    a["w13"] = np.concatenate([w1, w3], 1).reshape(NE, 2 * I, KC, P).transpose(3, 0, 2, 1)
    a["w2"] = w2.reshape(NE, C, 2, IH).transpose(3, 0, 2, 1)
    return {n: np.ascontiguousarray(v) for n, v in a.items()}


def kernel(**inputs):
    import concourse.bacc as bacc
    from concourse.bass_utils import run_bass_kernel_spmd

    arrays = lay_out(inputs)
    nc = bacc.Bacc("TRN2", target_bir_lowering=False, num_devices=1)
    args = [nc.dram_tensor(f"in_{n}", arrays[n].shape, mybir.dt.from_np(arrays[n].dtype), kind="ExternalInput").ap()
            for n in _INPUTS]
    out = nc.dram_tensor("out", (B, T, C), F32, kind="ExternalOutput").ap()
    build(nc, *args, out)
    r = run_bass_kernel_spmd(nc, [{f"in_{n}": arrays[n] for n in _INPUTS}], core_ids=[0])
    return r.results[0]["out"]
```

```python
import numpy as np
import concourse.bass as bass
from concourse import mybir
from contextlib import ExitStack

F32, F32R, BF16 = mybir.dt.float32, mybir.dt.float32r, mybir.dt.bfloat16
I8, I32, U32 = mybir.dt.int8, mybir.dt.int32, mybir.dt.uint32
ALU = mybir.AluOpType
ACT = mybir.ActivationFunctionType
AX = mybir.AxisListType

P = 128
B, T, C = 4, 512, 256
NT, KC = T // P, C // P
H, HD = 16, 16
KVH0 = 4
HALF_WINDOW = 64
NG, GH = 4, 4
NQKV = (C + 2 * KVH0 * HD, 3 * C)
QKH = (H + KVH0, 2 * H)
INTER = 1024
NI = INTER // P
E, I = 16, 176
SHARED = 2
NE = E + SHARED
IH = I // 2
TOK = B * T
TT = B * NT
NS = (2 * TOK + E * (P - 1)) // P
EPS = 1e-5
SCALE = HD ** -0.5
MASKED = -1e30

STACK = 64
SHIFT = 3 * HD
PAIRS = H // 2


def key_tile_queries(layer, kt):
    if layer == 1:
        return kt * P, T - kt * P
    lo, hi = max(0, kt * P - HALF_WINDOW), min(T, (kt + 1) * P + HALF_WINDOW)
    return lo, hi - lo


def query_tile_keys(layer, t):
    if layer == 1:
        return 0, (t + 1) * P
    return key_tile_queries(0, t)


PARTS = ([[(0, 0), (1, 192)], [(2, 0), (3, 256)]],
         [[(0, 0)], [(1, 0), (3, 384)], [(2, 0)]])
PART_COLS = tuple([sum(key_tile_queries(l, kt)[1] for kt, _ in part) for part in PARTS[l]] for l in (0, 1))
PROB_COLS = max(sum(c) for c in PART_COLS)
MAX_HEADS = tuple([min(2, 512 // query_tile_keys(l, t)[1]) for t in range(NT)] for l in (0, 1))
MAX_ITEMS = tuple([(t, j) for t in range(NT) for j in range(GH // MAX_HEADS[l][t])] for l in (0, 1))


class Signal:

    def __init__(self, sem, per, primed=0, before=0):
        self.sem, self.per, self.primed, self.before = sem, per, primed, before

    def at(self, turn, n):
        return self.sem, turn * self.per + (n + self.before + self.primed)


PEELED = 7
STEP_TURNS = (NS - PEELED) // 4


def run_steps(eng, step):
    assert PEELED + 4 * STEP_TURNS == NS

    def straight(q):
        step(q, q % 4, lambda stage: 0 <= q - stage < NS, lambda stage: (q - stage) // 4)

    for q in range(PEELED):
        straight(q)
    with eng.Fori(0, STEP_TURNS) as m:
        for i in range(PEELED, PEELED + 4):
            step(m * 4 + i, i % 4, lambda stage: True, lambda stage: m + (i - stage) // 4)
    for q in range(NS, NS + 3):
        straight(q)


def rotary_tables():
    half = HD // 2
    inv = (np.float32(1.0) / np.float32(10000.0) ** (np.arange(half, dtype=np.float32) / np.float32(half))).astype(np.float32)
    f = np.arange(T, dtype=np.float32)[:, None] * inv[None, :]
    c, s = np.cos(f).astype(np.float32), np.sin(f).astype(np.float32)
    cos = np.stack([c, c], -1).reshape(T, HD)
    sin = np.stack([-s, s], -1).reshape(T, HD)
    return np.ascontiguousarray(np.concatenate([cos, sin], 1))


def build(nc, x, wqkv0, wo0, sink, w_gate, w_up, w_down, s_gate, s_up, s_down,
          wqkv1, b_qkv, wo1, b_out, gate_w, w13, w2, rotary, out):
    ctx = ExitStack()
    scope = [ctx]

    def sb(name, shape, dt=F32):
        return scope[-1].enter_context(nc.sbuf_tensor(name, shape, dt))

    def signal(name, per, primed=0):
        return Signal(ctx.enter_context(nc.semaphore(name)), per, primed)

    x3_dram = nc.dram_tensor("x3_rows", (B, T, C), F32, kind="Internal").ap().rearrange("b (t p) c -> b p t c", p=P)
    def staged(name, *raises):
        sem = ctx.enter_context(nc.semaphore(name))
        return [Signal(sem, sum(raises), 0, sum(raises[:i])) for i in range(len(raises))]

    xs_dram = nc.dram_tensor("slot_x", (NS * P, C), F32, kind="Internal").ap()
    ys_dram = nc.dram_tensor("slot_y", (NS * P, C), F32, kind="Internal").ap()

    with ctx:
        ps = ctx.enter_context(nc.psum_tensor("ps", [P, 8, 512], F32))

        ident = sb("ident", [P, P])
        ident_b = sb("ident_b", [P, P], BF16)
        band = sb("band", [P, 256], BF16)
        causal_q = sb("causal_q", [P, P], BF16)
        causal_k = sb("causal_k", [P, P], BF16)
        rot = sb("rot", [P, NT, 2, HD])
        carry = sb("carry", [P, 8])
        neg_half = sb("neg_half", [P, 1])
        sink4 = sb("sink4", [P, H])
        iota_e = sb("iota_e", [P, E])
        zeros = sb("zeros", [P, C])
        tri = sb("tri", [P, P], BF16)
        ones_b = sb("ones_b", [P, P], BF16)
        iota_s = sb("iota_s", [P, NS])
        hot_all = sb("hot_all", [P, TT, 2, E])
        topw_all = sb("topw_all", [P, TT, 2])
        score = sb("score", [P, NT, E])
        top8 = sb("top8", [P, NT, 8])
        idx8 = sb("idx8", [P, NT, 8], U32)
        idxf = sb("idxf", [P, NT, 2])
        tsum = sb("tsum", [P, NT])
        phase1 = ExitStack()
        scope.append(phase1)
        wqkv_s = [sb(f"wqkv{l}_s", [P, 2, KC, NQKV[l]], F32R) for l in (0, 1)]
        wo_s = [sb(f"wo{l}_s", [P, 2, KC, C], F32R) for l in (0, 1)]
        wg_sb = sb("wg_sb", [P, KC, INTER], F32R)
        wu_sb = sb("wu_sb", [P, KC, INTER], F32R)
        wd_sb = sb("wd_sb", [P, NI, C], F32R)
        sg_sb = sb("sg_sb", [P, NI])
        su_sb = sb("su_sb", [P, NI])
        sd_sb = sb("sd_sb", [P, C])
        bqkv_sb = sb("bqkv_sb", [P, 3 * C])
        bout_sb = sb("bout_sb", [P, C])
        x0 = sb("x0", [P, NT, C])
        x1 = sb("x1", [P, NT, C])
        x2 = sb("x2", [P, NT, C])
        x3 = sb("x3", [P, NT, C])
        xT = sb("xT", [P, 2, KC, T], F32R)
        gw_raw = sb("gw_raw", [P, KC, E])
        gw_s = sb("gw_s", [P, 2, KC, E], F32R)
        topw = sb("topw", [P, NT, 2])
        hot = sb("hot", [P, NT, 2, E])
        mv = sb("mv", [P, NT, 2])
        stats = sb("stats", [P, NT, 6])
        rstd = sb("rstd", [P, NT])
        q_st = sb("q_st", [P, H, STACK])
        k_st = sb("k_st", [P, H, STACK])
        v_aug = [sb(f"v_aug{l}", [P, NT, (KVH0, H)[l], 32]) for l in (0, 1)]
        attn_scope = ExitStack()
        scope.append(attn_scope)
        qkv_sb = sb("qkv_sb", [P, 2, 3 * C])
        rot_c = sb("rot_c", [P, 2 * C])
        rot_s = sb("rot_s", [P, 2, 2 * C])
        qT = sb("qT", [P, PAIRS, T], F32R)
        kT = sb("kT", [P, PAIRS, T], F32R)
        negmax = sb("negmax", [P, NT, H])
        shift_row = sb("shift_row", [GH, 2, T], F32R)
        prob = sb("prob", [P, 2, GH, PROB_COLS])
        oT = sb("oT", [P, T])
        rden = sb("rden", [P, NT, GH])
        o_sb = sb("o_sb", [P, NT, C])
        scope.pop()
        attn_scope.close()
        ffn_scope = ExitStack()
        scope.append(ffn_scope)
        gate_sb = sb("gate_sb", [P, 2, T])
        fuse_sb = sb("fuse_sb", [P, 2, T])
        fT = sb("fT", [P, 2, NI, T], F32R)
        scope.pop()
        ffn_scope.close()
        stage_scope = ExitStack()
        scope.append(stage_scope)
        w_raw = [sb(f"w_raw{i}", [P, KC, n]) for i, n in enumerate((NQKV[0], C, NQKV[1], C))]
        scope.pop()
        stage_scope.close()
        scope.pop()
        phase1.close()
        phase2 = ExitStack()
        scope.append(phase2)
        w13_sb = sb("w13_sb", [P, NE, KC, 2 * I], F32R)
        w2_sb = sb("w2_sb", [IH, NE, 2, C], F32R)
        x3_all = sb("x3_all", [P, TT, C])
        y_all = sb("y_all", [P, TT, C])
        chosen = sb("chosen", [P, TT, E], BF16)
        tile_tot = sb("tile_tot", [P, E, TT])
        tile_inc = sb("tile_inc", [P, E, TT])
        scan_keep = sb("scan_keep", [P, E, TT])
        n_int = sb("n_int", [P, E], I32)
        room = sb("room", [P, E])
        room_inc = sb("room_inc", [P, E])
        ones_e = sb("ones_e", [P, E])
        pos = sb("pos", [P, TT, E])
        pos_hot = sb("pos_hot", [P, TT, 2, E])
        slot_f = sb("slot_f", [P, TT, 2])
        slot = sb("slot", [P, TT, 2], U32)
        past = sb("past", [P, NS, E])
        owner_f = sb("owner_f", [P, NS])
        owner = sb("owner", [P, NS], I32)
        xg = sb("xg", [P, NT, C])
        xgT = sb("xgT", [P, 2, KC, T], F32R)
        xs_sb = sb("xs_sb", [P, 4, C])
        xsT = sb("xsT", [P, 2, 2, KC, P], F32R)
        act_a = sb("act_a", [P, 2, I])
        h_sb = sb("h_sb", [P, 2, I])
        hT = sb("hT", [IH, 2, 2, 2, P], F32R)
        ys_sb = sb("ys_sb", [P, 4, C])
        back = sb("back", [P, 4, 2, C])
        mv2 = sb("mv2", [P, TT, 2])
        stats2 = sb("stats2", [P, TT, 6])
        rstd2 = sb("rstd2", [P, TT])
        scope.pop()
        phase2.close()

        w_in = [signal(f"w_in{i}", 0) for i in range(4)]
        consts_in = signal("consts_in", 0)
        w_int8 = signal("w_int8", 0)
        made = signal("made", 0)
        w_hi = signal("w_hi", 0)
        w_lo = signal("w_lo", 0)
        start_dve = signal("start_dve", 0)
        x0_in = signal("x0_in", 16)
        SPLITS = ("x0", "o0", "x1", "x2", "o1", "x3")
        tr, hi, lo = (dict(zip(SPLITS, staged(n, *[NT] * len(SPLITS)))) for n in ("tr", "hi", "lo"))
        qkv, qkv_out, cosd, roped, st_hi, st_lo, v_put = (staged(n, k, k) for n, k in (
            ("qkv", NT), ("qkv_out", NT), ("cosd", NT), ("roped", NT), ("st_hi", 2 * NT), ("st_lo", 2 * NT), ("v_put", NT)))
        q_tr, k_tr, q_out, k_out = (staged(n, NT, NT) for n in ("q_tr", "k_tr", "q_out", "k_out"))
        raw_score, maxed = (staged(n, *[NG * len(MAX_ITEMS[l]) for l in (0, 1)]) for n in ("raw_score", "maxed"))
        sunk = signal("sunk", NG)
        sh_tr, sh_out = (staged(n, NG, NG) for n in ("sh_tr", "sh_out"))
        sh_row = [staged(f"sh_row{g}", GH * 16, GH * 16) for g in range(NG)]
        scored, exped = (staged(n, *[NG * GH * len(PARTS[l]) for l in (0, 1)]) for n in ("scored", "exped"))
        pv = staged("pv", *[NG * len(PARTS[l]) for l in (0, 1)])
        oT_out, o_tr, o_put, rden_done = (staged(n, NG, NG) for n in ("oT_out", "o_tr", "o_put", "rden"))
        proj = staged("proj", NT, NT)
        var_done, rstd_done = (staged(n, NT, NT, NT) for n in ("var", "rstd"))
        normed = [signal(f"normed{i}", NT, primed=int(i == 0)) for i in range(3)]
        gated, upped, silued, fused, f_hi, f_lo = (signal(s, NI) for s in ("gated", "upped", "silued", "fused", "f_hi", "f_lo"))
        down = signal("down", NT)
        biased = signal("biased", NT)
        x3_kept = signal("x3_kept", 16, 16)
        logits, exp_l, routed = signal("logits", 1), signal("exp_l", 1), signal("routed", 3)
        DVE_STEPS = 2 * NT + NG + 10 * NT + 2 * NT + 5
        dve_step = signal("dve_step", DVE_STEPS)
        x3_back = signal("x3_back", 0)
        zero_x = signal("zero_x", 0)
        shared_in = signal("shared_in", 0)
        w13_in, w2_in, gw_in = signal("w13_in", 0), signal("w2_in", 0), signal("gw_in", 0)
        gw_split = signal("gw_split", 0)
        counted, place = signal("counted", 0), signal("place", 0)
        slotted, owned = signal("slotted", 0), signal("owned", 0)
        scattered = signal("scattered", 0)
        U = SHARED * NT
        xg_in = signal("xg_in", 16)
        xg_tr, xg_hi, xg_lo = (signal(n, NT, int(n == "xg_tr")) for n in ("xg_tr", "xg_hi", "xg_lo"))
        sh_up, sh_silu, sh_h, sh_htr, sh_hhi, sh_hlo = (signal(n, U) for n in ("sh_up", "sh_silu", "sh_h", "sh_htr", "sh_hhi", "sh_hlo"))
        sh_down, sh_y = signal("sh_down", NT), signal("sh_y", NT)
        xs_in = [signal(f"xs_in{r}", 0) for r in range(4)]
        ys_kept = [signal(f"ys_kept{r}", 0) for r in range(4)]
        xs_tr, xs_hi, xs_lo, e_up, e_silu, e_h, e_htr, e_hhi, e_hlo, e_down, e_y = (
            signal(n, 0) for n in ("xs_tr", "xs_hi", "xs_lo", "e_up", "e_silu", "e_h", "e_htr", "e_hhi", "e_hlo", "e_down", "e_y"))
        back_in = [signal(f"back_in{r}", 0) for r in range(4)]
        y_step = signal("y_step", 0)
        y_var, y_rstd, y_norm, y_out = (signal(n, 0) for n in ("y_var", "y_rstd", "y_norm", "y_out"))

        block = ctx.enter_context(nc.Block())

        @block.sync
        def _(sp):
            raw = (wqkv0, wo0, wqkv1, wo1)
            for i in range(4):
                sp.dma_start(w_raw[i][:], raw[i].rearrange("(k p) n -> p k n", p=P)).then_inc(w_in[i].sem, 16)
            with sp.Fori(0, B) as b:
                sp.wait_ge(*normed[0].at(b, 0))
                sp.dma_start(x0[:], x.rearrange("b (t p) c -> b p t c", p=P)[b]).then_inc(x0_in.sem, 16)
                for l in (0, 1):
                    for g in range(NG):
                        sp.wait_ge(*sh_out[l].at(b, g + 1))
                        for j in range(GH):
                            r = STACK * (j % 2) + SHIFT
                            sp.dma_start(qT[r:r + 1, 2 * g + j // 2, :].bitcast(F32),
                                         shift_row[j:j + 1, g % 2, :].bitcast(F32)).then_inc(sh_row[g][l].sem, 16)
                sp.wait_ge(*normed[2].at(b, NT))
                sp.dma_start(x3_dram[b], x3[:]).then_inc(x3_kept.sem, 16)
            sp.wait_ge(*x3_kept.at(B, 0))
            sp.wait_ge(*dve_step.at(B, 0))
            sp.dma_start(x3_all[:].rearrange("p (b t) c -> p b t c", b=B), x3_dram.rearrange("b p t c -> p b t c")).then_inc(x3_back.sem, 16)
            with sp.Fori(0, B) as b:
                sp.wait_ge(*xg_tr.at(b, 0))
                sp.dma_start(xg[:], x3_dram[b]).then_inc(xg_in.sem, 16)

            def load(q, r):
                if not (isinstance(q, int) and q < 4):
                    sp.wait_ge(xs_tr.sem, q - 3)
                sp.dma_start(xs_sb[:, r, :], xs_dram.rearrange("(s p) c -> s p c", p=P)[q]).then_inc(xs_in[r].sem, 16)

            sp.wait_ge(scattered.sem, 16 * 2 * TT)
            for q in range(4):
                load(q, q)
            with sp.Fori(0, (NS - 4) // 4) as m:
                for r in range(4):
                    load(m * 4 + (4 + r), r)
            for q in range(4 + (NS - 4) // 4 * 4, NS):
                load(q, q % 4)
            for g in range(B):
                sp.wait_ge(y_norm.sem, (g + 1) * NT)
                sp.dma_start(out[g].rearrange("(t p) c -> p t c", p=P), y_all[:, g * NT:(g + 1) * NT, :]).then_inc(y_out.sem, 16)
            sp.wait_ge(y_out.sem, 16 * B)

        @block.gpsimd
        def _(pool):
            n_made = [0]

            def then(ins):
                n_made[0] += 1
                ins.then_inc(made.sem, 1)
                pool.wait_ge(made.sem, n_made[0])

            then(pool.memset(ident[:], 0.0))
            then(pool.affine_select(out=ident[:], in_=ident[:], compare_op=ALU.not_equal, fill=1.0, base=0,
                                    pattern=[[-1, P]], channel_multiplier=1))
            pool.dma_start(wg_sb[:], w_gate.bitcast(I8).rearrange("(k p) n -> p k n", p=P)).then_inc(w_int8.sem, 16)
            pool.dma_start(wu_sb[:], w_up.bitcast(I8).rearrange("(k p) n -> p k n", p=P)).then_inc(w_int8.sem, 16)
            pool.dma_start(wd_sb[:], w_down.bitcast(I8).rearrange("(k p) n -> p k n", p=P)).then_inc(w_int8.sem, 16)
            then(pool.memset(ident_b[:], 0.0))
            then(pool.affine_select(out=ident_b[:], in_=ident_b[:], compare_op=ALU.not_equal, fill=1.0, base=0,
                                    pattern=[[-1, P]], channel_multiplier=1))
            then(pool.memset(band[:], 0.0))
            then(pool.affine_select(out=band[:], in_=band[:], compare_op=ALU.is_ge, fill=MASKED, base=0,
                                    pattern=[[1, 256]], channel_multiplier=-1))
            then(pool.affine_select(out=band[:], in_=band[:], compare_op=ALU.is_ge, fill=MASKED, base=2 * HALF_WINDOW,
                                    pattern=[[-1, 256]], channel_multiplier=1))
            then(pool.memset(causal_q[:], 0.0))
            then(pool.affine_select(out=causal_q[:], in_=causal_q[:], compare_op=ALU.is_ge, fill=MASKED, base=0,
                                    pattern=[[-1, P]], channel_multiplier=1))
            then(pool.memset(causal_k[:], 0.0))
            then(pool.affine_select(out=causal_k[:], in_=causal_k[:], compare_op=ALU.is_ge, fill=MASKED, base=0,
                                    pattern=[[1, P]], channel_multiplier=-1))
            then(pool.memset(neg_half[:], -0.5))
            then(pool.memset(ones_b[:], 1.0))
            then(pool.memset(tri[:], 0.0))
            then(pool.affine_select(out=tri[:], in_=tri[:], compare_op=ALU.is_ge, fill=1.0, base=0,
                                    pattern=[[-1, P]], channel_multiplier=1))
            then(pool.iota(iota_s[:], pattern=[[P, NS]], base=0, channel_multiplier=0,
                           allow_small_or_imprecise_dtypes=True))
            then(pool.iota(iota_e[:], pattern=[[1, E]], base=0, channel_multiplier=0,
                           allow_small_or_imprecise_dtypes=True))
            pool.wait_ge(consts_in.sem, 7 * 16)
            then(pool.tensor_scalar(out=sink4[:], in0=sink4[:], scalar1=1.0 / SCALE, scalar2=None, op0=ALU.mult))
            pool.wait_ge(w_lo.sem, 4)
            then(pool.memset(q_st[:], 0.0))
            then(pool.memset(k_st[:], 0.0))
            then(pool.memset(k_st[:, :, SHIFT:SHIFT + 1], 1.0))
            for l in (0, 1):
                then(pool.memset(v_aug[l][:], 0.0))
                then(pool.memset(v_aug[l][:, :, :, HD:HD + 1], 1.0))
            assert n_made[0] == MADE

            with pool.Fori(0, B) as b:

                def rstd_of(i):
                    for t in range(NT):
                        pool.wait_ge(*var_done[i].at(b, t + 1))
                        pool.tensor_tensor(out=rstd[:, t:t + 1], in0=mv[:, t, 1:2], in1=neg_half[:],
                                           op=ALU.pow).then_inc(rstd_done[i].sem, 1)

                for l in (0, 1):
                    nh = QKH[l]
                    kvh = (KVH0, H)[l]
                    for t in range(NT):
                        pool.wait_ge(*qkv_out[l].at(b, t + 1))
                        if t >= 1:
                            pool.wait_ge(*roped[l].at(b, t))
                        cos = rot[:, t, 0, :].unsqueeze(1).to_broadcast([P, nh, HD])
                        pool.tensor_tensor(out=rot_c[:, 0:nh * HD].rearrange("p (h d) -> p h d", d=HD),
                                           in0=qkv_sb[:, t % 2, 0:nh * HD].rearrange("p (h d) -> p h d", d=HD),
                                           in1=cos, op=ALU.mult).then_inc(cosd[l].sem, 1)
                        pool.tensor_copy(v_aug[l][:, t, :, 0:HD],
                                         qkv_sb[:, t % 2, nh * HD:(nh + kvh) * HD].rearrange("p (h d) -> p h d", d=HD)
                                         ).then_inc(v_put[l].sem, 1)
                    if l == 1:
                        for t in range(NT):
                            pool.wait_ge(*lo["x2"].at(b, t + 1))
                            pool.tensor_tensor(out=x2[:, t, :], in0=x2[:, t, :], in1=bout_sb[:],
                                               op=ALU.add).then_inc(biased.sem, 1)
                    rstd_of((0, 2)[l])
                    if l == 0:
                        for m in range(NI):
                            pool.wait_ge(*f_hi.at(b, m + 1))
                            pool.tensor_tensor(out=fT[:, 1, m, :], in0=fuse_sb[:, m % 2, :],
                                               in1=fT[:, 0, m, :].bitcast(F32), op=ALU.subtract).then_inc(f_lo.sem, 1)
                        rstd_of(1)

            pool.wait_ge(*x3_kept.at(B, 0))
            pool.wait_ge(*dve_step.at(B, 0))
            pool.dma_start(w13_sb[:, E:NE, :, :], w13[:, E:NE, :, :]).then_inc(shared_in.sem, 16)
            pool.dma_start(w2_sb[:, E:NE, :, :], w2[:, E:NE, :, :]).then_inc(shared_in.sem, 16)
            for e in range(0, E, 4):
                pool.dma_start(w13_sb[:, e:e + 4, :, :], w13[:, e:e + 4, :, :]).then_inc(w13_in.sem, 16)
                pool.dma_start(w2_sb[:, e:e + 4, :, :], w2[:, e:e + 4, :, :]).then_inc(w2_in.sem, 16)
            pool.memset(scan_keep[:], 1.0).then_inc(place.sem, 1)
            pool.wait_ge(place.sem, 1)
            pool.memset(scan_keep[:, :, 0:1], 0.0).then_inc(place.sem, 1)
            pool.memset(ones_e[:], 1.0).then_inc(place.sem, 1)
            pool.wait_ge(zero_x.sem, 16)
            pool.wait_ge(slotted.sem, 1)
            pool.wait_ge(x3_back.sem, 16)
            for t in range(TT):
                for k in (0, 1):
                    pool.indirect_dma_start(out=xs_dram, out_offset=bass.IndirectOffsetOnAxis(ap=slot[:, t, k:k + 1], axis=0),
                                            in_=x3_all[:, t, :], in_offset=None).then_inc(scattered.sem, 16)

            def store(q, r):
                pool.wait_ge(e_y.sem, q + 1)
                pool.dma_start(ys_dram.rearrange("(s p) c -> s p c", p=P)[q], ys_sb[:, r, :]).then_inc(ys_kept[r].sem, 16)

            for q in range(3):
                store(q, q)
            with pool.Fori(0, (NS - 3) // 4) as m:
                for i in range(4):
                    store(m * 4 + (3 + i), (3 + i) % 4)
            for r in range(4):
                pool.wait_ge(ys_kept[r].sem, 16 * len(range(r, NS, 4)))
            for t in range(TT):
                if t >= 4:
                    pool.wait_ge(y_var.sem, t - 3)
                for k in (0, 1):
                    pool.indirect_dma_start(out=back[:, t % 4, k, :], out_offset=None, in_=ys_dram,
                                            in_offset=bass.IndirectOffsetOnAxis(ap=slot[:, t, k:k + 1], axis=0)
                                            ).then_inc(back_in[t % 4].sem, 16)
                if t >= 1:
                    pool.wait_ge(y_var.sem, t)
                    pool.tensor_tensor(out=rstd2[:, t - 1:t], in0=mv2[:, t - 1, 1:2], in1=neg_half[:], op=ALU.pow).then_inc(y_rstd.sem, 1)
            pool.wait_ge(y_var.sem, TT)
            pool.tensor_tensor(out=rstd2[:, TT - 1:TT], in0=mv2[:, TT - 1, 1:2], in1=neg_half[:], op=ALU.pow).then_inc(y_rstd.sem, 1)

        @block.scalar
        def _(act):
            act.dma_start(rot[:], rotary.rearrange("(t p) (a d) -> p t a d", p=P, a=2)).then_inc(consts_in.sem, 16)
            act.dma_start(sink4[:], sink.partition_broadcast(P)).then_inc(consts_in.sem, 16)
            act.dma_start(sg_sb[:], s_gate).then_inc(consts_in.sem, 16)
            act.dma_start(su_sb[:], s_up).then_inc(consts_in.sem, 16)
            act.dma_start(sd_sb[:], s_down.partition_broadcast(P)).then_inc(consts_in.sem, 16)
            act.dma_start(bqkv_sb[:], b_qkv.partition_broadcast(P)).then_inc(consts_in.sem, 16)
            act.dma_start(bout_sb[:], b_out.partition_broadcast(P)).then_inc(consts_in.sem, 16)
            act.dma_start(gw_raw[:], gate_w.rearrange("(k p) e -> p k e", p=P)).then_inc(gw_in.sem, 16)
            dst = (wqkv_s[0], wo_s[0], wqkv_s[1], wo_s[1])
            for i in range(4):
                act.wait_ge(w_in[i].sem, 16)
                act.activation(dst[i][:, 0, :, :], w_raw[i][:], ACT.Copy).then_inc(w_hi.sem, 1)

            act.wait_ge(gw_in.sem, 16)
            act.activation(gw_s[:, 0, :, :], gw_raw[:], ACT.Copy).then_inc(gw_split.sem, 1)
            act.wait_ge(start_dve.sem, 1)
            act.dma_start(xs_dram.rearrange("(s p) c -> p s c", p=P), zeros[:].unsqueeze(1).to_broadcast([P, NS, C])
                          ).then_inc(zero_x.sem, 16)

            with act.Fori(0, B) as b:

                def split_hi(n, t):
                    act.wait_ge(*tr[n].at(b, t + 1))
                    act.activation(xT[:, 0, :, t * P:(t + 1) * P],
                                   ps[:, 6 + t % 2, 0:C].rearrange("p (k q) -> p k q", k=KC),
                                   ACT.Copy).then_inc(hi[n].sem, 1)

                def attention(l):
                    n_parts = len(PARTS[l])
                    for t in range(NT):
                        split_hi(("x0", "x2")[l], t)
                    def q_copy(t):
                        act.wait_ge(*q_tr[l].at(b, t + 1))
                        act.activation(qT[:, :, t * P:(t + 1) * P], ps[:, 2:4, :].rearrange("p a (n q) -> p (a n) q", q=P),
                                       ACT.Copy).then_inc(q_out[l].sem, 1)

                    def qkv_copy(t):
                        act.wait_ge(*qkv[0].at(b, t + 1))
                        if t >= 2:
                            act.wait_ge(*roped[0].at(b, t - 1))
                            act.wait_ge(*v_put[0].at(b, t - 1))
                        act.activation(qkv_sb[:, t % 2, 0:NQKV[0]], ps[:, t % 2, 0:NQKV[0]],
                                       ACT.Copy).then_inc(qkv_out[0].sem, 1)

                    if l == 0:
                        qkv_copy(0)
                        qkv_copy(1)
                    for t in range(NT):
                        act.wait_ge(*roped[l].at(b, t + 1))
                        if t >= 1:
                            act.wait_ge(*q_tr[l].at(b, t))
                        q = rot_s[:, t % 2, 0:C].rearrange("p (h d) -> p h d", d=HD)
                        act.activation(q_st[:, :, 0:2 * HD].rearrange("p h (r d) -> p h r d", r=2).bitcast(F32R),
                                       q.unsqueeze(2).to_broadcast([P, H, 2, HD]), ACT.Copy).then_inc(st_hi[l].sem, 1)
                        if t >= 1:
                            act.wait_ge(*k_tr[l].at(b, t))
                        nk = QKH[l] - H
                        k = rot_s[:, t % 2, C:C + nk * HD].rearrange("p (h d) -> p h d", d=HD)
                        if l == 1:
                            kd = k_st[:, :, 0:4 * HD].rearrange("p h (r d) -> p h r d", r=2)[:, :, :, 0:HD]
                            act.activation(kd.bitcast(F32R), k.unsqueeze(2).to_broadcast([P, H, 2, HD]),
                                           ACT.Copy).then_inc(st_hi[l].sem, 1)
                        else:
                            kk = k_st[:, 0:2 * KVH0, :].rearrange("p (h r) s -> p h r s", r=2)
                            kb = k.unsqueeze(2).to_broadcast([P, KVH0, 2, HD])
                            act.activation(kk[:, :, :, 0:HD].bitcast(F32R), kb, ACT.Copy)
                            act.activation(kk[:, :, :, 2 * HD:3 * HD].bitcast(F32R), kb,
                                           ACT.Copy).then_inc(st_hi[l].sem, 1)
                        if l == 0 and t + 2 < NT:
                            qkv_copy(t + 2)
                        if t >= 1:
                            q_copy(t - 1)
                    q_copy(NT - 1)

                    def shift_out(g):
                        act.wait_ge(*sh_tr[l].at(b, g + 1))
                        if g >= 2:
                            act.wait_ge(*sh_row[g - 2][l].at(b, GH * 16))
                        act.activation(shift_row[:, g % 2, :], ps[0:GH, 7, :], ACT.Copy).then_inc(sh_out[l].sem, 1)

                    def oT_copy(g):
                        act.wait_ge(*pv[l].at(b, (g + 1) * n_parts))
                        if g >= 1:
                            act.wait_ge(*o_tr[l].at(b, g))
                        act.activation(oT[:], ps[:, 6, :], ACT.Copy).then_inc(oT_out[l].sem, 1)

                    for s in range(NG + 2):
                        if 1 <= s <= NG:
                            shift_out(s - 1)
                        g = s - 2
                        if g < 0:
                            continue
                        if g >= 2:
                            act.wait_ge(*pv[l].at(b, (g - 1) * n_parts))
                        col = 0
                        for p in range(n_parts):
                            n = PART_COLS[l][p]
                            for j in range(GH):
                                i = (g * n_parts + p) * GH + j
                                act.wait_ge(*scored[l].at(b, i + 1))
                                act.activation(prob[:, g % 2, j, col:col + n], ps[:, 3 + i % 3, 0:n], ACT.Exp,
                                               scale=SCALE).then_inc(exped[l].sem, 1)
                            col += n
                            if p == 0 and g >= 1:
                                oT_copy(g - 1)
                    oT_copy(NG - 1)
                    for t in range(NT):
                        split_hi(("o0", "o1")[l], t)

                attention(0)
                for t in range(NT):
                    split_hi("x1", t)
                for m in range(NI):
                    act.wait_ge(*gated.at(b, m + 1))
                    if m >= 2:
                        act.wait_ge(*fused.at(b, m - 1))
                    act.activation(gate_sb[:, m % 2, :], ps[:, m % 2, :], ACT.Silu,
                                   scale=sg_sb[:, m:m + 1]).then_inc(silued.sem, 1)
                    if m >= 1:
                        act.wait_ge(*fused.at(b, m))
                        act.activation(fT[:, 0, m - 1, :], fuse_sb[:, (m - 1) % 2, :], ACT.Copy).then_inc(f_hi.sem, 1)
                act.wait_ge(*fused.at(b, NI))
                act.activation(fT[:, 0, NI - 1, :], fuse_sb[:, (NI - 1) % 2, :], ACT.Copy).then_inc(f_hi.sem, 1)
                attention(1)
                for t in range(NT):
                    split_hi("x3", t)
                act.wait_ge(*logits.at(b, 1))
                act.activation(score[:], ps[:, 0, 0:NT * E].rearrange("p (t e) -> p t e", e=E), ACT.Exp,
                               scale=-1.0).then_inc(exp_l.sem, 1)

            with act.Fori(0, B) as b:
                for t in range(NT):
                    act.wait_ge(*xg_tr.at(b, t + 1))
                    act.activation(xgT[:, 0, :, t * P:(t + 1) * P],
                                   ps[:, 3 + t % 2, 0:C].rearrange("p (k q) -> p k q", k=KC),
                                   ACT.Copy).then_inc(xg_hi.sem, 1)
                for u in range(U + 1):
                    if u < U:
                        act.wait_ge(*sh_up.at(b, u + 1))
                        act.activation(act_a[:, u % 2, :], ps[:, u % 2, 0:I], ACT.Silu).then_inc(sh_silu.sem, 1)
                    if u >= 1:
                        act.wait_ge(*sh_htr.at(b, u))
                        act.activation(hT[:, (u - 1) % 2, 0, :, :],
                                       ps[0:IH, 3 + (u - 1) % 2, 0:2 * P].rearrange("p (k q) -> p k q", k=2),
                                       ACT.Copy).then_inc(sh_hhi.sem, 1)

            def scalar_step(q, r, on, before):
                if on(0):
                    act.wait_ge(xs_tr.sem, q + 1)
                    act.activation(xsT[:, r % 2, 0, :, :], ps[:, 3 + r % 2, 0:C].rearrange("p (k n) -> p k n", k=KC),
                                   ACT.Copy).then_inc(xs_hi.sem, 1)
                if on(1):
                    act.wait_ge(e_up.sem, q)
                    act.activation(act_a[:, (r - 1) % 2, :], ps[:, (r - 1) % 2, 0:I], ACT.Silu).then_inc(e_silu.sem, 1)
                if on(2):
                    act.wait_ge(e_htr.sem, q - 1)
                    act.activation(hT[:, (r - 2) % 2, 0, :, :], ps[0:IH, 5 + (r - 2) % 2, 0:2 * P].rearrange("p (k n) -> p k n", k=2),
                                   ACT.Copy).then_inc(e_hhi.sem, 1)

            run_steps(act, scalar_step)

        @block.vector
        def _(dve):
            dst = (wqkv_s[0], wo_s[0], wqkv_s[1], wo_s[1])
            dve.memset(zeros[:], 0.0).then_inc(start_dve.sem, 1)
            for i, sig in enumerate((normed[0], x3_kept, xg_tr)):
                dve.memset(carry[:, i + 1:i + 2], 0.0).then_inc(sig.sem, sig.primed)
            for i in range(4):
                dve.wait_ge(w_hi.sem, i + 1)
                dve.tensor_tensor(out=dst[i][:, 1, :, :], in0=w_raw[i][:], in1=dst[i][:, 0, :, :].bitcast(F32),
                                  op=ALU.subtract).then_inc(w_lo.sem, 1)
            dve.wait_ge(gw_split.sem, 1)
            dve.tensor_tensor(out=gw_s[:, 1, :, :], in0=gw_raw[:], in1=gw_s[:, 0, :, :].bitcast(F32),
                              op=ALU.subtract).then_inc(gw_split.sem, 1)
            dve.wait_ge(consts_in.sem, 7 * 16)
            dve.wait_ge(made.sem, MADE)

            with dve.Fori(0, B) as b:
                steps = [0]

                def then(ins, carrier=False):
                    steps[0] += 1
                    ins.then_inc(dve_step.sem, 1)
                    dve.wait_ge(*dve_step.at(b, steps[0]))
                    if carrier:
                        dve.memset(carry[:, 0:1], 0.0)

                def split_lo(n, t):
                    dve.wait_ge(*hi[n].at(b, t + 1))
                    dve.tensor_tensor(out=xT[:, 1, :, t * P:(t + 1) * P],
                                      in0=ps[:, 6 + t % 2, 0:C].rearrange("p (k q) -> p k q", k=KC),
                                      in1=xT[:, 0, :, t * P:(t + 1) * P].bitcast(F32),
                                      op=ALU.subtract).then_inc(lo[n].sem, 1)

                def norm(i, ready, bank0, scale, residual, result):
                    if i == 2:
                        dve.wait_ge(*x3_kept.at(b, 0))
                    for t in range(NT):
                        dve.wait_ge(*ready.at(b, t + 1))
                        y = ps[:, bank0 + t % 2, 0:C]
                        if scale is not None:
                            then(dve.tensor_tensor(out=result[:, t, :], in0=y, in1=scale, op=ALU.mult))
                            y = result[:, t, :]
                        if i == 2:
                            dve.wait_ge(*biased.at(b, t + 1))
                        then(dve.tensor_tensor(out=result[:, t, :], in0=y, in1=residual[:, t, :], op=ALU.add))
                        then(dve.bn_stats(out=stats[:, t, :], in_=result[:, t, :]), carrier=True)
                        then(dve.bn_aggr(out=mv[:, t, :], in_=stats[:, t, :]))
                        dve.tensor_scalar(out=mv[:, t, 1:2], in0=mv[:, t, 1:2], scalar1=EPS, scalar2=None,
                                          op0=ALU.add).then_inc(var_done[i].sem, 1)
                        if t >= 1:
                            scale_tile(i, t - 1, result)
                    scale_tile(i, NT - 1, result)

                def scale_tile(i, t, result):
                    dve.wait_ge(*rstd_done[i].at(b, t + 1))
                    dve.tensor_scalar(out=result[:, t, :], in0=result[:, t, :], scalar1=mv[:, t, 0:1],
                                      scalar2=rstd[:, t:t + 1], op0=ALU.subtract, op1=ALU.mult).then_inc(normed[i].sem, 1)

                def attention(l):
                    n_parts, n_items = len(PARTS[l]), len(MAX_ITEMS[l])
                    nh = QKH[l]
                    nk = nh - H
                    for t in range(NT):
                        split_lo(("x0", "x2")[l], t)

                    def bias_out(t):
                        dve.wait_ge(*qkv[1].at(b, t + 1))
                        if t >= 2:
                            dve.wait_ge(*v_put[1].at(b, t - 1))
                            dve.wait_ge(*roped[1].at(b, t - 1))
                        bank = (0, 4)[t % 2]
                        dve.tensor_tensor(out=qkv_sb[:, t % 2, :], in0=ps[:, bank:bank + 2, :].rearrange("p a n -> p (a n)")[:, 0:3 * C],
                                          in1=bqkv_sb[:], op=ALU.add).then_inc(qkv_out[1].sem, 1)

                    if l == 1:
                        bias_out(0)
                    for t in range(NT):
                        if l == 1 and t + 1 < NT:
                            bias_out(t + 1)
                        dve.wait_ge(*qkv_out[l].at(b, t + 1))
                        src = qkv_sb[:, t % 2, 0:nh * HD].rearrange("p (h i a) -> p h i a", i=HD // 2, a=2)
                        dst_ = rot_s[:, t % 2, 0:nh * HD].rearrange("p (h i a) -> p h i a", i=HD // 2, a=2)
                        sin = rot[:, t, 1, :].rearrange("p (i a) -> p i a", a=2)
                        if t >= 2:
                            dve.wait_ge(*st_hi[l].at(b, 2 * (t - 1)))
                            dve.wait_ge(*st_lo[l].at(b, 2 * (t - 1)))
                        for a in (0, 1):
                            ins = dve.tensor_tensor(out=dst_[:, :, :, a], in0=src[:, :, :, 1 - a],
                                                    in1=sin[:, :, a].unsqueeze(1).to_broadcast([P, nh, HD // 2]), op=ALU.mult)
                            if a:
                                then(ins)
                        dve.wait_ge(*cosd[l].at(b, t + 1))
                        dve.tensor_tensor(out=rot_s[:, t % 2, 0:nh * HD], in0=rot_s[:, t % 2, 0:nh * HD],
                                          in1=rot_c[:, 0:nh * HD], op=ALU.add).then_inc(roped[l].sem, 1)
                        dve.wait_ge(*st_hi[l].at(b, 2 * t + 1))
                        q = rot_s[:, t % 2, 0:C].rearrange("p (h d) -> p h d", d=HD)
                        dve.tensor_tensor(out=q_st[:, :, 2 * HD:3 * HD], in0=q, in1=q_st[:, :, 0:HD],
                                          op=ALU.subtract).then_inc(st_lo[l].sem, 1)
                        dve.wait_ge(*st_hi[l].at(b, 2 * t + 2))
                        k = rot_s[:, t % 2, C:C + nk * HD].rearrange("p (h d) -> p h d", d=HD)
                        if l == 1:
                            dve.tensor_tensor(out=k_st[:, :, HD:2 * HD], in0=k, in1=k_st[:, :, 0:HD],
                                              op=ALU.subtract).then_inc(st_lo[l].sem, 1)
                        else:
                            kk = k_st[:, 0:2 * KVH0, :].rearrange("p (h r) s -> p h r s", r=2)
                            dve.tensor_tensor(out=kk[:, :, :, HD:2 * HD], in0=k.unsqueeze(2).to_broadcast([P, KVH0, 2, HD]),
                                              in1=kk[:, :, :, 0:HD], op=ALU.subtract).then_inc(st_lo[l].sem, 1)
                        if t >= 1:
                            k_copy(l, t - 1)
                    k_copy(l, NT - 1)

                    def normalise(g):
                        dve.wait_ge(*o_tr[l].at(b, g + 1))
                        o4 = ps[:, 7, :].rearrange("p (t h d) -> p t h d", t=NT, d=32)
                        dve.reciprocal(rden[:], o4[:, :, :, HD]).then_inc(rden_done[l].sem, 1)
                        dve.wait_ge(*rden_done[l].at(b, g + 1))
                        dve.tensor_tensor(
                            out=o_sb[:, :, g * GH * HD:(g + 1) * GH * HD].rearrange("p t (h d) -> p t h d", d=HD),
                            in0=o4[:, :, :, 0:HD], in1=rden[:].unsqueeze(3).to_broadcast([P, NT, GH, HD]),
                            op=ALU.mult).then_inc(o_put[l].sem, 1)

                    for s in range(NG + 2):
                        if s < NG:
                            for i, (t, j) in enumerate(MAX_ITEMS[l]):
                                n = query_tile_keys(l, t)[1]
                                mh = MAX_HEADS[l][t]
                                k = s * n_items + i
                                dve.wait_ge(*raw_score[l].at(b, k + 1))
                                dve.tensor_reduce(out=negmax[:, t, s * GH + j:(s + 1) * GH:GH // mh],
                                                  in_=ps[:, k % 3, 0:mh * n].rearrange("p (h n) -> p h n", n=n),
                                                  axis=AX.X, op=ALU.max, negate=True).then_inc(maxed[l].sem, 1)
                            if l == 0:
                                dve.wait_ge(*maxed[0].at(b, (s + 1) * n_items))
                                nm = negmax[:, :, s * GH:(s + 1) * GH]
                                sk = sink4[:, s * GH:(s + 1) * GH].unsqueeze(1).to_broadcast([P, NT, GH])
                                then(dve.tensor_tensor(out=nm, in0=nm, in1=sk, op=ALU.subtract))
                                dve.tensor_tensor(out=nm, in0=nm, in1=sk, op=ALU.add).then_inc(sunk.sem, 1)
                        if s >= 3:
                            normalise(s - 3)
                    normalise(NG - 1)
                    for t in range(NT):
                        split_lo(("o0", "o1")[l], t)

                def k_copy(l, t):
                    n_blk = (KVH0, PAIRS)[l]
                    dve.wait_ge(*k_tr[l].at(b, t + 1))
                    dve.tensor_copy(kT[:, 0:n_blk, t * P:(t + 1) * P],
                                    ps[:, 6:8, :].rearrange("p a (n q) -> p (a n) q", q=P)[:, 0:n_blk, :]).then_inc(k_out[l].sem, 1)

                attention(0)
                norm(0, proj[0], 0, None, x0[:], x1)
                for t in range(NT):
                    split_lo("x1", t)
                for m in range(NI):
                    dve.wait_ge(*silued.at(b, m + 1))
                    dve.wait_ge(*upped.at(b, m + 1))
                    if m >= 2:
                        dve.wait_ge(*f_lo.at(b, m - 1))
                    dve.scalar_tensor_tensor(out=fuse_sb[:, m % 2, :], in0=ps[:, 2 + m % 2, :], scalar=su_sb[:, m:m + 1],
                                             in1=gate_sb[:, m % 2, :], op0=ALU.mult, op1=ALU.mult).then_inc(fused.sem, 1)
                norm(1, down, 4, sd_sb[:], x1, x2)
                attention(1)
                norm(2, proj[1], 0, None, x2, x3)
                for t in range(NT):
                    split_lo("x3", t)
                dve.wait_ge(*exp_l.at(b, 1))
                then(dve.tensor_scalar(out=score[:], in0=score[:], scalar1=1.0, scalar2=None, op0=ALU.add))
                then(dve.reciprocal(score[:], score[:]), carrier=True)
                for t in range(NT):
                    then(dve.max(out=top8[:, t, :], in_=score[:, t, :]), carrier=True)
                    then(dve.max_index(out=idx8[:, t, :], in_max=top8[:, t, :], in_values=score[:, t, :]), carrier=t < NT - 1)
                dve.tensor_tensor(out=tsum[:], in0=top8[:, :, 0], in1=top8[:, :, 1], op=ALU.add)
                then(dve.tensor_copy(idxf[:], idx8[:, :, 0:2]))
                then(dve.reciprocal(tsum[:], tsum[:]))
                for s in (0, 1):
                    dve.tensor_tensor(out=hot[:, :, s, :], in0=iota_e[:].unsqueeze(1).to_broadcast([P, NT, E]),
                                      in1=idxf[:, :, s:s + 1].to_broadcast([P, NT, E]), op=ALU.is_equal).then_inc(routed.sem, 1)
                dve.tensor_tensor(out=topw[:], in0=top8[:, :, 0:2], in1=tsum[:].unsqueeze(2).to_broadcast([P, NT, 2]),
                                  op=ALU.mult).then_inc(routed.sem, 1)
                dve.wait_ge(*routed.at(b, 3))
                dve.tensor_copy(hot_all[:, bass.ds(b * NT, NT), :, :], hot[:])
                then(dve.tensor_copy(topw_all[:, bass.ds(b * NT, NT), :], topw[:]))
                assert steps[0] == DVE_STEPS, steps[0]

            n_place = [3]

            def after(ins):
                n_place[0] += 1
                ins.then_inc(place.sem, 1)
                dve.wait_ge(place.sem, n_place[0])

            dve.tensor_tensor(out=chosen[:], in0=hot_all[:, :, 0, :], in1=hot_all[:, :, 1, :], op=ALU.add).then_inc(counted.sem, 1)
            dve.wait_ge(counted.sem, 2)
            dve.wait_ge(place.sem, 3)
            after(dve.tensor_copy(tile_tot[:].rearrange("p e t -> p t e"), ps[:, 1, 0:TT * E].rearrange("p (t e) -> p t e", e=E)))
            after(dve.tensor_tensor_scan(out=tile_inc[:].rearrange("p e t -> p (e t)"), data0=scan_keep[:].rearrange("p e t -> p (e t)"),
                                         data1=tile_tot[:].rearrange("p e t -> p (e t)"), initial=0.0, op0=ALU.mult, op1=ALU.add))
            after(dve.tensor_scalar(out=n_int[:], in0=tile_inc[:, :, TT - 1], scalar1=float(P - 1), scalar2=None, op0=ALU.add))
            after(dve.tensor_scalar(out=n_int[:], in0=n_int[:], scalar1=7, scalar2=None, op0=ALU.logical_shift_right))
            after(dve.tensor_scalar(out=room[:], in0=n_int[:], scalar1=float(P), scalar2=None, op0=ALU.mult))
            after(dve.tensor_tensor_scan(out=room_inc[:], data0=ones_e[:], data1=room[:], initial=0.0, op0=ALU.mult, op1=ALU.add))
            after(dve.tensor_tensor(out=room[:], in0=room_inc[:], in1=room[:], op=ALU.subtract))
            after(dve.tensor_tensor(out=tile_inc[:], in0=tile_inc[:], in1=tile_tot[:], op=ALU.subtract))
            after(dve.tensor_tensor(out=tile_inc[:], in0=tile_inc[:], in1=room[:].unsqueeze(2).to_broadcast([P, E, TT]), op=ALU.add))
            after(dve.tensor_tensor(out=pos[:], in0=ps[:, 0, 0:TT * E].rearrange("p (t e) -> p t e", e=E),
                                    in1=tile_inc[:].rearrange("p e t -> p t e"), op=ALU.add))
            for s in (0, 1):
                ins = dve.tensor_tensor(out=pos_hot[:, :, s, :], in0=pos[:], in1=hot_all[:, :, s, :], op=ALU.mult)
                if s:
                    after(ins)
            after(dve.tensor_reduce(out=slot_f[:], in_=pos_hot[:], axis=AX.X, op=ALU.add))
            dve.tensor_copy(slot[:], slot_f[:]).then_inc(slotted.sem, 1)
            after(dve.tensor_tensor(out=past[:], in0=iota_s[:].unsqueeze(2).to_broadcast([P, NS, E]),
                                    in1=room_inc[:].unsqueeze(1).to_broadcast([P, NS, E]), op=ALU.is_ge))
            after(dve.tensor_reduce(out=owner_f[:], in_=past[:], axis=AX.X, op=ALU.add))
            dve.tensor_scalar(out=owner[:], in0=owner_f[:], scalar1=float(E - 1), scalar2=None, op0=ALU.min).then_inc(owned.sem, 1)

            dve.wait_ge(x3_back.sem, 16)
            with dve.Fori(0, B) as b:
                for t in range(NT):
                    dve.wait_ge(*xg_hi.at(b, t + 1))
                    dve.tensor_tensor(out=xgT[:, 1, :, t * P:(t + 1) * P],
                                      in0=ps[:, 3 + t % 2, 0:C].rearrange("p (k q) -> p k q", k=KC),
                                      in1=xgT[:, 0, :, t * P:(t + 1) * P].bitcast(F32),
                                      op=ALU.subtract).then_inc(xg_lo.sem, 1)
                for u in range(U + 2):
                    if u < U:
                        dve.wait_ge(*sh_silu.at(b, u + 1))
                        dve.tensor_tensor(out=h_sb[:, u % 2, :], in0=ps[:, u % 2, I:2 * I], in1=act_a[:, u % 2, :],
                                          op=ALU.mult).then_inc(sh_h.sem, 1)
                    if 1 <= u <= U:
                        dve.wait_ge(*sh_hhi.at(b, u))
                        dve.tensor_tensor(out=hT[:, (u - 1) % 2, 1, :, :],
                                          in0=ps[0:IH, 3 + (u - 1) % 2, 0:2 * P].rearrange("p (k q) -> p k q", k=2),
                                          in1=hT[:, (u - 1) % 2, 0, :, :].bitcast(F32), op=ALU.subtract).then_inc(sh_hlo.sem, 1)
                    if u >= 3 and u % 2 == 1:
                        t = (u - 3) // 2
                        dve.wait_ge(*sh_down.at(b, t + 1))
                        dve.tensor_tensor(out=y_all[:, bass.ds(b * NT + t, 1), :], in0=ps[:, 5 + t % 2, 0:C].unsqueeze(1),
                                          in1=x3_all[:, bass.ds(b * NT + t, 1), :], op=ALU.add).then_inc(sh_y.sem, 1)

            def vector_step(q, r, on, before):
                if on(0):
                    dve.wait_ge(xs_hi.sem, q + 1)
                    dve.tensor_tensor(out=xsT[:, r % 2, 1, :, :], in0=ps[:, 3 + r % 2, 0:C].rearrange("p (k n) -> p k n", k=KC),
                                      in1=xsT[:, r % 2, 0, :, :].bitcast(F32), op=ALU.subtract).then_inc(xs_lo.sem, 1)
                if on(1):
                    dve.wait_ge(e_silu.sem, q)
                    dve.tensor_tensor(out=h_sb[:, (r - 1) % 2, :], in0=ps[:, (r - 1) % 2, I:2 * I], in1=act_a[:, (r - 1) % 2, :],
                                      op=ALU.mult).then_inc(e_h.sem, 1)
                if on(2):
                    dve.wait_ge(e_hhi.sem, q - 1)
                    dve.tensor_tensor(out=hT[:, (r - 2) % 2, 1, :, :], in0=ps[0:IH, 5 + (r - 2) % 2, 0:2 * P].rearrange("p (k n) -> p k n", k=2),
                                      in1=hT[:, (r - 2) % 2, 0, :, :].bitcast(F32), op=ALU.subtract).then_inc(e_hlo.sem, 1)
                if on(3):
                    dve.wait_ge(e_down.sem, q - 2)
                    if not (isinstance(q, int) and q - 3 < 4):
                        dve.wait_ge(ys_kept[(r - 3) % 4].sem, before(3) * 16)
                    dve.tensor_copy(ys_sb[:, (r - 3) % 4, :], ps[:, (2, 7)[(r - 3) % 2], 0:C]).then_inc(e_y.sem, 1)

            run_steps(dve, vector_step)

            n_y = [0]

            def y_then(ins):
                n_y[0] += 1
                ins.then_inc(y_step.sem, 1)
                dve.wait_ge(y_step.sem, n_y[0])

            def finish(t):
                dve.wait_ge(y_rstd.sem, t + 1)
                dve.tensor_scalar(out=y_all[:, t, :], in0=y_all[:, t, :], scalar1=mv2[:, t, 0:1], scalar2=rstd2[:, t:t + 1],
                                  op0=ALU.subtract, op1=ALU.mult).then_inc(y_norm.sem, 1)

            for t in range(TT):
                dve.wait_ge(back_in[t % 4].sem, 32 * (t // 4 + 1))
                for k in (0, 1):
                    y_then(dve.scalar_tensor_tensor(out=y_all[:, t, :], in0=back[:, t % 4, k, :], scalar=topw_all[:, t, k:k + 1],
                                                    in1=y_all[:, t, :], op0=ALU.mult, op1=ALU.add))
                y_then(dve.bn_stats(out=stats2[:, t, :], in_=y_all[:, t, :]))
                y_then(dve.bn_aggr(out=mv2[:, t, :], in_=stats2[:, t, :]))
                dve.tensor_scalar(out=mv2[:, t, 1:2], in0=mv2[:, t, 1:2], scalar1=EPS, scalar2=None,
                                  op0=ALU.add).then_inc(y_var.sem, 1)
                if t >= 1:
                    finish(t - 1)
            finish(TT - 1)

        @block.tensor
        def _(pe):
            pe.wait_ge(made.sem, MADE)
            pe.wait_ge(w_lo.sem, 4)
            pe.wait_ge(gw_split.sem, 2)
            EXACT = ((0, 0), (0, 1), (1, 0))
            with pe.Fori(0, B) as b:

                def split_tr(n, src, ready, t):
                    pe.wait_ge(*ready)
                    if t >= 2:
                        pe.wait_ge(*lo[n].at(b, t - 1))
                    for k in range(KC):
                        ins = pe.transpose(ps[:, 6 + t % 2, k * P:(k + 1) * P], src[:, t, k * P:(k + 1) * P], ident[:])
                    ins.then_inc(tr[n].sem, 1)

                def product(dst, t, w, c0, n):
                    for i, (a, w_part) in enumerate(EXACT):
                        for k in range(KC):
                            ins = pe.matmul(dst, xT[:, a, k, t * P:(t + 1) * P], w[:, w_part, k, c0:c0 + n],
                                            start=(i + k == 0), stop=(i == 2 and k == KC - 1))
                    return ins

                def attention(l, src):
                    name = ("x0", "x2")[l]
                    n_parts, n_items = len(PARTS[l]), len(MAX_ITEMS[l])
                    for t in range(NT):
                        split_tr(name, src, x0_in.at(b, 16) if l == 0 else normed[1].at(b, t + 1), t)
                    for t in range(NT):
                        pe.wait_ge(*lo[name].at(b, t + 1))
                        if t >= 2:
                            pe.wait_ge(*qkv_out[l].at(b, t - 1))
                        if l == 0:
                            product(ps[:, t % 2, 0:NQKV[0]], t, wqkv_s[0], 0, NQKV[0]).then_inc(qkv[0].sem, 1)
                        else:
                            bank = (0, 4)[t % 2]
                            product(ps[:, bank, :], t, wqkv_s[1], 0, 512)
                            product(ps[:, bank + 1, 0:256], t, wqkv_s[1], 512, 256).then_inc(qkv[1].sem, 1)
                    n_blk = (KVH0, PAIRS)[l]
                    for t in range(NT):
                        pe.wait_ge(*st_lo[l].at(b, 2 * t + 1))
                        if t >= 1:
                            pe.wait_ge(*q_out[l].at(b, t))
                        for n in range(PAIRS):
                            ins = pe.transpose(ps[:, 2 + n // 4, (n % 4) * P:(n % 4 + 1) * P],
                                               q_st[:, 2 * n:2 * n + 2, :].rearrange("p h s -> p (h s)"), ident[:])
                        ins.then_inc(q_tr[l].sem, 1)
                        pe.wait_ge(*st_lo[l].at(b, 2 * t + 2))
                        if t >= 1:
                            pe.wait_ge(*k_out[l].at(b, t))
                        for n in range(n_blk):
                            ins = pe.transpose(ps[:, 6 + n // 4, (n % 4) * P:(n % 4 + 1) * P],
                                               k_st[:, 2 * n:2 * n + 2, :].rearrange("p h s -> p (h s)"), ident[:])
                        ins.then_inc(k_tr[l].sem, 1)

                    def raw_item(g, i):
                        t, j = MAX_ITEMS[l][i]
                        k0, n = query_tile_keys(l, t)
                        item = g * n_items + i
                        if item >= 3:
                            pe.wait_ge(*maxed[l].at(b, item - 2))
                        bank = item % 3
                        for jj in range(MAX_HEADS[l][t]):
                            h = g * GH + j + jj * (GH // MAX_HEADS[l][t])
                            p0 = STACK * (h % 2)
                            dst = ps[:, bank, jj * n:(jj + 1) * n]
                            if l == 0:
                                m0 = k0 - (t * P - HALF_WINDOW)
                                pe.matmul(dst, ident_b[:], band[:, m0:m0 + n], start=True, stop=False, skip_group_check=True)
                            else:
                                pe.matmul(ps[:, bank, (jj + 1) * n - P:(jj + 1) * n], ident_b[:], causal_q[:],
                                          start=True, stop=False, skip_group_check=True)
                            ins = pe.matmul(dst, qT[p0:p0 + SHIFT, h // 2, t * P:(t + 1) * P],
                                            kT[p0:p0 + SHIFT, h // 4 if l == 0 else h // 2, k0:k0 + n],
                                            start=False, stop=True, skip_group_check=True)
                        ins.then_inc(raw_score[l].sem, 1)

                    def score_item(g, i):
                        p, j = i // GH, i % GH
                        h = g * GH + j
                        item = g * n_parts * GH + i
                        if item >= 3:
                            pe.wait_ge(*exped[l].at(b, item - 2))
                        p0 = STACK * (h % 2)
                        for kt, col in PARTS[l][p]:
                            q0, n = key_tile_queries(l, kt)
                            dst = ps[:, 3 + item % 3, col:col + n]
                            if l == 0:
                                m0 = q0 - (kt * P - HALF_WINDOW)
                                pe.matmul(dst, ident_b[:], band[:, m0:m0 + n], start=True, stop=False, skip_group_check=True)
                            else:
                                pe.matmul(ps[:, 3 + item % 3, col:col + P], ident_b[:], causal_k[:],
                                          start=True, stop=False, skip_group_check=True)
                            ins = pe.matmul(dst, kT[p0:p0 + SHIFT + 1, h // 4 if l == 0 else h // 2, kt * P:(kt + 1) * P],
                                            qT[p0:p0 + SHIFT + 1, h // 2, q0:q0 + n], start=False, stop=True,
                                            skip_group_check=True)
                        ins.then_inc(scored[l].sem, 1)

                    def pv_part(g, p):
                        pe.wait_ge(*exped[l].at(b, (g * n_parts + p + 1) * GH))
                        if p == 0 and g >= 1:
                            pe.wait_ge(*oT_out[l].at(b, g))
                        off = sum(PART_COLS[l][:p])
                        for i, (kt, _) in enumerate(PARTS[l][p]):
                            q0, n = key_tile_queries(l, kt)
                            for j in range(GH):
                                h = g * GH + j
                                ins = pe.matmul(ps[32 * j:32 * j + 32, 6, q0:q0 + n],
                                                v_aug[l][:, kt, h // 4 if l == 0 else h, :],
                                                prob[:, g % 2, j, off:off + n], start=(p == 0 and i == 0),
                                                stop=(p == n_parts - 1 and i == len(PARTS[l][p]) - 1), skip_group_check=True)
                            off += n
                        ins.then_inc(pv[l].sem, 1)

                    def o_transposes(g):
                        pe.wait_ge(*oT_out[l].at(b, g + 1))
                        if g >= 1:
                            pe.wait_ge(*o_put[l].at(b, g))
                        for t in range(NT):
                            ins = pe.transpose(ps[:, 7, t * P:(t + 1) * P], oT[:, t * P:(t + 1) * P], ident[:])
                        ins.then_inc(o_tr[l].sem, 1)

                    pe.wait_ge(*q_out[l].at(b, NT))
                    pe.wait_ge(*k_out[l].at(b, NT))
                    pe.wait_ge(*v_put[l].at(b, NT))
                    for s in range(NG + 2):
                        g = s - 2
                        if 1 <= s <= NG:
                            if l == 0:
                                pe.wait_ge(*sunk.at(b, s))
                            else:
                                pe.wait_ge(*maxed[1].at(b, s * n_items))
                            if s >= 2:
                                pe.wait_ge(*sh_out[l].at(b, s - 1))
                            if s >= 4:
                                pe.wait_ge(*o_put[l].at(b, s - 3))
                            for t in range(NT):
                                ins = pe.transpose(ps[0:GH, 7, t * P:(t + 1) * P], negmax[:, t, (s - 1) * GH:s * GH], ident[:])
                            ins.then_inc(sh_tr[l].sem, 1)
                        if g >= 0:
                            pe.wait_ge(*sh_row[g][l].at(b, GH * 16))
                        for i in range(max(n_items, n_parts * GH)):
                            if g >= 0 and i < n_parts * GH:
                                score_item(g, i)
                            if s < NG and i < n_items:
                                raw_item(s, i)
                            if g >= 1 and i == 1:
                                pv_part(g - 1, n_parts - 1)
                            if g >= 1 and i == GH + 2:
                                if s <= NG:
                                    pe.wait_ge(*sh_out[l].at(b, s))
                                o_transposes(g - 1)
                            if g >= 0 and i % GH == 2 and 1 <= i // GH < n_parts:
                                pv_part(g, i // GH - 1)
                    pv_part(NG - 1, n_parts - 1)
                    o_transposes(NG - 1)
                    name = ("o0", "o1")[l]
                    for t in range(NT):
                        split_tr(name, o_sb, o_put[l].at(b, NG), t)
                    for t in range(NT):
                        pe.wait_ge(*lo[name].at(b, t + 1))
                        if t >= 2:
                            pe.wait_ge(*normed[2 * l].at(b, t - 1))
                        product(ps[:, t % 2, 0:C], t, wo_s[l], 0, C).then_inc(proj[l].sem, 1)

                attention(0, x0[:])
                for t in range(NT):
                    split_tr("x1", x1, normed[0].at(b, t + 1), t)
                pe.wait_ge(w_int8.sem, 48)
                pe.wait_ge(*lo["x1"].at(b, NT))
                for m in range(NI):
                    for w, bank0, sig, free in ((wg_sb, 0, gated, silued), (wu_sb, 2, upped, fused)):
                        if m >= 2:
                            pe.wait_ge(*free.at(b, m - 1))
                        for part in (0, 1):
                            for k in range(KC):
                                ins = pe.matmul(ps[:, bank0 + m % 2, :], w[:, k, m * P:(m + 1) * P], xT[:, part, k, :],
                                                start=(part + k == 0), stop=(part == 1 and k == KC - 1))
                        ins.then_inc(sig.sem, 1)
                for t in range(NT):
                    if t >= 2:
                        pe.wait_ge(*normed[1].at(b, t - 1))
                    for m in range(NI):
                        if t == 0:
                            pe.wait_ge(*f_lo.at(b, m + 1))
                        for part in (0, 1):
                            ins = pe.matmul(ps[:, 4 + t % 2, 0:C], fT[:, part, m, t * P:(t + 1) * P], wd_sb[:, m, :],
                                            start=(m + part == 0), stop=(m == NI - 1 and part == 1))
                    ins.then_inc(down.sem, 1)
                attention(1, x2)
                for t in range(NT):
                    split_tr("x3", x3, normed[2].at(b, t + 1), t)
                pe.wait_ge(*lo["x3"].at(b, NT))
                for t in range(NT):
                    for i, (a, w_part) in enumerate(EXACT):
                        for k in range(KC):
                            ins = pe.matmul(ps[:, 0, t * E:(t + 1) * E], xT[:, a, k, t * P:(t + 1) * P], gw_s[:, w_part, k, :],
                                            start=(i + k == 0), stop=(i == 2 and k == KC - 1))
                ins.then_inc(logits.sem, 1)

            pe.wait_ge(counted.sem, 1)
            all_chosen = chosen[:].rearrange("p t e -> p (t e)")
            pe.matmul(ps[:, 0, 0:TT * E], tri[:], all_chosen, start=True, stop=True)
            pe.matmul(ps[:, 1, 0:TT * E], ones_b[:], all_chosen, start=True, stop=True).then_inc(counted.sem, 1)
            pe.wait_ge(shared_in.sem, 32)
            pe.wait_ge(slotted.sem, 1)
            with pe.Fori(0, B) as b:
                pe.wait_ge(*xg_in.at(b, 16))
                for t in range(NT):
                    if t >= 2:
                        pe.wait_ge(*xg_lo.at(b, t - 1))
                    for k in range(KC):
                        ins = pe.transpose(ps[:, 3 + t % 2, k * P:(k + 1) * P], xg[:, t, k * P:(k + 1) * P], ident[:])
                    ins.then_inc(xg_tr.sem, 1)
                pe.wait_ge(*xg_lo.at(b, NT))

                def sh_upward(u):
                    if u >= 2:
                        pe.wait_ge(*sh_h.at(b, u - 1))
                    for part in (0, 1):
                        for k in range(KC):
                            ins = pe.matmul(ps[:, u % 2, 0:2 * I], xgT[:, part, k, (u // 2) * P:(u // 2 + 1) * P],
                                            w13_sb[:, E + u % 2, k, :], start=(part + k == 0), stop=(part == 1 and k == KC - 1))
                    ins.then_inc(sh_up.sem, 1)

                def sh_transpose(u):
                    pe.wait_ge(*sh_h.at(b, u + 1))
                    if u >= 2:
                        pe.wait_ge(*sh_hlo.at(b, u - 1))
                    for k in (0, 1):
                        ins = pe.transpose(ps[0:IH, 3 + u % 2, k * P:(k + 1) * P], h_sb[:, u % 2, k * IH:(k + 1) * IH], ident[:])
                    ins.then_inc(sh_htr.sem, 1)

                def sh_downward(u):
                    pe.wait_ge(*sh_hlo.at(b, u + 1))
                    t = u // 2
                    if t >= 2 and u % 2 == 0:
                        pe.wait_ge(*sh_y.at(b, t - 1))
                    for part in (0, 1):
                        for k in (0, 1):
                            ins = pe.matmul(ps[:, 5 + t % 2, 0:C], hT[:, u % 2, part, k, :], w2_sb[:, E + u % 2, k, :],
                                            start=(u % 2 + part + k == 0), stop=(u % 2 + part + k == 3))
                    if u % 2:
                        ins.then_inc(sh_down.sem, 1)

                for u in range(U + 2):
                    if u < U:
                        sh_upward(u)
                    if 1 <= u <= U:
                        sh_transpose(u - 1)
                    if u >= 2:
                        sh_downward(u - 2)

            def tensor_step(q, r, on, before):
                first = isinstance(q, int)
                if on(0):
                    pe.wait_ge(xs_in[r].sem, (before(0) + 1) * 16)
                    if not (first and q < 2):
                        pe.wait_ge(xs_lo.sem, q - 1)
                    for k in range(KC):
                        ins = pe.transpose(ps[:, 3 + r % 2, k * P:(k + 1) * P], xs_sb[:, r, k * P:(k + 1) * P], ident[:])
                    ins.then_inc(xs_tr.sem, 1)
                if on(1):
                    e = pe.value_load(owner[0:1, q - 1:q] if first else owner[0:1, bass.ds(q - 1, 1)], min_val=0, max_val=E - 1)
                    pe.wait_ge(xs_lo.sem, q)
                    if not (first and q < 3):
                        pe.wait_ge(e_h.sem, q - 2)
                    for part in (0, 1):
                        for k in range(KC):
                            ins = pe.matmul(ps[:, (r - 1) % 2, 0:2 * I], xsT[:, (r - 1) % 2, part, k, :], w13_sb[:, bass.ds(e, 1), k, :],
                                            start=(part + k == 0), stop=(part == 1 and k == KC - 1))
                    ins.then_inc(e_up.sem, 1)
                if on(2):
                    pe.wait_ge(e_h.sem, q - 1)
                    if not (first and q < 4):
                        pe.wait_ge(e_hlo.sem, q - 3)
                    for k in (0, 1):
                        ins = pe.transpose(ps[0:IH, 5 + (r - 2) % 2, k * P:(k + 1) * P], h_sb[:, (r - 2) % 2, k * IH:(k + 1) * IH], ident[:])
                    ins.then_inc(e_htr.sem, 1)
                if on(3):
                    e = pe.value_load(owner[0:1, q - 3:q - 2] if first else owner[0:1, bass.ds(q - 3, 1)], min_val=0, max_val=E - 1)
                    pe.wait_ge(e_hlo.sem, q - 2)
                    if not (first and q < 5):
                        pe.wait_ge(e_y.sem, q - 4)
                    for part in (0, 1):
                        for k in (0, 1):
                            ins = pe.matmul(ps[:, (2, 7)[(r - 3) % 2], 0:C], hT[:, (r - 3) % 2, part, k, :], w2_sb[:, bass.ds(e, 1), k, :],
                                            start=(part + k == 0), stop=(part + k == 2))
                    ins.then_inc(e_down.sem, 1)

            pe.wait_ge(owned.sem, 1)
            pe.wait_ge(w13_in.sem, 16 * E // 4)
            pe.wait_ge(w2_in.sem, 16 * E // 4)
            pe.wait_ge(*sh_y.at(B, 0))
            run_steps(pe, tensor_step)


MADE = 25
_INPUTS = ("x", "wqkv0", "wo0", "sink", "w_gate", "w_up", "w_down", "s_gate", "s_up", "s_down",
           "wqkv1", "b_qkv", "wo1", "b_out", "gate_w", "w13", "w2", "rotary")


def lay_out(inputs):
    g = {n: np.asarray(v) for n, v in inputs.items()}
    a = {
        "x": g["L0_attn_x"],
        "wqkv0": np.concatenate([g["L0_attn_wq"], g["L0_attn_wk"], g["L0_attn_wv"]], 1),
        "wo0": g["L0_attn_wo"], "sink": g["L0_attn_sink"].reshape(H),
        "w_gate": np.ascontiguousarray(g["L0_ffn_w_gate"]).view(np.int32), "w_up": np.ascontiguousarray(g["L0_ffn_w_up"]).view(np.int32), "w_down": np.ascontiguousarray(g["L0_ffn_w_down"]).view(np.int32),
        "s_gate": g["L0_ffn_s_gate"].reshape(NI, P).T, "s_up": g["L0_ffn_s_up"].reshape(NI, P).T, "s_down": g["L0_ffn_s_down"],
        "wqkv1": g["L1_attn_w_qkv"].T, "b_qkv": g["L1_attn_b_qkv"],
        "wo1": g["L1_attn_w_out"].T, "b_out": g["L1_attn_b_out"], "gate_w": g["L1_ffn_gate_w"].T,
        "rotary": rotary_tables(),
    }
    w1 = np.concatenate([g["L1_ffn_w1"], g["L1_ffn_sw1"].reshape(SHARED, I, C)])
    w3 = np.concatenate([g["L1_ffn_w3"], g["L1_ffn_sw3"].reshape(SHARED, I, C)])
    w2 = np.concatenate([g["L1_ffn_w2"], g["L1_ffn_sw2"].reshape(C, SHARED, I).transpose(1, 0, 2)])
    a["w13"] = np.concatenate([w1, w3], 1).reshape(NE, 2 * I, KC, P).transpose(3, 0, 2, 1)
    a["w2"] = w2.reshape(NE, C, 2, IH).transpose(3, 0, 2, 1)
    return {n: np.ascontiguousarray(v) for n, v in a.items()}


def kernel(**inputs):
    import concourse.bacc as bacc
    from concourse.bass_utils import run_bass_kernel_spmd

    arrays = lay_out(inputs)
    nc = bacc.Bacc("TRN2", target_bir_lowering=False, num_devices=1)
    args = [nc.dram_tensor(f"in_{n}", arrays[n].shape, mybir.dt.from_np(arrays[n].dtype), kind="ExternalInput").ap()
            for n in _INPUTS]
    out = nc.dram_tensor("out", (B, T, C), F32, kind="ExternalOutput").ap()
    build(nc, *args, out)
    r = run_bass_kernel_spmd(nc, [{f"in_{n}": arrays[n] for n in _INPUTS}], core_ids=[0])
    return r.results[0]["out"]
```

```python
import numpy as np
import concourse.bass as bass
from concourse import mybir
from contextlib import ExitStack

F32, F32R, BF16 = mybir.dt.float32, mybir.dt.float32r, mybir.dt.bfloat16
I8, I32, U32 = mybir.dt.int8, mybir.dt.int32, mybir.dt.uint32
ALU = mybir.AluOpType
ACT = mybir.ActivationFunctionType
AX = mybir.AxisListType

P = 128
B, T, C = 4, 512, 256
NT, KC = T // P, C // P
H, HD = 16, 16
KVH0 = 4
HALF_WINDOW = 64
NG, GH = 4, 4
NQKV = (C + 2 * KVH0 * HD, 3 * C)
QKH = (H + KVH0, 2 * H)
INTER = 1024
NI = INTER // P
E, I = 16, 176
SHARED = 2
NE = E + SHARED
IH = I // 2
TOK = B * T
TT = B * NT
NS = (2 * TOK + E * (P - 1)) // P
EPS = 1e-5
SCALE = HD ** -0.5
MASKED = -1e30

STACK = 64
SHIFT = 3 * HD
PAIRS = H // 2


def key_tile_queries(layer, kt):
    if layer == 1:
        return kt * P, T - kt * P
    lo, hi = max(0, kt * P - HALF_WINDOW), min(T, (kt + 1) * P + HALF_WINDOW)
    return lo, hi - lo


def query_tile_keys(layer, t):
    if layer == 1:
        return 0, (t + 1) * P
    return key_tile_queries(0, t)


def unseen(layer, kt):
    if layer == 1:
        return [(kt * P, (kt + 1) * P, 0, 1)]
    q0, n = key_tile_queries(0, kt)
    middle = kt * P + HALF_WINDOW
    return [(q0, middle, q0 + HALF_WINDOW - kt * P, 1), (middle, q0 + n, 0, -1)]


PARTS = ([[(0, 0), (1, 192)], [(2, 0), (3, 256)]],
         [[(0, 0)], [(1, 0), (3, 384)], [(2, 0)]])
PART_COLS = tuple([sum(key_tile_queries(l, kt)[1] for kt, _ in part) for part in PARTS[l]] for l in (0, 1))
PROB_BUFS = 3
BACK_BUFS = 6
IDLE_HEAD, IDLE_TAIL, IDLE_FFN = 10, 4, 4
PV_LAG = 6
MAX_HEADS = tuple([min(GH, 512 // query_tile_keys(l, t)[1]) for t in range(NT)] for l in (0, 1))
MAX_ITEMS = tuple([(t, j) for t in range(NT) for j in range(GH // MAX_HEADS[l][t])] for l in (0, 1))


SUM_BANKS = ((0, 1, 2, 3), (4, 5, 2, 3), (0, 1, 5, 0))
K_BANK = (4, 6)


class Signal:

    def __init__(self, sem, per, primed=0, before=0):
        self.sem, self.per, self.primed, self.before = sem, per, primed, before

    def at(self, turn, n):
        return self.sem, turn * self.per + (n + self.before + self.primed)


PEELED = 7
STEPS = 8
STEP_TURNS = (NS - PEELED) // STEPS


def run_steps(eng, step):
    assert PEELED + STEPS * STEP_TURNS == NS

    def straight(q):
        step(q, q % 4, lambda stage: 0 <= q - stage < NS, lambda stage: (q - stage) // 4)

    for q in range(PEELED):
        straight(q)
    with eng.Fori(0, STEP_TURNS) as m:
        for i in range(PEELED, PEELED + STEPS):
            step(m * STEPS + i, i % 4, lambda stage: True, lambda stage: m * (STEPS // 4) + (i - stage) // 4)
    for q in range(NS, NS + 3):
        straight(q)


def rotary_tables():
    half = HD // 2
    inv = (np.float32(1.0) / np.float32(10000.0) ** (np.arange(half, dtype=np.float32) / np.float32(half))).astype(np.float32)
    f = np.arange(T, dtype=np.float32)[:, None] * inv[None, :]
    c, s = np.cos(f).astype(np.float32), np.sin(f).astype(np.float32)
    cos = np.stack([c, c], -1).reshape(T, HD)
    sin = np.stack([-s, s], -1).reshape(T, HD)
    return np.ascontiguousarray(np.concatenate([cos, sin], 1))


def build(nc, x, wqkv0, wo0, sink, w_gate, w_up, w_down, s_gate, s_up, s_down,
          wqkv1, b_qkv, wo1, b_out, gate_w, w13, w2, rotary, out):
    ctx = ExitStack()
    scope = [ctx]

    def sb(name, shape, dt=F32):
        return scope[-1].enter_context(nc.sbuf_tensor(name, shape, dt))

    def signal(name, per, primed=0):
        return Signal(ctx.enter_context(nc.semaphore(name)), per, primed)

    x3_dram = nc.dram_tensor("x3_rows", (B, T, C), F32, kind="Internal").ap().rearrange("b (t p) c -> b p t c", p=P)
    def staged(name, *raises):
        sem = ctx.enter_context(nc.semaphore(name))
        return [Signal(sem, sum(raises), 0, sum(raises[:i])) for i in range(len(raises))]

    xs_dram = nc.dram_tensor("slot_x", (NS * P, C), F32, kind="Internal").ap()
    ys_dram = nc.dram_tensor("slot_y", (NS * P, C), F32, kind="Internal").ap()

    with ctx:
        ps = ctx.enter_context(nc.psum_tensor("ps", [P, 8, 512], F32))

        ident = sb("ident", [P, P])
        ident_r = sb("ident_r", [P, P], F32R)
        ident_b = sb("ident_b", [P, P], BF16)
        band = sb("band", [P, 256], BF16)
        causal_q = sb("causal_q", [P, P], BF16)
        rot = sb("rot", [P, NT, 2, HD])
        carry = sb("carry", [P, 8])
        carry_p = sb("carry_p", [P, 2 * NG * 3])
        idle_b = sb("idle_b", [P, 512], BF16)
        table_in, table_out = sb("table_in", [P, 1]), sb("table_out", [P, 4])
        neg_half = sb("neg_half", [P, 1])
        sink4 = sb("sink4", [P, H])
        iota_e = sb("iota_e", [P, E])
        zeros = sb("zeros", [P, C])
        tri = sb("tri", [P, P], BF16)
        ones_b = sb("ones_b", [P, P], BF16)
        scan_keep = sb("scan_keep", [P, E, TT])
        ones_e = sb("ones_e", [P, E])
        iota_s = sb("iota_s", [P, NS])
        logit_all = sb("logit_all", [P, TT + NT, E])
        phase1 = ExitStack()
        scope.append(phase1)
        wqkv_s = [sb(f"wqkv{l}_s", [P, 2, KC, NQKV[l]], F32R) for l in (0, 1)]
        wo_s = [sb(f"wo{l}_s", [P, 2, KC, C], F32R) for l in (0, 1)]
        wg_sb = sb("wg_sb", [P, KC, INTER], F32R)
        wu_sb = sb("wu_sb", [P, KC, INTER], F32R)
        wd_sb = sb("wd_sb", [P, NI, C], F32R)
        sg_sb = sb("sg_sb", [P, NI])
        su_sb = sb("su_sb", [P, NI])
        sd_sb = sb("sd_sb", [P, C])
        bqkv_sb = sb("bqkv_sb", [P, 3 * C])
        bout_sb = sb("bout_sb", [P, C])
        x0 = sb("x0", [P, NT, C])
        x1 = sb("x1", [P, NT, C])
        x2 = sb("x2", [P, NT, C])
        x3 = sb("x3", [P, NT, C])
        xT = sb("xT", [P, 2, KC, T], F32R)
        gw_raw = sb("gw_raw", [P, KC, E])
        gw_s = sb("gw_s", [P, 2, KC, E], F32R)
        mv = sb("mv", [P, NT, 2])
        stats = sb("stats", [P, NT, 6])
        rstd = sb("rstd", [P, NT])
        q_st = sb("q_st", [P, H, STACK], F32R)
        k_st = sb("k_st", [P, H, STACK], F32R)
        v_aug = [sb(f"v_aug{l}", [P, NT, (KVH0, H)[l], 32]) for l in (0, 1)]
        kT = sb("kT", [P, H, T], F32R)
        attn_scope = ExitStack()
        scope.append(attn_scope)
        prob = sb("prob", [P, PROB_BUFS, GH, 512])
        qkv_sb = sb("qkv_sb", [P, 6 * C])
        rot_c = sb("rot_c", [P, 2 * C])
        rot_s = sb("rot_s", [P, NT * QKH[0] * HD])
        qT = sb("qT", [P, PAIRS, T], F32R)
        negmax = sb("negmax", [P, NT, H], F32R)
        shift_row = sb("shift_row", [GH, 2, T], F32R)
        oT = sb("oT", [P, T])
        rden = sb("rden", [P, NT, GH])
        o_sb = sb("o_sb", [P, NT, C])
        scope.pop()
        attn_scope.close()
        ffn_scope = ExitStack()
        scope.append(ffn_scope)
        gate_sb = sb("gate_sb", [P, 2, T])
        fuse_sb = sb("fuse_sb", [P, 2, T])
        fT = sb("fT", [P, 2, NI, T], F32R)
        scope.pop()
        ffn_scope.close()
        stage_scope = ExitStack()
        scope.append(stage_scope)
        w_raw = [sb(f"w_raw{i}", [P, KC, n]) for i, n in enumerate((NQKV[0], C, NQKV[1], C))]
        scope.pop()
        stage_scope.close()
        scope.pop()
        phase1.close()
        phase2 = ExitStack()
        scope.append(phase2)
        w13_sb = sb("w13_sb", [P, NE, KC, 2 * I], F32R)
        w2_sb = sb("w2_sb", [IH, NE, 2, C], F32R)
        x3_all = sb("x3_all", [P, TT, C])
        y_all = sb("y_all", [P, TT, C])
        score = sb("score", [P, TT, E])
        top8 = sb("top8", [P, TT, 8])
        idx8 = sb("idx8", [P, TT, 8], U32)
        idxf = sb("idxf", [P, TT, 2])
        tsum = sb("tsum", [P, TT])
        hot_all = sb("hot_all", [P, TT, 2, E])
        topw_all = sb("topw_all", [P, TT, 2])
        chosen = sb("chosen", [P, TT, E], BF16)
        tile_tot = sb("tile_tot", [P, E, TT])
        tile_inc = sb("tile_inc", [P, E, TT])
        n_int = sb("n_int", [P, E], I32)
        room = sb("room", [P, E])
        room_inc = sb("room_inc", [P, E])
        pos = sb("pos", [P, TT, E])
        pos_hot = sb("pos_hot", [P, TT, 2, E])
        slot_f = sb("slot_f", [P, TT, 2])
        slot = sb("slot", [P, TT, 2], U32)
        past = sb("past", [P, NS, E])
        owner_f = sb("owner_f", [P, NS])
        owner = sb("owner", [P, NS], I32)
        xg = sb("xg", [P, NT, C])
        xgT = sb("xgT", [P, 2, KC, T], F32R)
        xs_sb = sb("xs_sb", [P, 4, C])
        xsT = sb("xsT", [P, 2, 2, KC, P], F32R)
        act_a = sb("act_a", [P, 2, I])
        h_sb = sb("h_sb", [P, 2, I])
        hT = sb("hT", [IH, 2, 2, 2, P], F32R)
        ys_sb = sb("ys_sb", [P, 4, C])
        back = sb("back", [P, BACK_BUFS, 2, C])
        mv2 = sb("mv2", [P, TT, 2])
        stats2 = sb("stats2", [P, TT, 6])
        rstd2 = sb("rstd2", [P, TT])
        scope.pop()
        phase2.close()

        def tile_of(buffer, width, l, t):
            o = (t if l == 0 else t % 2) * width
            return buffer[:, o:o + width]

        def qkv_tile(l, t):
            return tile_of(qkv_sb, NQKV[l], l, t)

        def rot_tile(l, t):
            return tile_of(rot_s, QKH[l] * HD, l, t)

        HEAD_STEPS = NT + 2
        N1 = len(PARTS[1])
        HEAD_SLOT = NG + 2 - HEAD_STEPS // N1
        assert HEAD_STEPS % N1 == 0 and HEAD_SLOT >= NG

        w_in = [signal(f"w_in{i}", 0) for i in range(4)]
        consts_in = signal("consts_in", 0)
        w_int8 = signal("w_int8", 0)
        made = signal("made", 0)
        w_hi = signal("w_hi", 0)
        w_lo = signal("w_lo", 0)
        start_dve = signal("start_dve", 0)
        x0_in = signal("x0_in", 16)
        SPLITS = ("x3", "o0", "x1", "x2", "o1")
        tr, hi, lo = (dict(zip(SPLITS, staged(n, *[NT] * len(SPLITS)))) for n in ("tr", "hi", "lo"))
        tr["x0"], hi["x0"], lo["x0"] = (signal(n, NT) for n in ("x0_tr", "x0_hi", "x0_lo"))
        qkv, qkv_out, cosd, roped, st_hi, st_lo, v_put = (staged(n, k, k) for n, k in (
            ("qkv", NT), ("qkv_out", NT), ("cosd", NT), ("roped", NT), ("st_hi", 2 * NT), ("st_lo", 2 * NT), ("v_put", NT)))
        q_tr, k_tr, q_out, k_even, k_odd = (staged(n, NT, NT) for n in ("q_tr", "k_tr", "q_out", "k_even", "k_odd"))
        raw_score, maxed = (staged(n, *[NG * len(MAX_ITEMS[l]) for l in (0, 1)]) for n in ("raw_score", "maxed"))
        sined = staged("sined", 2 * NT, 2 * NT)
        sunk = signal("sunk", NG)
        sh_tr, sh_out = (staged(n, NG, NG) for n in ("sh_tr", "sh_out"))
        sh_row = [staged(f"sh_row{g}", GH * 16, GH * 16) for g in range(NG)]
        scored, exped = (staged(n, *[NG * GH * len(PARTS[l]) for l in (0, 1)]) for n in ("scored", "exped"))
        kept = staged("kept", *[NG * len(PARTS[l]) for l in (0, 1)])
        pv = staged("pv", *[NG * len(PARTS[l]) for l in (0, 1)])
        oT_out, o_tr, o_put, rden_done = (staged(n, NG, NG) for n in ("oT_out", "o_tr", "o_put", "rden"))
        proj = staged("proj", NT, NT)
        var_done, rstd_done = (staged(n, NT, NT, NT) for n in ("var", "rstd"))
        normed = [signal(f"normed{i}", NT, int(i == 2)) for i in range(3)]
        gated, upped, silued, fused, f_hi, f_lo = (signal(s, NI) for s in ("gated", "upped", "silued", "fused", "f_hi", "f_lo"))
        down = signal("down", NT)
        biased = signal("biased", NT)
        x3_kept = signal("x3_kept", 16, 16)
        logits, logit_kept = signal("logits", 1), signal("logit_kept", 1)
        DVE_STEPS = NG + 10 * NT
        dve_step = signal("dve_step", DVE_STEPS)
        x3_back = signal("x3_back", 0)
        zero_x = signal("zero_x", 0)
        shared_in = signal("shared_in", 0)
        w13_in, w2_in, gw_in = signal("w13_in", 0), signal("w2_in", 0), signal("gw_in", 0)
        gw_split = signal("gw_split", 0)
        exp_l = signal("exp_l", 0)
        counted, place = signal("counted", 0), signal("place", 0)
        slotted, owned = signal("slotted", 0), signal("owned", 0)
        scattered = signal("scattered", 0)
        U = SHARED * NT
        xg_in = signal("xg_in", 16)
        xg_tr, xg_hi, xg_lo = (signal(n, NT, int(n == "xg_tr")) for n in ("xg_tr", "xg_hi", "xg_lo"))
        sh_up, sh_silu, sh_h, sh_htr, sh_hhi, sh_hlo = (signal(n, U) for n in ("sh_up", "sh_silu", "sh_h", "sh_htr", "sh_hhi", "sh_hlo"))
        sh_down, sh_y = signal("sh_down", NT), signal("sh_y", NT)
        xs_in = [signal(f"xs_in{r}", 0) for r in range(4)]
        ys_kept = [signal(f"ys_kept{r}", 0) for r in range(4)]
        xs_tr, xs_hi, xs_lo, e_up, e_silu, e_h, e_htr, e_hhi, e_hlo, e_down, e_y = (
            signal(n, 0) for n in ("xs_tr", "xs_hi", "xs_lo", "e_up", "e_silu", "e_h", "e_htr", "e_hhi", "e_hlo", "e_down", "e_y"))
        back_in = [signal(f"back_in{r}", 0) for r in range(BACK_BUFS)]
        y_step = signal("y_step", 0)
        y_var, y_rstd, y_norm, y_out = (signal(n, 0) for n in ("y_var", "y_rstd", "y_norm", "y_out"))

        block = ctx.enter_context(nc.Block())

        @block.sync
        def _(sp):
            raw = (wqkv0, wo0, wqkv1, wo1)
            for i in range(4):
                sp.dma_start(w_raw[i][:], raw[i].rearrange("(k p) n -> p k n", p=P)).then_inc(w_in[i].sem, 16)
            x_tiles = x.rearrange("b (t p) c -> b p t c", p=P)
            sp.dma_start(x0[:], x_tiles[0]).then_inc(x0_in.sem, 16)

            def batch(b, last):
                for l in (0, 1):
                    for g in range(NG):
                        sp.wait_ge(*sh_out[l].at(b, g + 1))
                        for j in range(GH):
                            r = STACK * (j % 2) + SHIFT
                            sp.dma_start(qT[r:r + 1, 2 * g + j // 2, :].bitcast(F32),
                                         shift_row[j:j + 1, g % 2, :].bitcast(F32)).then_inc(sh_row[g][l].sem, 16)
                    if l == 0 and not last:
                        sp.wait_ge(*normed[0].at(b, NT))
                        sp.dma_start(x0[:], x_tiles[b + 1]).then_inc(x0_in.sem, 16)
                sp.wait_ge(*normed[2].at(b, NT))
                sp.dma_start(x3_dram[b], x3[:]).then_inc(x3_kept.sem, 16)

            with sp.Fori(0, B - 1) as b:
                batch(b, False)
            batch(B - 1, True)
            sp.wait_ge(*x3_kept.at(B, 0))
            sp.wait_ge(*logit_kept.at(B, 1))
            sp.dma_start(x3_all[:].rearrange("p (b t) c -> p b t c", b=B), x3_dram.rearrange("b p t c -> p b t c")).then_inc(x3_back.sem, 16)
            with sp.Fori(0, B) as b:
                sp.wait_ge(*xg_tr.at(b, 0))
                sp.dma_start(xg[:], x3_dram[b]).then_inc(xg_in.sem, 16)

            def load(q, r):
                if not (isinstance(q, int) and q < 4):
                    sp.wait_ge(xs_tr.sem, q - 3)
                sp.dma_start(xs_sb[:, r, :], xs_dram.rearrange("(s p) c -> s p c", p=P)[q]).then_inc(xs_in[r].sem, 16)

            sp.wait_ge(scattered.sem, 16 * 2 * TT)
            for q in range(4):
                load(q, q)
            with sp.Fori(0, (NS - 4) // 4) as m:
                for r in range(4):
                    load(m * 4 + (4 + r), r)
            for q in range(4 + (NS - 4) // 4 * 4, NS):
                load(q, q % 4)
            for g in range(B):
                sp.wait_ge(y_norm.sem, (g + 1) * NT)
                sp.dma_start(out[g].rearrange("(t p) c -> p t c", p=P), y_all[:, g * NT:(g + 1) * NT, :]).then_inc(y_out.sem, 16)
            sp.wait_ge(y_out.sem, 16 * B)

        @block.gpsimd
        def _(pool):
            n_made = [0]

            def then(ins):
                n_made[0] += 1
                ins.then_inc(made.sem, 1)
                pool.wait_ge(made.sem, n_made[0])

            then(pool.memset(ident[:], 0.0))
            then(pool.affine_select(out=ident[:], in_=ident[:], compare_op=ALU.not_equal, fill=1.0, base=0,
                                    pattern=[[-1, P]], channel_multiplier=1))
            pool.dma_start(wg_sb[:], w_gate.bitcast(I8).rearrange("(k p) n -> p k n", p=P)).then_inc(w_int8.sem, 16)
            pool.dma_start(wu_sb[:], w_up.bitcast(I8).rearrange("(k p) n -> p k n", p=P)).then_inc(w_int8.sem, 16)
            pool.dma_start(wd_sb[:], w_down.bitcast(I8).rearrange("(k p) n -> p k n", p=P)).then_inc(w_int8.sem, 16)
            then(pool.tensor_copy(ident_r[:], ident[:]))
            then(pool.memset(ident_b[:], 0.0))
            then(pool.affine_select(out=ident_b[:], in_=ident_b[:], compare_op=ALU.not_equal, fill=1.0, base=0,
                                    pattern=[[-1, P]], channel_multiplier=1))
            then(pool.memset(band[:], 0.0))
            then(pool.affine_select(out=band[:], in_=band[:], compare_op=ALU.is_ge, fill=MASKED, base=0,
                                    pattern=[[1, 256]], channel_multiplier=-1))
            then(pool.affine_select(out=band[:], in_=band[:], compare_op=ALU.is_ge, fill=MASKED, base=2 * HALF_WINDOW,
                                    pattern=[[-1, 256]], channel_multiplier=1))
            then(pool.memset(causal_q[:], 0.0))
            then(pool.affine_select(out=causal_q[:], in_=causal_q[:], compare_op=ALU.is_ge, fill=MASKED, base=0,
                                    pattern=[[-1, P]], channel_multiplier=1))
            then(pool.memset(neg_half[:], -0.5))
            then(pool.memset(scan_keep[:], 1.0))
            then(pool.memset(scan_keep[:, :, 0:1], 0.0))
            then(pool.memset(ones_e[:], 1.0))
            then(pool.memset(ones_b[:], 1.0))
            then(pool.memset(tri[:], 0.0))
            then(pool.affine_select(out=tri[:], in_=tri[:], compare_op=ALU.is_ge, fill=1.0, base=0,
                                    pattern=[[-1, P]], channel_multiplier=1))
            then(pool.iota(iota_s[:], pattern=[[P, NS]], base=0, channel_multiplier=0,
                           allow_small_or_imprecise_dtypes=True))
            then(pool.iota(iota_e[:], pattern=[[1, E]], base=0, channel_multiplier=0,
                           allow_small_or_imprecise_dtypes=True))
            pool.wait_ge(consts_in.sem, 7 * 16)
            then(pool.tensor_scalar(out=sink4[:], in0=sink4[:], scalar1=1.0 / SCALE, scalar2=None, op0=ALU.mult))
            then(pool.memset(q_st[:].bitcast(F32), 0.0))
            then(pool.memset(k_st[:].bitcast(F32), 0.0))
            then(pool.memset(k_st[:, :, SHIFT:SHIFT + 1].bitcast(F32), 1.0))
            for l in (0, 1):
                then(pool.memset(v_aug[l][:], 0.0))
                then(pool.memset(v_aug[l][:, :, :, HD:HD + 1], 1.0))
            assert n_made[0] == MADE

            def project_rest(b, l, t):
                nh, kvh = QKH[l], (KVH0, H)[l]
                pool.wait_ge(*qkv_out[l].at(b, t + 1))
                if t >= 1:
                    pool.wait_ge(*roped[l].at(b, t))
                cos = rot[:, t, 0, :].unsqueeze(1).to_broadcast([P, nh, HD])
                pool.tensor_tensor(out=rot_c[:, 0:nh * HD].rearrange("p (h d) -> p h d", d=HD),
                                   in0=qkv_tile(l, t)[:, 0:nh * HD].rearrange("p (h d) -> p h d", d=HD),
                                   in1=cos, op=ALU.mult).then_inc(cosd[l].sem, 1)
                pool.tensor_copy(v_aug[l][:, t, :, 0:HD],
                                 qkv_tile(l, t)[:, nh * HD:(nh + kvh) * HD].rearrange("p (h d) -> p h d", d=HD)
                                 ).then_inc(v_put[l].sem, 1)

            def head_step(b, k):
                if 1 <= k <= NT:
                    project_rest(b, 0, k - 1)

            def batch(b, last):

                def rstd_of(i):
                    for t in range(NT):
                        pool.wait_ge(*var_done[i].at(b, t + 1))
                        pool.tensor_tensor(out=rstd[:, t:t + 1], in0=mv[:, t, 1:2], in1=neg_half[:],
                                           op=ALU.pow).then_inc(rstd_done[i].sem, 1)

                for l in (0, 1):
                    if l == 1:
                        for t in range(NT):
                            project_rest(b, 1, t)
                    if l == 1:
                        for t in range(NT):
                            pool.wait_ge(*lo["x2"].at(b, t + 1))
                            pool.tensor_tensor(out=x2[:, t, :], in0=x2[:, t, :], in1=bout_sb[:],
                                               op=ALU.add).then_inc(biased.sem, 1)
                    for g in range(NG):
                        for p, part in enumerate(PARTS[l]):
                            buf = (g * len(PARTS[l]) + p) % PROB_BUFS
                            pool.wait_ge(*exped[l].at(b, (g * len(PARTS[l]) + p + 1) * GH))
                            c = (l * NG + g) * 3 + p
                            pool.tensor_tensor(out=carry_p[:, c:c + 1], in0=neg_half[:], in1=neg_half[:], op=ALU.add)
                            for kt, col in part:
                                q0, n = key_tile_queries(l, kt)
                                for lo_q, hi_q, base, sign in unseen(l, kt):
                                    sel = prob[:, buf, :, col + lo_q - q0:col + hi_q - q0]
                                    ins = pool.affine_select(out=sel, in_=sel, compare_op=ALU.is_ge, fill=0.0, base=base,
                                                             pattern=[[0, GH], [sign, hi_q - lo_q]], channel_multiplier=-sign)
                            ins.then_inc(kept[l].sem, 1)
                            if l == 1 and g + 2 >= HEAD_SLOT and not last:
                                head_step(b + 1, (g + 2 - HEAD_SLOT) * N1 + p)
                    rstd_of((0, 2)[l])
                    if l == 0:
                        for m in range(NI):
                            pool.wait_ge(*f_hi.at(b, m + 1))
                            pool.tensor_tensor(out=fT[:, 1, m, :], in0=fuse_sb[:, m % 2, :],
                                               in1=fT[:, 0, m, :].bitcast(F32), op=ALU.subtract).then_inc(f_lo.sem, 1)
                        rstd_of(1)

            for k in range(HEAD_STEPS):
                head_step(0, k)
            with pool.Fori(0, B - 1) as b:
                batch(b, False)
            batch(B - 1, True)

            pool.wait_ge(*x3_kept.at(B, 0))
            pool.wait_ge(*logit_kept.at(B, 1))
            pool.dma_start(w13_sb[:, E:NE, :, :], w13[:, E:NE, :, :]).then_inc(shared_in.sem, 16)
            pool.dma_start(w2_sb[:, E:NE, :, :], w2[:, E:NE, :, :]).then_inc(shared_in.sem, 16)
            for e in range(0, E, 4):
                pool.dma_start(w13_sb[:, e:e + 4, :, :], w13[:, e:e + 4, :, :]).then_inc(w13_in.sem, 16)
                pool.dma_start(w2_sb[:, e:e + 4, :, :], w2[:, e:e + 4, :, :]).then_inc(w2_in.sem, 16)
            pool.wait_ge(zero_x.sem, 16)
            pool.wait_ge(slotted.sem, 1)
            pool.wait_ge(x3_back.sem, 16)
            for t in range(TT):
                for k in (0, 1):
                    pool.indirect_dma_start(out=xs_dram, out_offset=bass.IndirectOffsetOnAxis(ap=slot[:, t, k:k + 1], axis=0),
                                            in_=x3_all[:, t, :], in_offset=None).then_inc(scattered.sem, 16)

            def store(q, r):
                pool.wait_ge(e_y.sem, q + 1)
                pool.dma_start(ys_dram.rearrange("(s p) c -> s p c", p=P)[q], ys_sb[:, r, :]).then_inc(ys_kept[r].sem, 16)

            for q in range(3):
                store(q, q)
            with pool.Fori(0, (NS - 3) // 4) as m:
                for i in range(4):
                    store(m * 4 + (3 + i), (3 + i) % 4)
            for r in range(4):
                pool.wait_ge(ys_kept[r].sem, 16 * len(range(r, NS, 4)))
            def rstd_of_pair(t):
                pool.wait_ge(y_var.sem, t + 2)
                pool.tensor_tensor(out=rstd2[:, t:t + 2], in0=mv2[:, t:t + 2, 1], in1=neg_half[:].to_broadcast([P, 2]),
                                   op=ALU.pow).then_inc(y_rstd.sem, 1)

            for t in range(TT):
                if t >= BACK_BUFS:
                    pool.wait_ge(y_var.sem, t - BACK_BUFS + 1)
                for k in (0, 1):
                    pool.indirect_dma_start(out=back[:, t % BACK_BUFS, k, :], out_offset=None, in_=ys_dram,
                                            in_offset=bass.IndirectOffsetOnAxis(ap=slot[:, t, k:k + 1], axis=0)
                                            ).then_inc(back_in[t % BACK_BUFS].sem, 16)
                if t >= 4 and t % 2 == 0:
                    rstd_of_pair(t - 4)
            rstd_of_pair(TT - 4)
            rstd_of_pair(TT - 2)

        @block.scalar
        def _(act):
            act.dma_start(rot[:], rotary.rearrange("(t p) (a d) -> p t a d", p=P, a=2)).then_inc(consts_in.sem, 16)
            act.dma_start(sink4[:], sink.partition_broadcast(P)).then_inc(consts_in.sem, 16)
            act.dma_start(sg_sb[:], s_gate).then_inc(consts_in.sem, 16)
            act.dma_start(su_sb[:], s_up).then_inc(consts_in.sem, 16)
            act.dma_start(sd_sb[:], s_down.partition_broadcast(P)).then_inc(consts_in.sem, 16)
            act.dma_start(bqkv_sb[:], b_qkv.partition_broadcast(P)).then_inc(consts_in.sem, 16)
            act.dma_start(bout_sb[:], b_out.partition_broadcast(P)).then_inc(consts_in.sem, 16)
            act.dma_start(gw_raw[:], gate_w.rearrange("(k p) e -> p k e", p=P)).then_inc(gw_in.sem, 16)
            dst = (wqkv_s[0], wo_s[0], wqkv_s[1], wo_s[1])

            def load_table(i, func):
                act.activation(table_out[:, i:i + 1], table_in[:], func)

            def weights_hi(i):
                act.wait_ge(w_in[i].sem, 16)
                act.activation(dst[i][:, 0, :, :], w_raw[i][:], ACT.Copy).then_inc(w_hi.sem, 1)

            act.wait_ge(start_dve.sem, 1)
            load_table(3, ACT.Exp)
            weights_hi(0)
            act.wait_ge(start_dve.sem, 1)
            act.dma_start(xs_dram.rearrange("(s p) c -> p s c", p=P), zeros[:].unsqueeze(1).to_broadcast([P, NS, C])
                          ).then_inc(zero_x.sem, 16)

            def split_hi(b, n, t, bank0=6):
                act.wait_ge(*tr[n].at(b, t + 1))
                act.activation(xT[:, 0, :, t * P:(t + 1) * P],
                               ps[:, bank0 + t % 2, 0:C].rearrange("p (k q) -> p k q", k=KC),
                               ACT.Copy).then_inc(hi[n].sem, 1)

            def logits_out(turn):
                act.wait_ge(*logits.at(turn, 1))
                dst = logit_all[:, turn * NT:(turn + 1) * NT, :] if isinstance(turn, int) else logit_all[:, bass.ds(turn * NT, NT), :]
                act.activation(dst, ps[:, 0, 0:NT * E].rearrange("p (t e) -> p t e", e=E), ACT.Copy).then_inc(logit_kept.sem, 1)

            def head_step(b, k):
                if k < NT:
                    split_hi(b, "x0", k, bank0=0)
                if 1 <= k <= NT:
                    act.wait_ge(*qkv[0].at(b, k))
                    act.activation(qkv_tile(0, k - 1), ps[:, 2, 0:NQKV[0]], ACT.Copy).then_inc(qkv_out[0].sem, 1)

            def stack(b, l, t):
                act.wait_ge(*roped[l].at(b, t + 1))
                if t >= 1:
                    act.wait_ge(*q_tr[l].at(b, t))
                q = rot_tile(l, t)[:, 0:C].rearrange("p (h d) -> p h d", d=HD)
                act.activation(q_st[:, :, 0:2 * HD].rearrange("p h (r d) -> p h r d", r=2),
                               q.unsqueeze(2).to_broadcast([P, H, 2, HD]), ACT.Copy).then_inc(st_hi[l].sem, 1)
                if t >= 1:
                    act.wait_ge(*k_tr[l].at(b, t))
                nk = QKH[l] - H
                k = rot_tile(l, t)[:, C:C + nk * HD].rearrange("p (h d) -> p h d", d=HD)
                if l == 1:
                    kd = k_st[:, :, 0:4 * HD].rearrange("p h (r d) -> p h r d", r=2)[:, :, :, 0:HD]
                    act.activation(kd, k.unsqueeze(2).to_broadcast([P, H, 2, HD]), ACT.Copy).then_inc(st_hi[l].sem, 1)
                else:
                    kk = k_st[:, 0:2 * KVH0, :].rearrange("p (h r) s -> p h r s", r=2)
                    kb = k.unsqueeze(2).to_broadcast([P, KVH0, 2, HD])
                    act.activation(kk[:, :, :, 0:HD], kb, ACT.Copy)
                    act.activation(kk[:, :, :, 2 * HD:3 * HD], kb, ACT.Copy).then_inc(st_hi[l].sem, 1)
                if t >= 1:
                    stack_out(b, l, t - 1)

            def stack_out(b, l, t):
                act.wait_ge(*q_tr[l].at(b, t + 1))
                act.activation(qT[:, :, t * P:(t + 1) * P], ps[:, 2:4, :].rearrange("p a (n q) -> p (a n) q", q=P),
                               ACT.Copy).then_inc(q_out[l].sem, 1)
                n_blk = (KVH0, PAIRS)[l]
                act.wait_ge(*k_tr[l].at(b, t + 1))
                act.activation(kT[STACK:P, 1:2 * n_blk:2, t * P:(t + 1) * P],
                               ps[STACK:P, K_BANK[l]:K_BANK[l] + 2, :].rearrange("p a (n q) -> p (a n) q", q=P)[:, 0:n_blk, :],
                               ACT.Copy).then_inc(k_odd[l].sem, 1)

            def batch(b, last):

                def attention(l):
                    n_parts = len(PARTS[l])
                    if l == 1:
                        for t in range(NT):
                            split_hi(b, "x2", t)
                        for t in range(NT):
                            stack(b, 1, t)
                        stack_out(b, 1, NT - 1)

                    def shift_out(g):
                        act.wait_ge(*sh_tr[l].at(b, g + 1))
                        if g >= 2:
                            act.wait_ge(*sh_row[g - 2][l].at(b, GH * 16))
                        act.activation(shift_row[:, g % 2, :], ps[0:GH, 7, :], ACT.Copy).then_inc(sh_out[l].sem, 1)

                    def oT_copy(g):
                        act.wait_ge(*pv[l].at(b, (g + 1) * n_parts))
                        if g >= 1:
                            act.wait_ge(*o_tr[l].at(b, g))
                        act.activation(oT[:], ps[:, 6, :], ACT.Copy).then_inc(oT_out[l].sem, 1)

                    for s in range(NG + 2):
                        if 1 <= s <= NG:
                            shift_out(s - 1)
                        if l == 0 and s < 2:
                            for t in (2 * s, 2 * s + 1):
                                split_hi(b, "x3", t, bank0=4)
                        if l == 0 and s == NG + 1:
                            logits_out(b)
                        g = s - 2
                        if g < 0:
                            continue
                        for p in range(n_parts):
                            n = PART_COLS[l][p]
                            part = g * n_parts + p
                            if part >= PROB_BUFS:
                                act.wait_ge(*pv[l].at(b, part - PROB_BUFS + 1))
                            for j in range(GH):
                                i = part * GH + j
                                act.wait_ge(*scored[l].at(b, i + 1))
                                act.activation(prob[:, part % PROB_BUFS, j, 0:n], ps[:, 3 + i % 3, 0:n], ACT.Exp,
                                               scale=SCALE).then_inc(exped[l].sem, 1)
                                if p == 1 and j == 1 and g >= 1:
                                    oT_copy(g - 1)
                            if l == 1 and s >= HEAD_SLOT and not last:
                                head_step(b + 1, (s - HEAD_SLOT) * N1 + p)
                    if l == 0:
                        load_table(0, ACT.Silu)
                    oT_copy(NG - 1)
                    for t in range(NT):
                        split_hi(b, ("o0", "o1")[l], t)

                attention(0)
                for t in range(NT):
                    split_hi(b, "x1", t)
                for m in range(NI):
                    act.wait_ge(*gated.at(b, m + 1))
                    if m >= 2:
                        act.wait_ge(*fused.at(b, m - 1))
                    act.activation(gate_sb[:, m % 2, :], ps[:, m % 2, :], ACT.Silu,
                                   scale=sg_sb[:, m:m + 1]).then_inc(silued.sem, 1)
                    if m >= 1:
                        act.wait_ge(*fused.at(b, m))
                        act.activation(fT[:, 0, m - 1, :], fuse_sb[:, (m - 1) % 2, :], ACT.Copy).then_inc(f_hi.sem, 1)
                act.wait_ge(*fused.at(b, NI))
                act.activation(fT[:, 0, NI - 1, :], fuse_sb[:, (NI - 1) % 2, :], ACT.Copy).then_inc(f_hi.sem, 1)
                load_table(1, ACT.Exp)
                attention(1)
                if not last:
                    for t in range(NT):
                        stack(b + 1, 0, t)
                    stack_out(b + 1, 0, NT - 1)
            for k in range(HEAD_STEPS):
                head_step(0, k)
            act.wait_ge(made.sem, MADE)
            act.wait_ge(start_dve.sem, 2)
            for t in range(NT):
                stack(0, 0, t)
            stack_out(0, 0, NT - 1)
            for i in range(1, 4):
                weights_hi(i)
            act.wait_ge(gw_in.sem, 16)
            act.activation(gw_s[:, 0, :, :], gw_raw[:], ACT.Copy).then_inc(gw_split.sem, 1)
            with act.Fori(0, B - 1) as b:
                batch(b, False)
            batch(B - 1, True)
            for t in range(NT):
                split_hi(B, "x3", t, bank0=4)
            logits_out(B)

            act.wait_ge(*logit_kept.at(B, 1))
            act.wait_ge(*x3_kept.at(B, 0))
            act.activation(score[:], logit_all[:, NT:, :], ACT.Exp, scale=-1.0).then_inc(exp_l.sem, 1)
            load_table(2, ACT.Silu)

            with act.Fori(0, B) as b:
                for t in range(NT):
                    act.wait_ge(*xg_tr.at(b, t + 1))
                    act.activation(xgT[:, 0, :, t * P:(t + 1) * P],
                                   ps[:, 3 + t % 2, 0:C].rearrange("p (k q) -> p k q", k=KC),
                                   ACT.Copy).then_inc(xg_hi.sem, 1)
                for u in range(U + 1):
                    if u < U:
                        act.wait_ge(*sh_up.at(b, u + 1))
                        act.activation(act_a[:, u % 2, :], ps[:, u % 2, 0:I], ACT.Silu).then_inc(sh_silu.sem, 1)
                    if u >= 1:
                        act.wait_ge(*sh_htr.at(b, u))
                        act.activation(hT[:, (u - 1) % 2, 0, :, :],
                                       ps[0:IH, 3 + (u - 1) % 2, 0:2 * P].rearrange("p (k q) -> p k q", k=2),
                                       ACT.Copy).then_inc(sh_hhi.sem, 1)

            def scalar_step(q, r, on, before):
                if on(0):
                    act.wait_ge(xs_tr.sem, q + 1)
                    act.activation(xsT[:, r % 2, 0, :, :], ps[:, 3 + r % 2, 0:C].rearrange("p (k n) -> p k n", k=KC),
                                   ACT.Copy).then_inc(xs_hi.sem, 1)
                if on(1):
                    act.wait_ge(e_up.sem, q)
                    act.activation(act_a[:, (r - 1) % 2, :], ps[:, (r - 1) % 2, 0:I], ACT.Silu).then_inc(e_silu.sem, 1)
                if on(2):
                    act.wait_ge(e_htr.sem, q - 1)
                    act.activation(hT[:, (r - 2) % 2, 0, :, :], ps[0:IH, 5 + (r - 2) % 2, 0:2 * P].rearrange("p (k n) -> p k n", k=2),
                                   ACT.Copy).then_inc(e_hhi.sem, 1)

            run_steps(act, scalar_step)

        @block.vector
        def _(dve):
            dst = (wqkv_s[0], wo_s[0], wqkv_s[1], wo_s[1])
            dve.memset(table_in[:], 0.0)
            dve.memset(idle_b[:], 0.0)
            dve.memset(zeros[:], 0.0).then_inc(start_dve.sem, 1)
            for i, sig in enumerate((x3_kept, xg_tr)):
                dve.memset(carry[:, i + 1:i + 2], 0.0).then_inc(sig.sem, sig.primed)
            dve.memset(x3[:], 0.0).then_inc(normed[2].sem, 1)
            dve.memset(kT[:].bitcast(F32), 0.0).then_inc(start_dve.sem, 1)

            def weights_lo(i):
                dve.wait_ge(w_hi.sem, i + 1)
                dve.tensor_tensor(out=dst[i][:, 1, :, :], in0=w_raw[i][:], in1=dst[i][:, 0, :, :].bitcast(F32),
                                  op=ALU.subtract).then_inc(w_lo.sem, 1)

            weights_lo(0)
            dve.wait_ge(consts_in.sem, 7 * 16)

            def split_lo(b, n, t, bank0=6):
                dve.wait_ge(*hi[n].at(b, t + 1))
                dve.tensor_tensor(out=xT[:, 1, :, t * P:(t + 1) * P],
                                  in0=ps[:, bank0 + t % 2, 0:C].rearrange("p (k q) -> p k q", k=KC),
                                  in1=xT[:, 0, :, t * P:(t + 1) * P].bitcast(F32),
                                  op=ALU.subtract).then_inc(lo[n].sem, 1)

            def rope(b, l, t):
                nh = QKH[l]
                dve.wait_ge(*qkv_out[l].at(b, t + 1))
                src = qkv_tile(l, t)[:, 0:nh * HD].rearrange("p (h i a) -> p h i a", i=HD // 2, a=2)
                dst_ = rot_tile(l, t).rearrange("p (h i a) -> p h i a", i=HD // 2, a=2)
                sin = rot[:, t, 1, :].rearrange("p (i a) -> p i a", a=2)
                if t >= 2 and l == 1:
                    dve.wait_ge(*st_hi[l].at(b, 2 * (t - 1)))
                    dve.wait_ge(*st_lo[l].at(b, 2 * (t - 1)))
                for a in (0, 1):
                    dve.tensor_tensor(out=dst_[:, :, :, a], in0=src[:, :, :, 1 - a],
                                      in1=sin[:, :, a].unsqueeze(1).to_broadcast([P, nh, HD // 2]), op=ALU.mult
                                      ).then_inc(sined[l].sem, 1)
                dve.wait_ge(*sined[l].at(b, 2 * t + 2))
                dve.wait_ge(*cosd[l].at(b, t + 1))
                dve.tensor_tensor(out=rot_tile(l, t), in0=rot_tile(l, t), in1=rot_c[:, 0:nh * HD],
                                  op=ALU.add).then_inc(roped[l].sem, 1)

            def stack(b, l, t):
                nk = QKH[l] - H
                dve.wait_ge(*roped[l].at(b, t + 1))
                dve.wait_ge(*st_hi[l].at(b, 2 * t + 1))
                q = rot_tile(l, t)[:, 0:C].rearrange("p (h d) -> p h d", d=HD)
                dve.tensor_tensor(out=q_st[:, :, 2 * HD:3 * HD], in0=q, in1=q_st[:, :, 0:HD].bitcast(F32),
                                  op=ALU.subtract).then_inc(st_lo[l].sem, 1)
                dve.wait_ge(*st_hi[l].at(b, 2 * t + 2))
                k = rot_tile(l, t)[:, C:C + nk * HD].rearrange("p (h d) -> p h d", d=HD)
                if l == 1:
                    dve.tensor_tensor(out=k_st[:, :, HD:2 * HD], in0=k, in1=k_st[:, :, 0:HD].bitcast(F32),
                                      op=ALU.subtract).then_inc(st_lo[l].sem, 1)
                else:
                    kk = k_st[:, 0:2 * KVH0, :].rearrange("p (h r) s -> p h r s", r=2)
                    dve.tensor_tensor(out=kk[:, :, :, HD:2 * HD], in0=k.unsqueeze(2).to_broadcast([P, KVH0, 2, HD]),
                                      in1=kk[:, :, :, 0:HD].bitcast(F32), op=ALU.subtract).then_inc(st_lo[l].sem, 1)
                if t >= 1:
                    k_copy(b, l, t - 1)

            def k_copy(b, l, t):
                n_blk = (KVH0, PAIRS)[l]
                dve.wait_ge(*k_tr[l].at(b, t + 1))
                dve.tensor_copy(kT[0:STACK, 0:2 * n_blk:2, t * P:(t + 1) * P],
                                ps[0:STACK, K_BANK[l]:K_BANK[l] + 2, :].rearrange("p a (n q) -> p (a n) q", q=P)[:, 0:n_blk, :]
                                ).then_inc(k_even[l].sem, 1)

            def head_step(b, k):
                if k < NT:
                    split_lo(b, "x0", k, bank0=0)
                if k >= 2:
                    rope(b, 0, k - 2)

            def batch(b, last):
                steps = [0]

                def then(ins, carrier=False):
                    steps[0] += 1
                    ins.then_inc(dve_step.sem, 1)
                    dve.wait_ge(*dve_step.at(b, steps[0]))
                    if carrier:
                        dve.memset(carry[:, 0:1], 0.0)

                def norm(i, ready, scale, residual, result):
                    if i == 2:
                        dve.wait_ge(*x3_kept.at(b, 0))
                    for t in range(NT):
                        dve.wait_ge(*ready.at(b, t + 1))
                        y = ps[:, SUM_BANKS[i][t], 0:C]
                        if scale is not None:
                            then(dve.tensor_tensor(out=result[:, t, :], in0=y, in1=scale, op=ALU.mult))
                            y = result[:, t, :]
                        if i == 2:
                            dve.wait_ge(*biased.at(b, t + 1))
                        then(dve.tensor_tensor(out=result[:, t, :], in0=y, in1=residual[:, t, :], op=ALU.add))
                        then(dve.bn_stats(out=stats[:, t, :], in_=result[:, t, :]), carrier=True)
                        then(dve.bn_aggr(out=mv[:, t, :], in_=stats[:, t, :]))
                        dve.tensor_scalar(out=mv[:, t, 1:2], in0=mv[:, t, 1:2], scalar1=EPS, scalar2=None,
                                          op0=ALU.add).then_inc(var_done[i].sem, 1)
                        if t >= 1:
                            scale_tile(i, t - 1, result)
                        if i < 2 and t >= 2:
                            split_lo(b, ("x1", "x2")[i], t - 2)
                        if i == 2 and not last:
                            stack(b + 1, 0, t)
                    scale_tile(i, NT - 1, result)
                    if i < 2:
                        for t in (NT - 2, NT - 1):
                            split_lo(b, ("x1", "x2")[i], t)
                    if i == 2 and not last:
                        k_copy(b + 1, 0, NT - 1)

                def scale_tile(i, t, result):
                    dve.wait_ge(*rstd_done[i].at(b, t + 1))
                    dve.tensor_scalar(out=result[:, t, :], in0=result[:, t, :], scalar1=mv[:, t, 0:1],
                                      scalar2=rstd[:, t:t + 1], op0=ALU.subtract, op1=ALU.mult).then_inc(normed[i].sem, 1)

                def attention(l):
                    n_parts, n_items = len(PARTS[l]), len(MAX_ITEMS[l])
                    def bias_out(t):
                        dve.wait_ge(*qkv[1].at(b, t + 1))
                        if t >= 2:
                            dve.wait_ge(*v_put[1].at(b, t - 1))
                            dve.wait_ge(*roped[1].at(b, t - 1))
                        bank = (0, 4)[t % 2]
                        dve.tensor_tensor(out=qkv_tile(1, t), in0=ps[:, bank:bank + 2, :].rearrange("p a n -> p (a n)")[:, 0:3 * C],
                                          in1=bqkv_sb[:], op=ALU.add).then_inc(qkv_out[1].sem, 1)

                    if l == 1:
                        bias_out(0)
                        bias_out(1)
                        rope(b, 1, 0)
                        for t in range(NT):
                            if t + 1 < NT:
                                rope(b, 1, t + 1)
                            stack(b, 1, t)
                            if t + 2 < NT:
                                bias_out(t + 2)
                        k_copy(b, 1, NT - 1)

                    def normalise(g):
                        dve.wait_ge(*o_tr[l].at(b, g + 1))
                        o4 = ps[:, 7, :].rearrange("p (t h d) -> p t h d", t=NT, d=32)
                        dve.reciprocal(rden[:], o4[:, :, :, HD]).then_inc(rden_done[l].sem, 1)
                        dve.wait_ge(*rden_done[l].at(b, g + 1))
                        dve.tensor_tensor(
                            out=o_sb[:, :, g * GH * HD:(g + 1) * GH * HD].rearrange("p t (h d) -> p t h d", d=HD),
                            in0=o4[:, :, :, 0:HD], in1=rden[:].unsqueeze(3).to_broadcast([P, NT, GH, HD]),
                            op=ALU.mult).then_inc(o_put[l].sem, 1)

                    for s in range(NG + 2):
                        if s < NG:
                            for i, (t, j) in enumerate(MAX_ITEMS[l]):
                                n = query_tile_keys(l, t)[1]
                                mh = MAX_HEADS[l][t]
                                k = s * n_items + i
                                dve.wait_ge(*raw_score[l].at(b, k + 1))
                                dve.tensor_reduce(out=negmax[:, t, s * GH + j * mh:s * GH + (j + 1) * mh],
                                                  in_=ps[:, k % 3, 0:mh * n].rearrange("p (h n) -> p h n", n=n),
                                                  axis=AX.X, op=ALU.max, negate=True).then_inc(maxed[l].sem, 1)
                            if l == 0:
                                dve.wait_ge(*maxed[0].at(b, (s + 1) * n_items))
                                nm = negmax[:, :, s * GH:(s + 1) * GH]
                                sk = sink4[:, s * GH:(s + 1) * GH].unsqueeze(1).to_broadcast([P, NT, GH])
                                then(dve.tensor_tensor(out=nm, in0=nm.bitcast(F32), in1=sk, op=ALU.subtract))
                                dve.tensor_tensor(out=nm, in0=nm.bitcast(F32), in1=sk, op=ALU.add).then_inc(sunk.sem, 1)
                        if l == 0 and s < 2:
                            for t in (2 * s, 2 * s + 1):
                                split_lo(b, "x3", t, bank0=4)
                        ahead = l == 1 and s >= HEAD_SLOT and not last
                        if ahead:
                            head_step(b + 1, (s - HEAD_SLOT) * N1)
                        if s >= 3:
                            normalise(s - 3)
                        if ahead:
                            for p in range(1, N1):
                                head_step(b + 1, (s - HEAD_SLOT) * N1 + p)
                    normalise(NG - 1)
                    for t in range(NT):
                        split_lo(b, ("o0", "o1")[l], t)

                attention(0)
                norm(0, proj[0], None, x0[:], x1)
                for m in range(NI):
                    dve.wait_ge(*silued.at(b, m + 1))
                    dve.wait_ge(*upped.at(b, m + 1))
                    if m >= 2:
                        dve.wait_ge(*f_lo.at(b, m - 1))
                    dve.scalar_tensor_tensor(out=fuse_sb[:, m % 2, :], in0=ps[:, 2 + m % 2, :], scalar=su_sb[:, m:m + 1],
                                             in1=gate_sb[:, m % 2, :], op0=ALU.mult, op1=ALU.mult).then_inc(fused.sem, 1)
                norm(1, down, sd_sb[:], x1, x2)
                attention(1)
                norm(2, proj[1], None, x2, x3)
                assert steps[0] == DVE_STEPS, steps[0]

            for k in range(HEAD_STEPS):
                head_step(0, k)
            dve.wait_ge(made.sem, MADE)
            dve.wait_ge(start_dve.sem, 2)
            for t in range(NT):
                stack(0, 0, t)
            k_copy(0, 0, NT - 1)
            for i in range(1, 4):
                weights_lo(i)
            dve.wait_ge(gw_split.sem, 1)
            dve.tensor_tensor(out=gw_s[:, 1, :, :], in0=gw_raw[:], in1=gw_s[:, 0, :, :].bitcast(F32),
                              op=ALU.subtract).then_inc(gw_split.sem, 1)
            with dve.Fori(0, B - 1) as b:
                batch(b, False)
            batch(B - 1, True)
            for t in range(NT):
                split_lo(B, "x3", t, bank0=4)

            n_place = [0]

            def after(ins):
                n_place[0] += 1
                ins.then_inc(place.sem, 1)
                dve.wait_ge(place.sem, n_place[0])

            dve.wait_ge(*x3_kept.at(B, 0))
            dve.wait_ge(exp_l.sem, 1)
            after(dve.tensor_scalar(out=score[:], in0=score[:], scalar1=1.0, scalar2=None, op0=ALU.add))
            after(dve.reciprocal(score[:], score[:]))
            for t in range(TT):
                ins = dve.max(out=top8[:, t, :], in_=score[:, t, :])
            after(ins)
            for t in range(TT):
                ins = dve.max_index(out=idx8[:, t, :], in_max=top8[:, t, :], in_values=score[:, t, :])
            after(ins)
            dve.tensor_tensor(out=tsum[:], in0=top8[:, :, 0], in1=top8[:, :, 1], op=ALU.add)
            after(dve.tensor_copy(idxf[:], idx8[:, :, 0:2]))
            dve.reciprocal(tsum[:], tsum[:])
            for s in (0, 1):
                ins = dve.tensor_tensor(out=hot_all[:, :, s, :], in0=iota_e[:].unsqueeze(1).to_broadcast([P, TT, E]),
                                        in1=idxf[:, :, s:s + 1].to_broadcast([P, TT, E]), op=ALU.is_equal)
            after(ins)
            dve.tensor_tensor(out=topw_all[:], in0=top8[:, :, 0:2], in1=tsum[:].unsqueeze(2).to_broadcast([P, TT, 2]), op=ALU.mult)
            dve.tensor_tensor(out=chosen[:], in0=hot_all[:, :, 0, :], in1=hot_all[:, :, 1, :], op=ALU.add).then_inc(counted.sem, 1)
            dve.wait_ge(counted.sem, 2)
            after(dve.tensor_copy(tile_tot[:].rearrange("p e t -> p t e"), ps[:, 7, 0:TT * E].rearrange("p (t e) -> p t e", e=E)))
            after(dve.tensor_tensor_scan(out=tile_inc[:].rearrange("p e t -> p (e t)"), data0=scan_keep[:].rearrange("p e t -> p (e t)"),
                                         data1=tile_tot[:].rearrange("p e t -> p (e t)"), initial=0.0, op0=ALU.mult, op1=ALU.add))
            after(dve.tensor_scalar(out=n_int[:], in0=tile_inc[:, :, TT - 1], scalar1=float(P - 1), scalar2=None, op0=ALU.add))
            after(dve.tensor_scalar(out=n_int[:], in0=n_int[:], scalar1=7, scalar2=None, op0=ALU.logical_shift_right))
            after(dve.tensor_scalar(out=room[:], in0=n_int[:], scalar1=float(P), scalar2=None, op0=ALU.mult))
            after(dve.tensor_tensor_scan(out=room_inc[:], data0=ones_e[:], data1=room[:], initial=0.0, op0=ALU.mult, op1=ALU.add))
            after(dve.tensor_tensor(out=room[:], in0=room_inc[:], in1=room[:], op=ALU.subtract))
            after(dve.tensor_tensor(out=tile_inc[:], in0=tile_inc[:], in1=tile_tot[:], op=ALU.subtract))
            after(dve.tensor_tensor(out=tile_inc[:], in0=tile_inc[:], in1=room[:].unsqueeze(2).to_broadcast([P, E, TT]), op=ALU.add))
            after(dve.tensor_tensor(out=pos[:], in0=ps[:, 2, 0:TT * E].rearrange("p (t e) -> p t e", e=E),
                                    in1=tile_inc[:].rearrange("p e t -> p t e"), op=ALU.add))
            for s in (0, 1):
                ins = dve.tensor_tensor(out=pos_hot[:, :, s, :], in0=pos[:], in1=hot_all[:, :, s, :], op=ALU.mult)
                if s:
                    after(ins)
            after(dve.tensor_reduce(out=slot_f[:], in_=pos_hot[:], axis=AX.X, op=ALU.add))
            dve.tensor_copy(slot[:], slot_f[:]).then_inc(slotted.sem, 1)
            after(dve.tensor_tensor(out=past[:], in0=iota_s[:].unsqueeze(2).to_broadcast([P, NS, E]),
                                    in1=room_inc[:].unsqueeze(1).to_broadcast([P, NS, E]), op=ALU.is_ge))
            after(dve.tensor_reduce(out=owner_f[:], in_=past[:], axis=AX.X, op=ALU.add))
            dve.tensor_scalar(out=owner[:], in0=owner_f[:], scalar1=float(E - 1), scalar2=None, op0=ALU.min).then_inc(owned.sem, 1)

            dve.wait_ge(x3_back.sem, 16)
            with dve.Fori(0, B) as b:
                for t in range(NT):
                    dve.wait_ge(*xg_hi.at(b, t + 1))
                    dve.tensor_tensor(out=xgT[:, 1, :, t * P:(t + 1) * P],
                                      in0=ps[:, 3 + t % 2, 0:C].rearrange("p (k q) -> p k q", k=KC),
                                      in1=xgT[:, 0, :, t * P:(t + 1) * P].bitcast(F32),
                                      op=ALU.subtract).then_inc(xg_lo.sem, 1)
                for u in range(U + 2):
                    if u < U:
                        dve.wait_ge(*sh_silu.at(b, u + 1))
                        dve.tensor_tensor(out=h_sb[:, u % 2, :], in0=ps[:, u % 2, I:2 * I], in1=act_a[:, u % 2, :],
                                          op=ALU.mult).then_inc(sh_h.sem, 1)
                    if 1 <= u <= U:
                        dve.wait_ge(*sh_hhi.at(b, u))
                        dve.tensor_tensor(out=hT[:, (u - 1) % 2, 1, :, :],
                                          in0=ps[0:IH, 3 + (u - 1) % 2, 0:2 * P].rearrange("p (k q) -> p k q", k=2),
                                          in1=hT[:, (u - 1) % 2, 0, :, :].bitcast(F32), op=ALU.subtract).then_inc(sh_hlo.sem, 1)
                    if u >= 3 and u % 2 == 1:
                        t = (u - 3) // 2
                        dve.wait_ge(*sh_down.at(b, t + 1))
                        dve.tensor_tensor(out=y_all[:, bass.ds(b * NT + t, 1), :], in0=ps[:, 5 + t % 2, 0:C].unsqueeze(1),
                                          in1=x3_all[:, bass.ds(b * NT + t, 1), :], op=ALU.add).then_inc(sh_y.sem, 1)

            def vector_step(q, r, on, before):
                if on(0):
                    dve.wait_ge(xs_hi.sem, q + 1)
                    dve.tensor_tensor(out=xsT[:, r % 2, 1, :, :], in0=ps[:, 3 + r % 2, 0:C].rearrange("p (k n) -> p k n", k=KC),
                                      in1=xsT[:, r % 2, 0, :, :].bitcast(F32), op=ALU.subtract).then_inc(xs_lo.sem, 1)
                if on(1):
                    dve.wait_ge(e_silu.sem, q)
                    dve.tensor_tensor(out=h_sb[:, (r - 1) % 2, :], in0=ps[:, (r - 1) % 2, I:2 * I], in1=act_a[:, (r - 1) % 2, :],
                                      op=ALU.mult).then_inc(e_h.sem, 1)
                if on(2):
                    dve.wait_ge(e_hhi.sem, q - 1)
                    dve.tensor_tensor(out=hT[:, (r - 2) % 2, 1, :, :], in0=ps[0:IH, 5 + (r - 2) % 2, 0:2 * P].rearrange("p (k n) -> p k n", k=2),
                                      in1=hT[:, (r - 2) % 2, 0, :, :].bitcast(F32), op=ALU.subtract).then_inc(e_hlo.sem, 1)
                if on(3):
                    dve.wait_ge(e_down.sem, q - 2)
                    if not (isinstance(q, int) and q - 3 < 4):
                        dve.wait_ge(ys_kept[(r - 3) % 4].sem, before(3) * 16)
                    dve.tensor_copy(ys_sb[:, (r - 3) % 4, :], ps[:, (2, 7)[(r - 3) % 2], 0:C]).then_inc(e_y.sem, 1)

            run_steps(dve, vector_step)

            n_y = [0]

            def y_then(ins):
                n_y[0] += 1
                ins.then_inc(y_step.sem, 1)
                dve.wait_ge(y_step.sem, n_y[0])

            def finish(t):
                dve.wait_ge(y_rstd.sem, t // 2 + 1)
                dve.tensor_scalar(out=y_all[:, t, :], in0=y_all[:, t, :], scalar1=mv2[:, t, 0:1], scalar2=rstd2[:, t:t + 1],
                                  op0=ALU.subtract, op1=ALU.mult).then_inc(y_norm.sem, 1)

            for t in range(TT):
                dve.wait_ge(back_in[t % BACK_BUFS].sem, 32 * (t // BACK_BUFS + 1))
                for k in (0, 1):
                    y_then(dve.scalar_tensor_tensor(out=y_all[:, t, :], in0=back[:, t % BACK_BUFS, k, :], scalar=topw_all[:, t, k:k + 1],
                                                    in1=y_all[:, t, :], op0=ALU.mult, op1=ALU.add))
                y_then(dve.bn_stats(out=stats2[:, t, :], in_=y_all[:, t, :]))
                y_then(dve.bn_aggr(out=mv2[:, t, :], in_=stats2[:, t, :]))
                dve.tensor_scalar(out=mv2[:, t, 1:2], in0=mv2[:, t, 1:2], scalar1=EPS, scalar2=None,
                                  op0=ALU.add).then_inc(y_var.sem, 1)
                if t >= 5 and t % 2:
                    finish(t - 5)
                    finish(t - 4)
            for t in range(TT - 4, TT):
                finish(t)

        @block.tensor
        def _(pe):
            pe.wait_ge(made.sem, 2)
            pe.wait_ge(w_lo.sem, 1)
            EXACT = ((0, 0), (0, 1), (1, 0))

            def keep_clock(bank, n):
                for _ in range(n):
                    pe.matmul(ps[:, bank, :], ident_b[:], idle_b[:], start=True, stop=True)

            def split_tr(b, n, src, ready, t, bank0=6):
                if ready is not None:
                    pe.wait_ge(*ready)
                if t >= 2:
                    pe.wait_ge(*lo[n].at(b, t - 1))
                for k in range(KC):
                    ins = pe.transpose(ps[:, bank0 + t % 2, k * P:(k + 1) * P], src[:, t, k * P:(k + 1) * P], ident[:])
                ins.then_inc(tr[n].sem, 1)

            def product(dst, t, w, c0, n):
                for i, (a, w_part) in enumerate(EXACT):
                    for k in range(KC):
                        ins = pe.matmul(dst, xT[:, a, k, t * P:(t + 1) * P], w[:, w_part, k, c0:c0 + n],
                                        start=(i + k == 0), stop=(i == 2 and k == KC - 1))
                return ins

            def head_step(b, k):
                if k < NT:
                    split_tr(b, "x0", x0, x0_in.at(b, 16), k, bank0=0)
                if 1 <= k <= NT:
                    pe.wait_ge(*lo["x0"].at(b, k))
                    if k >= 2:
                        pe.wait_ge(*qkv_out[0].at(b, k - 1))
                    product(ps[:, 2, 0:NQKV[0]], k - 1, wqkv_s[0], 0, NQKV[0]).then_inc(qkv[0].sem, 1)

            def x3_tr(turn, t):
                split_tr(turn, "x3", x3, None, t, bank0=4)

            def router(turn):
                for t in range(NT):
                    for i, (a, w_part) in enumerate(EXACT):
                        for k in range(KC):
                            ins = pe.matmul(ps[:, 0, t * E:(t + 1) * E], xT[:, a, k, t * P:(t + 1) * P], gw_s[:, w_part, k, :],
                                            start=(i + k == 0), stop=(i == 2 and k == KC - 1))
                ins.then_inc(logits.sem, 1)

            def stack_tr(b, l, t):
                n_blk = (KVH0, PAIRS)[l]
                pe.wait_ge(*st_lo[l].at(b, 2 * t + 1))
                if t >= 1:
                    pe.wait_ge(*q_out[l].at(b, t))
                elif l == 0:
                    pe.wait_ge(*qkv_out[0].at(b, NT))
                for n in range(PAIRS):
                    ins = pe.matmul(ps[:, 2 + n // 4, (n % 4) * P:(n % 4 + 1) * P],
                                    q_st[:, 2 * n:2 * n + 2, :].rearrange("p h s -> p (h s)"), ident_r[:],
                                    start=True, stop=True)
                ins.then_inc(q_tr[l].sem, 1)
                pe.wait_ge(*st_lo[l].at(b, 2 * t + 2))
                if t >= 1:
                    pe.wait_ge(*k_even[l].at(b, t))
                    pe.wait_ge(*k_odd[l].at(b, t))
                for n in range(n_blk):
                    ins = pe.matmul(ps[:, K_BANK[l] + n // 4, (n % 4) * P:(n % 4 + 1) * P],
                                    k_st[:, 2 * n:2 * n + 2, :].rearrange("p h s -> p (h s)"), ident_r[:],
                                    start=True, stop=True)
                ins.then_inc(k_tr[l].sem, 1)

            def batch(b, last):

                def attention(l):
                    n_parts, n_items = len(PARTS[l]), len(MAX_ITEMS[l])
                    if l == 1:
                        split_tr(b, "x2", x2, normed[1].at(b, NT - 1), NT - 2)
                        for t in range(NT):
                            if t == 1:
                                split_tr(b, "x2", x2, normed[1].at(b, NT), NT - 1)
                            pe.wait_ge(*lo["x2"].at(b, t + 1))
                            if t >= 2:
                                pe.wait_ge(*qkv_out[1].at(b, t - 1))
                            bank = (0, 4)[t % 2]
                            product(ps[:, bank, :], t, wqkv_s[1], 0, 512)
                            product(ps[:, bank + 1, 0:256], t, wqkv_s[1], 512, 256).then_inc(qkv[1].sem, 1)
                        for t in range(NT):
                            if t >= 2:
                                pe.wait_ge(*qkv_out[1].at(b, NT - 1))
                                keep_clock(0, IDLE_HEAD)
                            stack_tr(b, 1, t)
                        keep_clock(0, IDLE_HEAD)

                    def k_block(h):
                        return 2 * (h // 4) + h % 2 if l == 0 else h

                    def raw_item(g, i):
                        t, j = MAX_ITEMS[l][i]
                        k0, n = query_tile_keys(l, t)
                        item = g * n_items + i
                        if item >= 3:
                            pe.wait_ge(*maxed[l].at(b, item - 2))
                        bank = item % 3
                        mh = MAX_HEADS[l][t]
                        dst = ps[:, bank, 0:mh * n].rearrange("p (h n) -> p h n", n=n)
                        if l == 0:
                            m0 = k0 - (t * P - HALF_WINDOW)
                            pe.matmul(dst, ident_b[:], band[:, m0:m0 + n].unsqueeze(1).to_broadcast([P, mh, n]),
                                      start=True, stop=False, skip_group_check=True)
                        else:
                            pe.matmul(dst[:, :, n - P:n], ident_b[:], causal_q[:].unsqueeze(1).to_broadcast([P, mh, P]),
                                      start=True, stop=False, skip_group_check=True)
                        for jj in range(mh):
                            h = g * GH + j * mh + jj
                            ins = pe.matmul(dst[:, jj, :], qT[:, h // 2, t * P:(t + 1) * P], kT[:, k_block(h), k0:k0 + n],
                                            start=False, stop=True, skip_group_check=True)
                        ins.then_inc(raw_score[l].sem, 1)

                    def score_item(g, i):
                        p, j = i // GH, i % GH
                        h = g * GH + j
                        item = g * n_parts * GH + i
                        if item >= 3:
                            pe.wait_ge(*exped[l].at(b, item - 2))
                        for kt, col in PARTS[l][p]:
                            q0, n = key_tile_queries(l, kt)
                            ins = pe.matmul(ps[:, 3 + item % 3, col:col + n],
                                            kT[:, k_block(h), kt * P:(kt + 1) * P], qT[:, h // 2, q0:q0 + n], start=True, stop=True,
                                            skip_group_check=True)
                        ins.then_inc(scored[l].sem, 1)

                    def pv_part(g, p):
                        pe.wait_ge(*kept[l].at(b, g * n_parts + p + 1))
                        if p == 0 and g >= 1:
                            pe.wait_ge(*oT_out[l].at(b, g))
                        for i, (kt, off) in enumerate(PARTS[l][p]):
                            q0, n = key_tile_queries(l, kt)
                            for j in range(GH):
                                h = g * GH + j
                                ins = pe.matmul(ps[32 * j:32 * j + 32, 6, q0:q0 + n],
                                                v_aug[l][:, kt, h // 4 if l == 0 else h, :],
                                                prob[:, (g * n_parts + p) % PROB_BUFS, j, off:off + n], start=(p == 0 and i == 0),
                                                stop=(p == n_parts - 1 and i == len(PARTS[l][p]) - 1), skip_group_check=True)
                        ins.then_inc(pv[l].sem, 1)

                    def o_transposes(g):
                        pe.wait_ge(*oT_out[l].at(b, g + 1))
                        if g >= 1:
                            pe.wait_ge(*o_put[l].at(b, g))
                        for t in range(NT):
                            ins = pe.transpose(ps[:, 7, t * P:(t + 1) * P], oT[:, t * P:(t + 1) * P], ident[:])
                        ins.then_inc(o_tr[l].sem, 1)

                    pe.wait_ge(*q_out[l].at(b, NT))
                    pe.wait_ge(*k_even[l].at(b, NT))
                    pe.wait_ge(*k_odd[l].at(b, NT))
                    pe.wait_ge(*v_put[l].at(b, NT))
                    for s in range(NG + 2):
                        g = s - 2
                        if 1 <= s <= NG:
                            if l == 0:
                                pe.wait_ge(*sunk.at(b, s))
                            else:
                                pe.wait_ge(*maxed[1].at(b, s * n_items))
                            if s >= 2:
                                pe.wait_ge(*sh_out[l].at(b, s - 1))
                            if s >= 4:
                                pe.wait_ge(*o_put[l].at(b, s - 3))
                            for t in range(NT):
                                ins = pe.matmul(ps[0:GH, 7, t * P:(t + 1) * P], negmax[:, t, (s - 1) * GH:s * GH], ident_r[:],
                                                start=True, stop=True)
                            ins.then_inc(sh_tr[l].sem, 1)
                        if l == 0 and s == NG:
                            router(b)
                        if l == 0 and s == 2:
                            pe.wait_ge(*lo["x3"].at(b, NT))
                        if g >= 0:
                            pe.wait_ge(*sh_row[g][l].at(b, GH * 16))
                        for i in range(max(n_items, n_parts * GH)):
                            if g >= 0 and i < n_parts * GH:
                                score_item(g, i)
                            if s < NG and i < n_items:
                                raw_item(s, i)
                            if l == 1 and s >= HEAD_SLOT and i % GH == GH - 1 and i // GH < n_parts and not last:
                                head_step(b + 1, (s - HEAD_SLOT) * N1 + i // GH)
                            item = g * n_parts * GH + i - PV_LAG
                            if g >= 0 and i < n_parts * GH and item >= 0 and item % GH == GH - 1:
                                pv_part(*divmod(item // GH, n_parts))
                            if g >= 1 and i == GH + 3:
                                if s <= NG:
                                    pe.wait_ge(*sh_out[l].at(b, s))
                                o_transposes(g - 1)
                        if l == 0 and s < 2:
                            if s == 0:
                                pe.wait_ge(*normed[2].at(b, 0))
                            for t in (2 * s, 2 * s + 1):
                                x3_tr(b, t)
                    for part in range(NG * n_parts - (PV_LAG + GH - 1) // GH, NG * n_parts):
                        pv_part(*divmod(part, n_parts))
                    o_transposes(NG - 1)
                    name = ("o0", "o1")[l]
                    for t in range(NT):
                        split_tr(b, name, o_sb, o_put[l].at(b, NG), t)
                    for t in range(NT):
                        pe.wait_ge(*lo[name].at(b, t + 1))
                        if l == 0 and t == 0:
                            pe.wait_ge(*logit_kept.at(b, 1))
                        bank = SUM_BANKS[2 * l][t]
                        if bank in SUM_BANKS[2 * l][:t]:
                            pe.wait_ge(*normed[2 * l].at(b, SUM_BANKS[2 * l].index(bank) + 1))
                        product(ps[:, bank, 0:C], t, wo_s[l], 0, C).then_inc(proj[l].sem, 1)
                        if l == 1 and t >= 1 and not last:
                            stack_tr(b + 1, 0, t - 1)
                        if l == 0 and t >= 2:
                            split_tr(b, "x1", x1, normed[0].at(b, t - 1), t - 2)
                    if l == 1 and not last:
                        keep_clock(6, IDLE_TAIL)
                        stack_tr(b + 1, 0, NT - 1)
                        keep_clock(6, IDLE_TAIL)

                attention(0)
                for t in (NT - 2, NT - 1):
                    split_tr(b, "x1", x1, normed[0].at(b, t + 1), t)
                pe.wait_ge(w_int8.sem, 48)
                keep_clock(0, IDLE_FFN)
                pe.wait_ge(*lo["x1"].at(b, NT))
                for m in range(NI):
                    for w, bank0, sig, free in ((wg_sb, 0, gated, silued), (wu_sb, 2, upped, fused)):
                        if m >= 2:
                            pe.wait_ge(*free.at(b, m - 1))
                        for part in (0, 1):
                            for k in range(KC):
                                ins = pe.matmul(ps[:, bank0 + m % 2, :], w[:, k, m * P:(m + 1) * P], xT[:, part, k, :],
                                                start=(part + k == 0), stop=(part == 1 and k == KC - 1))
                        ins.then_inc(sig.sem, 1)
                for t in range(NT):
                    for m in range(NI):
                        if t == 0:
                            pe.wait_ge(*f_lo.at(b, m + 1))
                        for part in (0, 1):
                            ins = pe.matmul(ps[:, SUM_BANKS[1][t], 0:C], fT[:, part, m, t * P:(t + 1) * P], wd_sb[:, m, :],
                                            start=(m + part == 0), stop=(m == NI - 1 and part == 1))
                    ins.then_inc(down.sem, 1)
                    if t >= 2:
                        split_tr(b, "x2", x2, normed[1].at(b, t - 1), t - 2)
                attention(1)
            for k in range(HEAD_STEPS):
                head_step(0, k)
            pe.wait_ge(made.sem, MADE)
            for t in range(NT):
                stack_tr(0, 0, t)
            pe.wait_ge(w_lo.sem, 4)
            pe.wait_ge(gw_split.sem, 2)
            with pe.Fori(0, B - 1) as b:
                batch(b, False)
            batch(B - 1, True)
            pe.wait_ge(*normed[2].at(B, 0))
            for t in range(NT):
                x3_tr(B, t)
            pe.wait_ge(*lo["x3"].at(B, NT))
            router(B)

            pe.wait_ge(counted.sem, 1)
            all_chosen = chosen[:].rearrange("p t e -> p (t e)")
            pe.matmul(ps[:, 2, 0:TT * E], tri[:], all_chosen, start=True, stop=True)
            pe.matmul(ps[:, 7, 0:TT * E], ones_b[:], all_chosen, start=True, stop=True).then_inc(counted.sem, 1)
            pe.wait_ge(shared_in.sem, 32)
            with pe.Fori(0, B) as b:
                pe.wait_ge(*xg_in.at(b, 16))
                for t in range(NT):
                    if t >= 2:
                        pe.wait_ge(*xg_lo.at(b, t - 1))
                    for k in range(KC):
                        ins = pe.transpose(ps[:, 3 + t % 2, k * P:(k + 1) * P], xg[:, t, k * P:(k + 1) * P], ident[:])
                    ins.then_inc(xg_tr.sem, 1)
                pe.wait_ge(*xg_lo.at(b, NT))

                def sh_upward(u):
                    if u >= 2:
                        pe.wait_ge(*sh_h.at(b, u - 1))
                    for part in (0, 1):
                        for k in range(KC):
                            ins = pe.matmul(ps[:, u % 2, 0:2 * I], xgT[:, part, k, (u // 2) * P:(u // 2 + 1) * P],
                                            w13_sb[:, E + u % 2, k, :], start=(part + k == 0), stop=(part == 1 and k == KC - 1))
                    ins.then_inc(sh_up.sem, 1)

                def sh_transpose(u):
                    pe.wait_ge(*sh_h.at(b, u + 1))
                    if u >= 2:
                        pe.wait_ge(*sh_hlo.at(b, u - 1))
                    for k in (0, 1):
                        ins = pe.transpose(ps[0:IH, 3 + u % 2, k * P:(k + 1) * P], h_sb[:, u % 2, k * IH:(k + 1) * IH], ident[:])
                    ins.then_inc(sh_htr.sem, 1)

                def sh_downward(u):
                    pe.wait_ge(*sh_hlo.at(b, u + 1))
                    t = u // 2
                    if t >= 2 and u % 2 == 0:
                        pe.wait_ge(*sh_y.at(b, t - 1))
                    for part in (0, 1):
                        for k in (0, 1):
                            ins = pe.matmul(ps[:, 5 + t % 2, 0:C], hT[:, u % 2, part, k, :], w2_sb[:, E + u % 2, k, :],
                                            start=(u % 2 + part + k == 0), stop=(u % 2 + part + k == 3))
                    if u % 2:
                        ins.then_inc(sh_down.sem, 1)

                for u in range(U + 2):
                    if u < U:
                        sh_upward(u)
                    if 1 <= u <= U:
                        sh_transpose(u - 1)
                    if u >= 2:
                        sh_downward(u - 2)

            loaded = []

            def expert_of(q, stage):
                n = len(steps_done)
                if stage == 3:
                    for step, e in loaded[-3:]:
                        if step == n - 2 and (n - 2 >= turn_start(n)):
                            return e
                tile = q - stage
                e = pe.value_load(owner[0:1, tile:tile + 1] if isinstance(tile, int) else owner[0:1, bass.ds(tile, 1)],
                                  min_val=0, max_val=E - 1)
                if stage == 1:
                    loaded.append((n, e))
                return e

            steps_done = []

            def turn_start(n):
                return 0 if n < PEELED else PEELED if n < PEELED + STEPS else PEELED + STEPS

            def tensor_step(q, r, on, before):
                first = isinstance(q, int)
                if on(0):
                    pe.wait_ge(xs_in[r].sem, (before(0) + 1) * 16)
                    if not (first and q < 2):
                        pe.wait_ge(xs_lo.sem, q - 1)
                    for k in range(KC):
                        ins = pe.transpose(ps[:, 3 + r % 2, k * P:(k + 1) * P], xs_sb[:, r, k * P:(k + 1) * P], ident[:])
                    ins.then_inc(xs_tr.sem, 1)
                if on(1):
                    e = expert_of(q, 1)
                    pe.wait_ge(xs_lo.sem, q)
                    if not (first and q < 3):
                        pe.wait_ge(e_h.sem, q - 2)
                    for part in (0, 1):
                        for k in range(KC):
                            ins = pe.matmul(ps[:, (r - 1) % 2, 0:2 * I], xsT[:, (r - 1) % 2, part, k, :], w13_sb[:, bass.ds(e, 1), k, :],
                                            start=(part + k == 0), stop=(part == 1 and k == KC - 1))
                    ins.then_inc(e_up.sem, 1)
                if on(2):
                    pe.wait_ge(e_h.sem, q - 1)
                    if not (first and q < 4):
                        pe.wait_ge(e_hlo.sem, q - 3)
                    for k in (0, 1):
                        ins = pe.transpose(ps[0:IH, 5 + (r - 2) % 2, k * P:(k + 1) * P], h_sb[:, (r - 2) % 2, k * IH:(k + 1) * IH], ident[:])
                    ins.then_inc(e_htr.sem, 1)
                if on(3):
                    e = expert_of(q, 3)
                    pe.wait_ge(e_hlo.sem, q - 2)
                    if not (first and q < 5):
                        pe.wait_ge(e_y.sem, q - 4)
                    for part in (0, 1):
                        for k in (0, 1):
                            ins = pe.matmul(ps[:, (2, 7)[(r - 3) % 2], 0:C], hT[:, (r - 3) % 2, part, k, :], w2_sb[:, bass.ds(e, 1), k, :],
                                            start=(part + k == 0), stop=(part + k == 2))
                    ins.then_inc(e_down.sem, 1)
                steps_done.append(q)

            pe.wait_ge(owned.sem, 1)
            pe.wait_ge(w13_in.sem, 16 * E // 4)
            pe.wait_ge(w2_in.sem, 16 * E // 4)
            pe.wait_ge(*sh_y.at(B, 0))
            run_steps(pe, tensor_step)


MADE = 27
_INPUTS = ("x", "wqkv0", "wo0", "sink", "w_gate", "w_up", "w_down", "s_gate", "s_up", "s_down",
           "wqkv1", "b_qkv", "wo1", "b_out", "gate_w", "w13", "w2", "rotary")


def lay_out(inputs):
    g = {n: np.asarray(v) for n, v in inputs.items()}
    a = {
        "x": g["L0_attn_x"],
        "wqkv0": np.concatenate([g["L0_attn_wq"], g["L0_attn_wk"], g["L0_attn_wv"]], 1),
        "wo0": g["L0_attn_wo"], "sink": g["L0_attn_sink"].reshape(H),
        "w_gate": np.ascontiguousarray(g["L0_ffn_w_gate"]).view(np.int32), "w_up": np.ascontiguousarray(g["L0_ffn_w_up"]).view(np.int32), "w_down": np.ascontiguousarray(g["L0_ffn_w_down"]).view(np.int32),
        "s_gate": g["L0_ffn_s_gate"].reshape(NI, P).T, "s_up": g["L0_ffn_s_up"].reshape(NI, P).T, "s_down": g["L0_ffn_s_down"],
        "wqkv1": g["L1_attn_w_qkv"].T, "b_qkv": g["L1_attn_b_qkv"],
        "wo1": g["L1_attn_w_out"].T, "b_out": g["L1_attn_b_out"], "gate_w": g["L1_ffn_gate_w"].T,
        "rotary": rotary_tables(),
    }
    w1 = np.concatenate([g["L1_ffn_w1"], g["L1_ffn_sw1"].reshape(SHARED, I, C)])
    w3 = np.concatenate([g["L1_ffn_w3"], g["L1_ffn_sw3"].reshape(SHARED, I, C)])
    w2 = np.concatenate([g["L1_ffn_w2"], g["L1_ffn_sw2"].reshape(C, SHARED, I).transpose(1, 0, 2)])
    a["w13"] = np.concatenate([w1, w3], 1).reshape(NE, 2 * I, KC, P).transpose(3, 0, 2, 1)
    a["w2"] = w2.reshape(NE, C, 2, IH).transpose(3, 0, 2, 1)
    return {n: np.ascontiguousarray(v) for n, v in a.items()}


def kernel(**inputs):
    import concourse.bacc as bacc
    from concourse.bass_utils import run_bass_kernel_spmd

    arrays = lay_out(inputs)
    nc = bacc.Bacc("TRN2", target_bir_lowering=False, num_devices=1)
    args = [nc.dram_tensor(f"in_{n}", arrays[n].shape, mybir.dt.from_np(arrays[n].dtype), kind="ExternalInput").ap()
            for n in _INPUTS]
    out = nc.dram_tensor("out", (B, T, C), F32, kind="ExternalOutput").ap()
    build(nc, *args, out)
    r = run_bass_kernel_spmd(nc, [{f"in_{n}": arrays[n] for n in _INPUTS}], core_ids=[0])
    return r.results[0]["out"]
```
